# Optimizing a Trainium2 kernel written in Bass

```python
import numpy as np
import jax
import jax.numpy as jnp

def _softmax(x, axis=-1):
    return jax.nn.softmax(x, axis=axis)

def _gelu(x):
    return jax.nn.gelu(x, approximate=True)

def _silu(x):
    return jax.nn.silu(x)

def _sigmoid(x):
    return jax.nn.sigmoid(x)

def _layernorm(x, axis=-1, eps=1e-05):
    m = jnp.mean(x, axis=axis, keepdims=True)
    v = jnp.var(x, axis=axis, keepdims=True)
    return (x - m) / jnp.sqrt(v + eps)

def _scatter_add(tgt, idx, src, axis=0):
    return tgt.at[idx].add(src)

def _segment_sum(src, seg, n):
    return jax.ops.segment_sum(src, seg, n)
kernel_name = 'mk_perceiver_d1_seqx_r4_407259'

def setup_inputs(seed: int=0):
    np.random.seed(seed)
    _w = jnp.asarray

    def _rec_inputs():
        import jax
        import jax.numpy as jnp
        _rk = jax.random.key(seed)
        x = -0.0002928 + 1 * jax.random.normal(jax.random.fold_in(_rk, 1), (32, 32, 256), jnp.float32)
        _lenS = 32 - jax.random.randint(jax.random.fold_in(_rk, 7), (32,), 0, max(1, 32 // 4) + 1, jnp.int32)
        _lenS2 = 257 - jax.random.randint(jax.random.fold_in(_rk, 8), (32,), 0, max(1, 257 // 4) + 1, jnp.int32)
        _ctx_1024P = jax.random.normal(jax.random.fold_in(_rk, 11), (32, 16, 256), jnp.float32)
        _ctx_1024c = jax.random.dirichlet(jax.random.fold_in(_rk, 511), 0.3 * jnp.ones((16,), jnp.float32), (32, 257))
        _ctx_1024t = jnp.einsum('bsk,bkd->bsd', _ctx_1024c, _ctx_1024P)
        _ctx_1024t = _ctx_1024t * jax.lax.rsqrt(jnp.mean(jnp.square(_ctx_1024t)) + 1e-12) * 0.953939
        ctx_1024 = -1.39393e-06 + 0.999914 * (_ctx_1024t + 0.3 * jax.random.normal(jax.random.fold_in(_rk, 611), (32, 257, 256), jnp.float32))
        _validS = jnp.arange(32)[None, :] < _lenS[:, None]
        _validS2 = jnp.arange(257)[None, :] < _lenS2[:, None]
        _causal = jnp.tril(jnp.ones((32, 32), dtype=bool))
        mask_1x1xSxS2_ik1 = jnp.where(jnp.broadcast_to(_validS2[0:1, None, None, :], (1, 1, 32, 257)), 1, 0).astype(jnp.int32)
        return (x, ctx_1024, mask_1x1xSxS2_ik1)
    x, ctx_1024, mask_1x1xSxS2_ik1 = _rec_inputs()

    def _L0_xattn_setup():
        import jax, jax.numpy as jnp
        import numpy as np
        D_MODEL = 256
        N_HEAD = 16
        HEAD = D_MODEL // N_HEAD

        def _split_heads(x):
            B, S, _ = x.shape
            return x.reshape(B, S, N_HEAD, HEAD).transpose(0, 2, 1, 3)
        key = jax.random.key(seed)
        ks = jax.random.split(key, 12)
        B, S = (2, 512)
        s = 1.0 / np.sqrt(D_MODEL)
        inp = {'q': jax.random.normal(ks[0], (B, S, D_MODEL), jnp.float32), 'k': jax.random.normal(ks[1], (B, S, D_MODEL), jnp.float32), 'v': jax.random.normal(ks[2], (B, S, D_MODEL), jnp.float32), 'mask': jax.random.randint(ks[3], (1, 1, S, S), 0, 2, jnp.int32), 'wq': jax.random.normal(ks[4], (D_MODEL, D_MODEL), jnp.float32) * s, 'bq': jnp.zeros((D_MODEL,), jnp.float32), 'wk': jax.random.normal(ks[5], (D_MODEL, D_MODEL), jnp.float32) * s, 'bk': jnp.zeros((D_MODEL,), jnp.float32), 'wv': jax.random.normal(ks[6], (D_MODEL, D_MODEL), jnp.float32) * s, 'bv': jnp.zeros((D_MODEL,), jnp.float32), 'wo': jax.random.normal(ks[7], (D_MODEL, D_MODEL), jnp.float32) * s, 'bo': jnp.zeros((D_MODEL,), jnp.float32)}
        return inp
    _L0_xattn_all = _L0_xattn_setup()
    _L0_xattn_in = {k: v for k, v in _L0_xattn_all.items() if k in ('wq', 'bq', 'wk', 'bk', 'wv', 'bv', 'wo', 'bo')}
    del _L0_xattn_all

    def _L0_attn_setup():
        import jax, jax.numpy as jnp
        import numpy as np
        B, S, E, H = (2, 512, 256, 8)
        DH = E // H
        F = DH // 2
        key = jax.random.key(seed)
        ks = jax.random.split(key, 7)
        sc = E ** (-0.5)
        return {'x': jax.random.normal(ks[0], (B, S, E), dtype=jnp.float32), 'Wq': jax.random.normal(ks[1], (E, E), dtype=jnp.float32) * sc, 'Wk': jax.random.normal(ks[2], (E, E), dtype=jnp.float32) * sc, 'Wv': jax.random.normal(ks[3], (E, E), dtype=jnp.float32) * sc, 'norm_w': jnp.ones((H, DH), dtype=jnp.float32), 'Wo': jax.random.normal(ks[4], (E, E), dtype=jnp.float32) * sc, 'bo': jnp.zeros((E,), dtype=jnp.float32), 'diff_weight': jnp.float32(0.2)}
    _L0_attn_all = _L0_attn_setup()
    _L0_attn_in = {k: v for k, v in _L0_attn_all.items() if k in ('Wq', 'Wk', 'Wv', 'norm_w', 'Wo', 'bo', 'diff_weight')}
    del _L0_attn_all

    def _L0_ffn_setup():
        import jax, jax.numpy as jnp
        import numpy as np
        D_MODEL, D_FF, N_EXPERTS, TOP_K = (256, 512, 8, 2)
        B, S = (2, 512)
        key = jax.random.key(seed)
        ks = jax.random.split(key, 6)
        sd = 1.0 / np.sqrt(D_MODEL)
        sf = 1.0 / np.sqrt(D_FF)
        return {'x': jax.random.normal(ks[0], (B, S, D_MODEL), jnp.float32), 'router_w': jax.random.normal(ks[1], (N_EXPERTS, D_MODEL), jnp.float32) * sd, 'gate_w': jax.random.normal(ks[2], (N_EXPERTS, D_MODEL, D_FF), jnp.float32) * sd, 'gate_b': jnp.zeros((N_EXPERTS, D_FF), jnp.float32), 'up_w': jax.random.normal(ks[3], (N_EXPERTS, D_MODEL, D_FF), jnp.float32) * sd, 'up_b': jnp.zeros((N_EXPERTS, D_FF), jnp.float32), 'down_w': jax.random.normal(ks[4], (N_EXPERTS, D_FF, D_MODEL), jnp.float32) * sf, 'down_b': jnp.zeros((N_EXPERTS, D_MODEL), jnp.float32)}
    _L0_ffn_all = _L0_ffn_setup()
    _L0_ffn_in = {k: v for k, v in _L0_ffn_all.items() if k in ('router_w', 'gate_w', 'gate_b', 'up_w', 'up_b', 'down_w', 'down_b')}
    del _L0_ffn_all
    return {'x': x, 'ctx_1024': ctx_1024, 'mask_1x1xSxS2_ik1': mask_1x1xSxS2_ik1, 'L0_xattn_wq': _L0_xattn_in['wq'], 'L0_xattn_bq': _L0_xattn_in['bq'], 'L0_xattn_wk': _L0_xattn_in['wk'], 'L0_xattn_bk': _L0_xattn_in['bk'], 'L0_xattn_wv': _L0_xattn_in['wv'], 'L0_xattn_bv': _L0_xattn_in['bv'], 'L0_xattn_wo': _L0_xattn_in['wo'], 'L0_xattn_bo': _L0_xattn_in['bo'], 'L0_attn_Wq': _L0_attn_in['Wq'], 'L0_attn_Wk': _L0_attn_in['Wk'], 'L0_attn_Wv': _L0_attn_in['Wv'], 'L0_attn_norm_w': _L0_attn_in['norm_w'], 'L0_attn_Wo': _L0_attn_in['Wo'], 'L0_attn_bo': _L0_attn_in['bo'], 'L0_attn_diff_weight': _L0_attn_in['diff_weight'], 'L0_ffn_router_w': _L0_ffn_in['router_w'], 'L0_ffn_gate_w': _L0_ffn_in['gate_w'], 'L0_ffn_gate_b': _L0_ffn_in['gate_b'], 'L0_ffn_up_w': _L0_ffn_in['up_w'], 'L0_ffn_up_b': _L0_ffn_in['up_b'], 'L0_ffn_down_w': _L0_ffn_in['down_w'], 'L0_ffn_down_b': _L0_ffn_in['down_b']}

def reference(x, ctx_1024, mask_1x1xSxS2_ik1, L0_xattn_wq, L0_xattn_bq, L0_xattn_wk, L0_xattn_bk, L0_xattn_wv, L0_xattn_bv, L0_xattn_wo, L0_xattn_bo, L0_attn_Wq, L0_attn_Wk, L0_attn_Wv, L0_attn_norm_w, L0_attn_Wo, L0_attn_bo, L0_attn_diff_weight, L0_ffn_router_w, L0_ffn_gate_w, L0_ffn_gate_b, L0_ffn_up_w, L0_ffn_up_b, L0_ffn_down_w, L0_ffn_down_b):
    import jax
    import jax.numpy as jnp

    def _L0_xattn_ref(q, k, v, mask, wq, bq, wk, bk, wv, bv, wo, bo):
        import jax, jax.numpy as jnp
        import numpy as np
        D_MODEL = 256
        N_HEAD = 16
        HEAD = D_MODEL // N_HEAD

        def _split_heads(x):
            B, S, _ = x.shape
            return x.reshape(B, S, N_HEAD, HEAD).transpose(0, 2, 1, 3)
        q_s = _split_heads(q @ wq.T + bq)
        k_s = _split_heads(k @ wk.T + bk)
        v_s = _split_heads(v @ wv.T + bv)
        scale = 1.0 / np.sqrt(HEAD)
        score = jnp.einsum('bhqd,bhkd->bhqk', q_s, k_s) * scale
        score = jnp.where(mask == 0, jnp.float32(-10000.0), score)
        attn = jax.nn.softmax(score, axis=-1)
        out = jnp.einsum('bhqk,bhkd->bhqd', attn, v_s)
        B, H, S, Dh = out.shape
        out = out.transpose(0, 2, 1, 3).reshape(B, S, H * Dh)
        return out @ wo.T + bo

    def _L0_attn_ref(x, Wq, Wk, Wv, norm_w, Wo, bo, diff_weight):
        import jax, jax.numpy as jnp
        import numpy as np
        B, S, E, H = (2, 512, 256, 8)
        DH = E // H
        F = DH // 2
        b, s, e = x.shape
        qs = (x @ Wq.T).reshape(b, s, H, 2, F)
        ks_ = (x @ Wk.T).reshape(b, s, H, 2, F)
        vs = (x @ Wv.T).reshape(b, s, H, DH)
        scale = F ** (-0.5)
        scores = jnp.einsum('bqhif,bkhif->ibhqk', qs, ks_) * scale
        atts = jax.nn.softmax(scores, axis=-1)
        att = atts[0] - diff_weight * atts[1]
        o = jnp.einsum('bhqk,bkhe->bqhe', att, vs)
        eps = jnp.finfo(o.dtype).eps
        rms = jax.lax.rsqrt(jnp.mean(o * o, axis=(-2, -1), keepdims=True) + eps)
        normed = (o * rms * norm_w).reshape(b, s, e)
        return (normed @ Wo.T + bo) * (1.0 - diff_weight)

    def _L0_ffn_ref(x, router_w, gate_w, gate_b, up_w, up_b, down_w, down_b):
        import jax, jax.numpy as jnp
        import numpy as np
        D_MODEL, D_FF, N_EXPERTS, TOP_K = (256, 512, 8, 2)
        B, S = (2, 512)
        b, s, d = x.shape
        xf = x.reshape(b * s, d)
        n = xf.shape[0]
        router_logits = xf @ router_w.T
        probs = jax.nn.softmax(router_logits, axis=-1)
        topv, topi = jax.lax.top_k(probs, TOP_K)
        mask = jnp.zeros_like(probs).at[jnp.arange(n)[:, None], topi].set(1.0)
        probs = probs * mask
        probs = probs / (probs.sum(axis=-1, keepdims=True) + 1e-09)
        g = jnp.einsum('nd,edf->nef', xf, gate_w) + gate_b
        u = jnp.einsum('nd,edf->nef', xf, up_w) + up_b
        h = jax.nn.silu(g) * u
        expert_out = jnp.einsum('nef,efd->ned', h, down_w) + down_b
        y = jnp.einsum('ne,ned->nd', probs, expert_out)
        return y.reshape(b, s, d)
    x = x + _L0_xattn_ref(_layernorm(x, axis=-1), ctx_1024, ctx_1024, mask_1x1xSxS2_ik1, L0_xattn_wq, L0_xattn_bq, L0_xattn_wk, L0_xattn_bk, L0_xattn_wv, L0_xattn_bv, L0_xattn_wo, L0_xattn_bo)
    x = x + _L0_attn_ref(_layernorm(x, axis=-1), L0_attn_Wq, L0_attn_Wk, L0_attn_Wv, L0_attn_norm_w, L0_attn_Wo, L0_attn_bo, L0_attn_diff_weight)
    x = x + _L0_ffn_ref(_layernorm(x, axis=-1), L0_ffn_router_w, L0_ffn_gate_w, L0_ffn_gate_b, L0_ffn_up_w, L0_ffn_up_b, L0_ffn_down_w, L0_ffn_down_b)
    return x

_drawn_inputs = setup_inputs


def setup_inputs(seed=0):
    import zlib

    import numpy as np

    out = dict(_drawn_inputs(seed))
    spreads = {'L0_xattn_bq': (0.0, 0.1),
     'L0_xattn_bk': (0.0, 0.8),
     'L0_xattn_bv': (0.0, 0.1),
     'L0_xattn_bo': (0.0, 0.1),
     'L0_attn_norm_w': (1.0, 0.2),
     'L0_attn_bo': (0.0, 0.1),
     'L0_ffn_gate_b': (0.0, 0.1),
     'L0_ffn_up_b': (0.0, 0.267),
     'L0_ffn_down_b': (0.0, 0.1)}
    factors = {}
    for name, (base, spread) in spreads.items():
        noise = np.random.default_rng([zlib.crc32(name.encode()), seed]).standard_normal(out[name].shape)
        drawn = base * np.exp(spread * noise) if base else spread * noise
        out[name] = jnp.asarray(drawn.astype(out[name].dtype))
    for name, factor in factors.items():
        out[name] = (out[name] * factor).astype(out[name].dtype)
    return out
```

```python
from contextlib import ExitStack

import concourse.bass as bass
from concourse import mybir

ALU = mybir.AluOpType
ACT = mybir.ActivationFunctionType
AX = mybir.AxisListType
F32 = mybir.dt.float32
I32 = mybir.dt.int32
U32 = mybir.dt.uint32

P = 128
D = 256
DC = D // P
B = 32
S = 32
K = 257
KM = 256
KT = KM // P
H = 16
HD = D // H
GH = P // S
G = H // GH
HH = H // DC
T = B * S // P
BT = P // S
E = 8
F = 512
FT = F // P
TOK = B * S
NCH = TOK // 512
MASKED = 10000.0
BIG = 3.0e38
LN_EPS = 1e-5
RMS_EPS = 1.1920928955078125e-07
QSCALE = HD ** -0.5
H_FREE = 2
Y_FREE = 4
POOL_STEPS, DVE_STEPS = 3, 23


class Steps:

    def __init__(self, eng, sem):
        self.eng, self.sem, self.n, self.base = eng, sem, 0, 0

    def __call__(self, ins):
        self.n += 1
        ins.then_inc(self.sem, 1)
        self.eng.wait_ge(self.sem, self.base + self.n)


def tile_loop(eng, steps, per_tile, body):
    body(0, True, False, False)
    body(1, True, True, False)
    before = steps.n
    with eng.Fori(2, T) as t:
        steps.base, steps.n = (t - 2) * per_tile + before, 0
        body(t, True, True, True)
        assert steps.n == per_tile, (steps.sem, steps.n)
    steps.base, steps.n = 0, before + (T - 2) * per_tile
    body(T, False, True, True)
    body(T + 1, False, False, True)


def perceiver_program(nc, x, ctxT, ctx_tailT, mask, wqT, wkT, wvT, columns, woT, bo,
                      sqT, skT, svT, soT, sbo, diff_weight,
                      routerT, gate_w, gate_b, up_w, up_b, down_w, down_b, out):
    with ExitStack() as ctx:
        def sb(name, shape, dt=F32):
            return ctx.enter_context(nc.sbuf_tensor(name, shape, dt))

        def sem(name):
            return ctx.enter_context(nc.semaphore(name))

        bank = [ctx.enter_context(nc.psum_tensor(f"bank{i}", [P, 512], F32)) for i in range(8)]

        ident = sb("ident", [P, P])
        ones_col = sb("ones_col", [P, 1])
        ones_rows = sb("ones_rows", [S, P])
        head_mask = sb("head_mask", [P, HH])
        parity = sb("parity", [P, 2])
        expert_no = sb("expert_no", [P, E])
        group_mask = sb("group_mask", [P, D])
        neg_half = sb("neg_half", [P, T])
        wq, wk, wv, wo = (sb(n, [P, DC, D]) for n in ("wq", "wk", "wv", "wo"))
        sq, sk, sv, so_raw, so = (sb(n, [P, DC, D]) for n in ("sq", "sk", "sv", "so_raw", "so"))
        wr = sb("wr", [P, DC, E])
        cols = sb("cols", [P, 4, DC])
        bo_b = sb("bo_b", [P, D])
        sbo_b = sb("sbo_b", [P, D])
        sbo_s = sb("sbo_s", [P, D])
        dw = sb("dw", [P, 1])
        one_m_dw = sb("one_m_dw", [P, 1])
        sign = sb("sign", [P, 2])
        bg_c = sb("bg_c", [P, E, FT])
        bu_c = sb("bu_c", [P, E, FT])
        bd_r = sb("bd_r", [E, D])
        mask_i = sb("mask_i", [P, K], I32)
        masked = sb("masked", [P, K])
        mask_add = sb("mask_add", [P, K])
        all_masked = sb("all_masked", [P, 1])
        row_valid = sb("row_valid", [P, 1])
        valid_diag = sb("valid_diag", [S, S])
        q_factor = sb("q_factor", [P, S])
        x_all = sb("x_all", [P, T, D])
        xn_all = sb("xn_all", [P, T, D])
        xnT_all = sb("xnT_all", [P, DC, TOK])
        qT = sb("qT", [P, DC, TOK])
        stats0 = sb("stats0", [P, T, 6])
        mv0 = sb("mv0", [P, T, 2])
        rstd0 = sb("rstd0", [P, T])
        ctx_tail = sb("ctx_tail", [P, DC, G, B])
        k_tail = sb("k_tail", [P, DC, B])
        v_tail_m = sb("v_tail_m", [P, D])
        shared = sb("shared", [P, B * D])
        v_tail = shared[0:G, :].rearrange("g (b d) -> g b d", b=B)
        ctx_b = [sb(f"ctx{j}", [P, DC, KM]) for j in range(BT)]
        kT = [sb(f"kT{i}", [P, DC, K]) for i in range(2)]
        v = [sb(f"val{i}", [P, KT, D]) for i in range(2)]
        v_end = [sb(f"v_end{i}", [G, D]) for i in range(2)]
        q_bd = [sb(f"q_bd{i}", [P, DC, HH, S]) for i in range(2)]
        s_m = [sb(f"s_m{g}", [P, K]) for g in range(G)]
        s_min = sb("s_min", [P, G])
        p_exp = [sb(f"p_exp{g}", [P, K]) for g in range(G)]
        p_sum = sb("p_sum", [P, G])
        p_inv = sb("p_inv", [P, G])
        p_n = [sb(f"p_n{i}", [P, G, K]) for i in range(2)]
        pT = [sb(f"pT{c}", [P, KT, 2 * P]) for c in range(DC)]
        p_end = sb("p_end", [G, P])
        o_even = sb("o_even", [P, DC, S])
        oT = sb("oT", [P, DC, P])
        x1 = sb("x1", [P, D])
        x1b = sb("x1b", [P, D])
        stats = sb("stats", [P, 6])
        mv = sb("mv", [P, 2])
        rstd = sb("rstd", [P, 1])
        xn1 = sb("xn1", [P, D])
        xn1T = sb("xn1T", [P, DC, P])
        qk1 = sb("qk1", [P, 2, DC, P])
        q1_bd = sb("q1_bd", [P, DC, BT, HH, S])
        v1 = sb("v1", [P, D])
        s1 = sb("s1", [P, H, S])
        s1_max = sb("s1_max", [P, H])
        s1_c = sb("s1_c", [P, H, S])
        p1 = sb("p1", [P, H, S])
        p1_sum = sb("p1_sum", [P, H])
        p1_inv = sb("p1_inv", [P, H])
        p1_fac = sb("p1_fac", [P, H])
        p1_n = sb("p1_n", [P, H, S])
        att = sb("att", [P, H // 2, S])
        attT_bd = sb("attT_bd", [P, H // 2, BT, S])
        o1T = sb("o1T", [P, DC, P])
        o1_sq = sb("o1_sq", [P, DC, P])
        ms = sb("ms", [P, 1])
        rms = sb("rms", [P, 1])
        stats2 = sb("stats2", [P, 6])
        mv2 = sb("mv2", [P, 2])
        rstd2 = sb("rstd2", [P, 1])
        xn2 = sb("xn2", [P, D])
        xn2T = sb("xn2T", [P, DC, P])
        logits = sb("logits", [P, T, E])
        top8 = sb("top8", [P, T, 8])
        top_i = sb("top_i", [P, T, 8], U32)
        top_f = sb("top_f", [P, T, 2])
        hit = sb("hit", [P, 2, T, E])
        lg_c = sb("lg_c", [P, T, E])
        lg_e = sb("lg_e", [P, T, E])
        lg_sum = sb("lg_sum", [P, T])
        lg_inv = sb("lg_inv", [P, T])
        pr = sb("pr", [P, T, E])
        pr_m = sb("pr_m", [P, T, E])
        pr_sum = sb("pr_sum", [P, T])
        pr_inv = sb("pr_inv", [P, T])
        gates = sb("gates", [P, T, E])
        gatesT = sb("gatesT", [E, T, P])
        wg_b = [sb(f"wg{i}", [P, DC, F]) for i in range(2)]
        wu_b = [sb(f"wu{i}", [P, DC, F]) for i in range(2)]
        wd_b = [sb(f"wd{i}", [P, FT, D]) for i in range(2)]
        silu = [sb(f"silu{i}", [P, 512]) for i in range(2)]
        hT = [shared[:, i * FT * 512:(i + 1) * FT * 512].rearrange("p (f n) -> p f n", f=FT) for i in range(2)]
        token = sb("token", [P, 6])

        x_in, small_in, wq_in, wkv_in, wo_in, self_in, tail_in, vtail_in = (
            sem(n) for n in ("x_in", "small_in", "wq_in", "wkv_in", "wo_in", "self_in", "tail_in", "vtail_in"))
        mask_in = sem("mask_in")
        ctx_in = [sem(f"ctx_in{j}") for j in range(BT)]
        experts_in = [sem(f"experts_in{i}") for i in range(2)]
        out_done = sem("out_done")
        pool_steps, dve_steps, act_steps = sem("pool_steps"), sem("dve_steps"), sem("act_steps")
        consts_ready, var0_ready, rstd0_ready, xn0_ready = (
            sem(n) for n in ("consts_ready", "var0_ready", "rstd0_ready", "xn0_ready"))
        xT0_ps, xT0_evac, q0_ps, q0_evac, valid_diag_ready, valid_ps, q_factor_ready = (
            sem(n) for n in ("xT0_ps", "xT0_evac", "q0_ps", "q0_evac", "valid_diag_ready", "valid_ps", "q_factor_ready"))
        ktail_ps, tails_evac, vtail_ps, xb_ready = (
            sem(n) for n in ("ktail_ps", "tails_evac", "vtail_ps", "xb_ready"))
        k_ps, k_evac, v_ps, v_evac, batch_ready = (
            sem(n) for n in ("k_ps", "k_evac", "v_ps", "v_evac", "batch_ready"))
        s_ps, s_masked, exp_done, p_normed = (sem(n) for n in ("s_ps", "s_masked", "exp_done", "p_normed"))
        pT_ps, pT0_evac, pT1_evac, end_ps, end_evac, o_ps, o_evac = (
            sem(n) for n in ("pT_ps", "pT0_evac", "pT1_evac", "end_ps", "end_evac", "o_ps", "o_evac"))
        y_ps, var1_ready, x1_ready, rstd1_ready, xn1_ready, x1T_ps, x1T_evac = (
            sem(n) for n in ("y_ps", "var1_ready", "x1_ready", "rstd1_ready", "xn1_ready", "x1T_ps", "x1T_evac"))
        qk1_ps, qk1_evac, q1_bd_ready, v1_ps, v1_evac, s1_ps, s1_evac = (
            sem(n) for n in ("qk1_ps", "qk1_evac", "q1_bd_ready", "v1_ps", "v1_evac", "s1_ps", "s1_evac"))
        s1_ready, exp1_done, attT_ready, o1_ps, o1_evac, y1_ps, ms_ready, rms_ready = (
            sem(n) for n in ("s1_ready", "exp1_done", "attT_ready", "o1_ps", "o1_evac", "y1_ps", "ms_ready", "rms_ready"))
        var2_ready, rstd2_ready, xn2_ready, x2T_ps, x2T_evac, x2T_kept, lg_ps, lg_evac = (
            sem(n) for n in ("var2_ready", "rstd2_ready", "xn2_ready", "x2T_ps", "x2T_evac", "x2T_kept", "lg_ps", "lg_evac"))
        lg_centred, lg_exp, gates_ready, gT_ps, gT_evac, bd_ps, y_seeded = (
            sem(n) for n in ("lg_centred", "lg_exp", "gates_ready", "gT_ps", "gT_evac", "bd_ps", "y_seeded"))
        gate_ps, up_ps, silu_done, h_ready, down_ps, y_added = (
            sem(n) for n in ("gate_ps", "up_ps", "silu_done", "h_ready", "down_ps", "y_added"))

        def settle(eng):
            eng.nop(nofuse=True)

        block = ctx.enter_context(nc.Block())

        def halves(w):
            return w.rearrange("(c p) n -> p c n", p=P)

        @block.sync
        def _(sp):
            sp.dma_start(x_all[:, :, :], x.rearrange("(t p) d -> p t d", p=P)).then_inc(x_in, 16)
            sp.dma_start(cols[:, :, :], columns).then_inc(small_in, 16)
            sp.dma_start(bo_b[:, :], bo.partition_broadcast(P)).then_inc(small_in, 16)
            sp.dma_start(sbo_b[:, :], sbo.partition_broadcast(P)).then_inc(small_in, 16)
            sp.dma_start(dw[:, :], diff_weight.partition_broadcast(P)).then_inc(small_in, 16)
            for h in range(GH):
                sp.dma_start(mask_i[h * S:(h + 1) * S, :], mask).then_inc(mask_in, 16)
            sp.dma_start(wq[:, :, :], halves(wqT)).then_inc(wq_in, 16)
            for g in range(G):
                sp.dma_start(ctx_tail[:, :, g, :], halves(ctx_tailT)).then_inc(tail_in, 16)
            sp.dma_start(wk[:, :, :], halves(wkT)).then_inc(wkv_in, 16)
            sp.dma_start(wv[:, :, :], halves(wvT)).then_inc(wkv_in, 16)

            def load_context(t, j):
                sp.dma_start(ctx_b[j][:, :, :],
                             ctxT.rearrange("(c p) (t j) k -> p c t j k", p=P, j=BT)[:, :, t, j, 0:KM]
                             ).then_inc(ctx_in[j], 16)

            for j in range(BT):
                load_context(0, j)
            sp.dma_start(wo[:, :, :], halves(woT)).then_inc(wo_in, 16)
            for dst, src in ((sq, sqT), (sk, skT), (sv, svT), (so_raw, soT), (wr, routerT)):
                sp.dma_start(dst[:, :, :], halves(src)).then_inc(self_in, 16)
            sp.dma_start(bg_c[:, :, :], gate_b).then_inc(self_in, 16)
            sp.dma_start(bu_c[:, :, :], up_b).then_inc(self_in, 16)
            sp.dma_start(bd_r[:, :], down_b).then_inc(self_in, 16)
            sp.wait_ge(tails_evac, 2)
            sp.dma_start(v_tail[:, :, :].rearrange("g b d -> g (b d)"), v_tail_m[:, :]).then_inc(vtail_in, 16)

            def load_expert(e, i):
                sp.dma_start(wg_b[i][:, :, :], gate_w.rearrange("e (c p) f -> p e c f", p=P)[:, e, :, :]
                             ).then_inc(experts_in[i], 16)
                sp.dma_start(wu_b[i][:, :, :], up_w.rearrange("e (c p) f -> p e c f", p=P)[:, e, :, :]
                             ).then_inc(experts_in[i], 16)
                sp.dma_start(wd_b[i][:, :, :], down_w.rearrange("e (c p) f -> p e c f", p=P)[:, e, :, :]
                             ).then_inc(experts_in[i], 16)

            for i in range(2):
                load_expert(i, i)
            with sp.Fori(1, T) as t:
                for j in range(BT):
                    sp.wait_ge(v_ps, t * BT + (j - BT + 1))
                    load_context(t, j)
            with sp.Fori(1, E // 2) as pair:
                for i in range(2):
                    sp.wait_ge(down_ps, (pair * 2 + (i - 1)) * NCH)
                    load_expert(pair * 2 + i, i)
            for n in range(NCH):
                sp.wait_ge(y_added, Y_FREE + 4 * ((E - 1) * NCH + n + 1))
                sp.dma_start(out.rearrange("(t p) d -> p t d", p=P)[:, 4 * n:4 * n + 4, :],
                             xn_all[:, 4 * n:4 * n + 4, :]).then_inc(out_done, 16)
            sp.wait_ge(out_done, 16 * NCH)

        @block.gpsimd
        def _(pool):
            step = Steps(pool, pool_steps)
            g = nc.gpsimd
            g.memset(ident[:, :], 0.0)
            g.memset(ones_col[:, :], 1.0)
            g.memset(ones_rows[:, :], 1.0)
            g.memset(neg_half[:, :], -0.5)
            g.memset(attT_bd[:, :, :, :], 0.0)
            for e in range(E):
                g.memset(expert_no[:, e:e + 1], float(e))
            step(g.memset(head_mask[:, :], 1.0))
            step(g.affine_select(out=head_mask[:, :], in_=head_mask[:, :], compare_op=ALU.is_ge, fill=0.0,
                                 base=0, pattern=[[-HD, HH]], channel_multiplier=1))
            g.affine_select(out=ident[:, :], in_=ident[:, :], compare_op=ALU.not_equal, fill=1.0,
                            base=0, pattern=[[-1, P]], channel_multiplier=1)
            g.affine_select(out=head_mask[:, :], in_=head_mask[:, :], compare_op=ALU.is_ge, fill=0.0,
                            base=HD - 1, pattern=[[HD, HH]], channel_multiplier=-1).then_inc(consts_ready, 1)
            pool.wait_ge(var0_ready, 1)
            step(g.tensor_scalar(rstd0[:, :], mv0[:, :, 1], LN_EPS, None, ALU.add))
            g.tensor_tensor(rstd0[:, :], rstd0[:, :], neg_half[:, :], ALU.pow).then_inc(rstd0_ready, 1)
            pool.wait_ge(xn0_ready, T)
            pool.wait_ge(small_in, 16 * 4)
            g.tensor_tensor(x_all[:, :, :], x_all[:, :, :],
                            bo_b[:, :].unsqueeze(1).to_broadcast([P, T, D]), ALU.add).then_inc(xb_ready, 1)

            def prepare_batch(t, j):
                i = j % 2
                b = t * BT + j
                if not isinstance(t, int) or b >= 2:
                    pool.wait_ge(o_ps, b - 1)
                g.tensor_tensor(
                    q_bd[i][:, :, :, :],
                    qT[:, :, bass.ds(b * S, S)].unsqueeze(2).to_broadcast([P, DC, HH, S]),
                    head_mask[:, :].unsqueeze(1).unsqueeze(3).to_broadcast([P, DC, HH, S]), ALU.mult)
                g.tensor_copy(kT[i][:, :, KM:K], k_tail[:, :, bass.ds(b, 1)]).then_inc(batch_ready, 1)

            pool.wait_ge(q0_evac, 2 * NCH)
            pool.wait_ge(tails_evac, 2)

            def body(t, cross, attend, close):
                if cross:
                    prepare_batch(t, 0)
                if close:
                    pool.wait_ge(ms_ready, t - 1)
                    step(g.tensor_tensor(rms[:, :], ms[:, :], neg_half[:, 0:1], ALU.pow))
                    settle(pool)
                    g.tensor_scalar(rms[:, :], rms[:, :], one_m_dw[:, 0:1], None, ALU.mult).then_inc(rms_ready, 1)
                    pool.wait_ge(var2_ready, t - 1)
                    settle(pool)
                    step(g.tensor_scalar(rstd2[:, :], mv2[:, 1:2], LN_EPS, None, ALU.add))
                    g.tensor_tensor(rstd2[:, :], rstd2[:, :], neg_half[:, 0:1], ALU.pow).then_inc(rstd2_ready, 1)
                if cross:
                    prepare_batch(t, 1)
                if close:
                    pool.wait_ge(x2T_evac, t - 1)
                    g.tensor_copy(xnT_all[:, :, bass.ds((t - 2) * P, P)], xn2T[:, :, :]).then_inc(x2T_kept, 1)
                if attend:
                    pool.wait_ge(var1_ready, t)
                    settle(pool)
                    step(g.tensor_scalar(rstd[:, :], mv[:, 1:2], LN_EPS, None, ALU.add))
                    g.tensor_tensor(rstd[:, :], rstd[:, :], neg_half[:, 0:1], ALU.pow).then_inc(rstd1_ready, 1)
                if cross:
                    prepare_batch(t, 2)
                if attend:
                    pool.wait_ge(qk1_evac, t)
                    q4 = qk1[:, 0, :, :].rearrange("p c (b q) -> p c b q", b=BT)
                    for c in range(DC):
                        ins = g.tensor_tensor(
                            q1_bd[:, c, :, :, :],
                            q4[:, c, :, :].unsqueeze(2).to_broadcast([P, BT, HH, S]),
                            head_mask[:, :].unsqueeze(1).unsqueeze(3).to_broadcast([P, BT, HH, S]), ALU.mult)
                    ins.then_inc(q1_bd_ready, 1)
                if cross:
                    prepare_batch(t, 3)

            tile_loop(pool, step, POOL_STEPS, body)

        @block.tensor
        def _(pe):
            step = Steps(pe, None)
            mm = nc.tensor.matmul
            pe.wait_ge(consts_ready, 1)
            for t in range(T):
                pe.wait_ge(xn0_ready, t + 1)
                for c in range(DC):
                    ins = nc.tensor.transpose(bank[t // 2][:, ((t % 2) * DC + c) * P:((t % 2) * DC + c + 1) * P],
                                              xn_all[:, t, c * P:(c + 1) * P], ident[:, :])
                ins.then_inc(xT0_ps, 1)
            pe.wait_ge(wq_in, 16)
            for n in range(NCH):
                pe.wait_ge(xT0_evac, 2 * (n + 1))
                for oc in range(DC):
                    for c in range(DC):
                        ins = mm(bank[4 + 2 * n + oc][:, :], wq[:, c, oc * P:(oc + 1) * P],
                                 xnT_all[:, c, n * 512:(n + 1) * 512], start=(c == 0), stop=(c == DC - 1))
                    ins.then_inc(q0_ps, 1)
            pe.wait_ge(valid_diag_ready, 1)
            mm(bank[0][:, 0:S], ones_rows[:, :], valid_diag[:, :], start=True, stop=True).then_inc(valid_ps, 1)
            pe.wait_ge(tail_in, 16 * G)
            pe.wait_ge(wkv_in, 32)
            for oc in range(DC):
                for c in range(DC):
                    ins = mm(bank[1][:, oc * B:(oc + 1) * B], wk[:, c, oc * P:(oc + 1) * P], ctx_tail[:, c, 0, :],
                             start=(c == 0), stop=(c == DC - 1))
            ins.then_inc(ktail_ps, 1)
            for c in range(DC):
                ins = mm(bank[2][:, 0:D], ctx_tail[:, c, :, :].rearrange("p g b -> p (g b)"), wv[:, c, :],
                         start=(c == 0), stop=(c == DC - 1))
            ins.then_inc(vtail_ps, 1)
            pe.wait_ge(q_factor_ready, 1)
            pe.wait_ge(tails_evac, 2)
            pe.wait_ge(q0_evac, 2 * NCH)

            def first(t, n=0):
                return isinstance(t, int) and t <= n

            def project(t, j):
                b = t * BT + j
                pe.wait_ge(ctx_in[j], 16 * (t + 1))
                if not first(b):
                    pe.wait_ge(k_evac, b)
                for oc in range(DC):
                    for c in range(DC):
                        ins = mm(bank[0][:, oc * KM:(oc + 1) * KM], wk[:, c, oc * P:(oc + 1) * P], ctx_b[j][:, c, :],
                                 start=(c == 0), stop=(c == DC - 1))
                ins.then_inc(k_ps, 1)
                if not first(b):
                    pe.wait_ge(v_evac, b)
                for kt in range(KT):
                    for c in range(DC):
                        ins = mm(bank[1][:, kt * D:(kt + 1) * D], ctx_b[j][:, c, kt * P:(kt + 1) * P], wv[:, c, :],
                                 start=(c == 0), stop=(c == DC - 1))
                ins.then_inc(v_ps, 1)

            def scores(t, j, c):
                b = t * BT + j
                i = j % 2
                if c == 0:
                    pe.wait_ge(k_evac, b + 1)
                    pe.wait_ge(batch_ready, b + 1)
                for g in (2 * c, 2 * c + 1):
                    if not (isinstance(b, int) and b == 0 and g < 2):
                        pe.wait_ge(s_masked, 4 * b + g - 1)
                    mm(bank[2 + g % 2][:, 0:K],
                       q_bd[i][:, c, (g % 2) * GH:(g % 2 + 1) * GH, :].rearrange("p h q -> p (h q)"),
                       kT[i][:, c, :], start=True, stop=True).then_inc(s_ps, 1)

            def turn(t, j, c):
                b = t * BT + j
                pe.wait_ge(p_normed, 4 * b + 2 * c + 2)
                if not first(b):
                    pe.wait_ge(pT0_evac if c == 0 else pT1_evac, b)
                for kt in range(KT):
                    for g in range(2):
                        ins = nc.tensor.transpose(bank[4 + c][:, kt * 2 * P + g * P:kt * 2 * P + (g + 1) * P],
                                                  p_n[j % 2][:, 2 * c + g, kt * P:(kt + 1) * P], ident[:, :])
                ins.then_inc(pT_ps, 1)
                if c == 1:
                    if not first(b):
                        pe.wait_ge(o_evac, b)
                    nc.tensor.transpose(bank[6][0:G, P:2 * P], p_n[j % 2][:, :, KM:K].squeeze(2),
                                        ident[:, :]).then_inc(end_ps, 1)

            def weigh(t, j):
                b = t * BT + j
                pe.wait_ge(v_evac, b + 1)
                pe.wait_ge(pT0_evac, b + 1)
                pe.wait_ge(pT1_evac, b + 1)
                pe.wait_ge(end_evac, b + 1)
                for c in range(DC):
                    for kt in range(KT + 1):
                        for r in range(4):
                            o = bank[6][32 * r:32 * r + 32, c * 64:(c + 1) * 64]
                            d0 = c * P + 32 * r
                            if kt < KT:
                                ins = mm(o, v[j % 2][:, kt, d0:d0 + 32], pT[c][:, kt, 64 * r:64 * r + 64],
                                         start=(kt == 0), stop=False)
                            else:
                                ins = mm(o, v_end[j % 2][:, d0:d0 + 32], p_end[:, (64 * r) % P:(64 * r) % P + 64],
                                         start=False, stop=True)
                ins.then_inc(o_ps, 1)

            misc = bank[7]

            def close_weigh(t):
                pe.wait_ge(attT_ready, t - 1)
                for h in range(H // 2):
                    r, c = h % 4, h // 4
                    ins = mm(misc[32 * r:32 * r + 32, c * P:(c + 1) * P], v1[:, 32 * h:32 * h + 32],
                             attT_bd[:, h, :, :].rearrange("p b q -> p (b q)"), start=True, stop=True)
                ins.then_inc(o1_ps, 1)

            def close_project(t):
                pe.wait_ge(o1_evac, 2 * (t - 1))
                for c in range(DC):
                    mm(misc[:, 0:D], o1T[:, c, :], so[:, c, :], start=(c == 0), stop=(c == DC - 1))
                for c in range(DC):
                    ins = mm(misc[:, D:D + 1], o1_sq[:, c, :], ones_col[:, :], start=(c == 0), stop=(c == DC - 1))
                ins.then_inc(y1_ps, 1)

            def turn_rows(rows, ready, count, done):
                pe.wait_ge(ready, count)
                for c in range(DC):
                    ins = nc.tensor.transpose(misc[:, c * P:(c + 1) * P], rows[:, c * P:(c + 1) * P], ident[:, :])
                ins.then_inc(done, 1)

            def close_route(t):
                pe.wait_ge(x2T_evac, t - 1)
                for c in range(DC):
                    ins = mm(misc[:, 0:E], xn2T[:, c, :], wr[:, c, :], start=(c == 0), stop=(c == DC - 1))
                ins.then_inc(lg_ps, 1)

            def attend_project(t):
                if first(t, 1):
                    pe.wait_ge(wo_in, 16)
                pe.wait_ge(o_evac, BT * t)
                if not first(t, 1):
                    pe.wait_ge(lg_evac, t - 1)
                for c in range(DC):
                    ins = mm(misc[:, 0:D], oT[:, c, :], wo[:, c, :], start=(c == 0), stop=(c == DC - 1))
                ins.then_inc(y_ps, 1)

            def attend_qk(t):
                if first(t, 1):
                    pe.wait_ge(self_in, 16 * 8)
                pe.wait_ge(x1T_evac, t)
                for n, w in enumerate((sq, sk)):
                    for oc in range(DC):
                        for c in range(DC):
                            ins = mm(misc[:, (n * DC + oc) * P:(n * DC + oc + 1) * P],
                                     w[:, c, oc * P:(oc + 1) * P], xn1T[:, c, :], start=(c == 0), stop=(c == DC - 1))
                ins.then_inc(qk1_ps, 1)

            def attend_v(t):
                pe.wait_ge(qk1_evac, t)
                for c in range(DC):
                    ins = mm(misc[:, 0:D], xn1T[:, c, :], sv[:, c, :], start=(c == 0), stop=(c == DC - 1))
                ins.then_inc(v1_ps, 1)

            def attend_scores(t):
                pe.wait_ge(v1_evac, t)
                pe.wait_ge(q1_bd_ready, t)
                for c in range(DC):
                    for b in range(BT):
                        ins = mm(misc[32 * b:32 * b + 32, c * 256:(c + 1) * 256], qk1[:, 1, c, b * S:(b + 1) * S],
                                 q1_bd[:, c, b, :, :].rearrange("p h q -> p (h q)"), start=True, stop=True)
                ins.then_inc(s1_ps, 1)

            def body(t, cross, attend, close):
                for j in range(BT):
                    pt, pj = (t, j - 1) if j else (t - 1, BT - 1)
                    has_prev = cross if j else (not first(t) and (cross or attend))
                    if cross:
                        project(t, j)
                    if j == 0 and close:
                        close_weigh(t)
                    if j == 1 and close:
                        turn_rows(xn2, xn2_ready, t - 1, x2T_ps)
                    if j == 2 and attend:
                        turn_rows(xn1, xn1_ready, t, x1T_ps)
                    if j == 3 and attend:
                        attend_scores(t)
                    if has_prev:
                        turn(pt, pj, 0)
                    if cross:
                        scores(t, j, 0)
                    if j == 1 and close:
                        close_route(t)
                    if j == 2 and attend:
                        attend_qk(t)
                    if has_prev:
                        turn(pt, pj, 1)
                    if cross:
                        scores(t, j, 1)
                    if j == 0 and close:
                        close_project(t)
                    if j == 1 and attend:
                        attend_project(t)
                    if j == 2 and attend:
                        attend_v(t)
                    if has_prev:
                        weigh(pt, pj)

            tile_loop(pe, step, 0, body)

            for t in range(T):
                pe.wait_ge(gates_ready, 1)
                if t == 0:
                    pe.wait_ge(lg_evac, T)
                if t >= 2:
                    pe.wait_ge(gT_evac, t - 1)
                nc.tensor.transpose(bank[t % 2][0:E, 0:P], gates[:, t, :], ident[:, :]).then_inc(gT_ps, 1)
                pe.wait_ge(gT_evac, t + 1)
                if t >= 2:
                    pe.wait_ge(y_seeded, t - 1)
                mm(bank[2 + t % 2][:, 0:D], gatesT[:, t, :], bd_r[:, :], start=True, stop=True).then_inc(bd_ps, 1)
            pe.wait_ge(y_seeded, T)
            pe.wait_ge(x2T_kept, T)
            with pe.Fori(0, E // 2) as pair:
                for i in range(2):
                    pe.wait_ge(experts_in[i], 48 * (pair + 1))
                    for n in range(NCH):
                        q0 = (pair * 2 + i) * NCH + n
                        for f in range(FT):
                            for w, bk0, done in ((wg_b[i], 0, gate_ps), (wu_b[i], 2, up_ps)):
                                pe.wait_ge(h_ready, q0 * FT + f + 1)
                                for c in range(DC):
                                    ins = mm(bank[bk0 + f % 2][:, :], w[:, c, f * P:(f + 1) * P],
                                             xnT_all[:, c, n * 512:(n + 1) * 512], start=(c == 0), stop=(c == DC - 1))
                                ins.then_inc(done, 1)
                        for f in range(FT):
                            pe.wait_ge(h_ready, q0 * FT + f + 1 + H_FREE)
                            for k in range(4):
                                if f == 0:
                                    pe.wait_ge(y_added, q0 * 4 + k + 1)
                                ins = mm(bank[4 + k][:, 0:D], hT[n % 2][:, f, k * P:(k + 1) * P], wd_b[i][:, f, :],
                                         start=(f == 0), stop=(f == FT - 1))
                        ins.then_inc(down_ps, 1)

        @block.scalar
        def _(act):
            a = nc.scalar
            for i in range(T // 2):
                act.wait_ge(xT0_ps, 2 * i + 2)
                a.copy(xnT_all[:, :, 2 * i * P:(2 * i + 2) * P].rearrange("p c (t k) -> p t c k", t=2),
                       bank[i][:, :].rearrange("p (t c k) -> p t c k", t=2, c=DC)).then_inc(xT0_evac, 1)
            act.wait_ge(small_in, 16 * 4)
            act.wait_ge(vtail_in, 16)

            def body(t, cross, attend, close):
                misc = bank[7]
                turned = misc[:, 0:DC * P].rearrange("p (c k) -> p c k", c=DC)
                for j in range(BT):
                    b = t * BT + j
                    i = j % 2
                    has_prev = cross if j else (not (isinstance(t, int) and t <= 0) and (cross or attend))
                    if cross:
                        act.wait_ge(k_ps, b + 1)
                        for oc in range(DC):
                            ins = a.activation(kT[i][:, oc, 0:KM], bank[0][:, oc * KM:(oc + 1) * KM], ACT.Identity,
                                               bias=cols[:, 1, oc:oc + 1])
                        ins.then_inc(k_evac, 1)
                        act.wait_ge(v_ps, b + 1)
                        a.copy(v_end[i][:, :], v_tail[:, bass.ds(b, 1), :].squeeze(1))
                        a.copy(v[i][:, :, :], bank[1][:, :].rearrange("p (k d) -> p k d", k=KT)).then_inc(v_evac, 1)
                    if j == 0 and close:
                        act.wait_ge(o1_ps, t - 1)
                        a.copy(o1T[:, :, :], turned).then_inc(o1_evac, 1)
                        a.activation(o1_sq[:, :, :], turned, ACT.Square).then_inc(o1_evac, 1)
                    if j == 1 and close:
                        act.wait_ge(x2T_ps, t - 1)
                        if not (isinstance(t, int) and t <= 2):
                            act.wait_ge(x2T_kept, t - 2)
                        a.copy(xn2T[:, :, :], turned).then_inc(x2T_evac, 1)
                    if j == 2 and attend:
                        act.wait_ge(x1T_ps, t)
                        a.copy(xn1T[:, :, :], turned).then_inc(x1T_evac, 1)
                    if has_prev:
                        act.wait_ge(pT_ps, 2 * b - 1)
                        a.copy(pT[0][:, :, :], bank[4][:, :].rearrange("p (k n) -> p k n", k=KT)).then_inc(pT0_evac, 1)
                    for g in range(G):
                        if cross:
                            act.wait_ge(s_masked, 4 * b + g + 1)
                            if not (isinstance(b, int) and b == 0):
                                act.wait_ge(p_normed, 4 * (b - 1) + g + 1)
                            a.activation(p_exp[g][:, :], s_m[g][:, :], ACT.Exp, bias=s_min[:, g:g + 1], scale=-1.0,
                                         accum_out=p_sum[:, g:g + 1]).then_inc(exp_done, 1)
                        if g == 1 and j == 2 and attend:
                            act.wait_ge(qk1_ps, t)
                            a.activation(qk1[:, :, :, :], misc[:, :].rearrange("p (n c k) -> p n c k", n=2, c=DC),
                                         ACT.Copy, scale=QSCALE ** 0.5).then_inc(qk1_evac, 1)
                        if g == 1 and j == 3 and attend:
                            act.wait_ge(s1_ready, t)
                            a.activation(p1[:, :, :], s1_c[:, :, :], ACT.Exp).then_inc(exp1_done, 1)
                        if g == 3 and j == 2 and attend:
                            act.wait_ge(v1_ps, t)
                            a.copy(v1[:, :], misc[:, 0:D]).then_inc(v1_evac, 1)

            tile_loop(act, Steps(act, act_steps), 0, body)
            act.wait_ge(lg_centred, 1)
            a.activation(lg_e[:, :, :], lg_c[:, :, :], ACT.Exp).then_inc(lg_exp, 1)
            for t in range(T):
                act.wait_ge(gT_ps, t + 1)
                a.copy(gatesT[:, t, :], bank[t % 2][0:E, 0:P]).then_inc(gT_evac, 1)
            with act.Fori(0, E // 2) as pair:
                for i in range(2):
                    for n in range(NCH):
                        for f in range(FT):
                            m = ((pair * 2 + i) * NCH + n) * FT + f
                            act.wait_ge(gate_ps, m + 1)
                            act.wait_ge(h_ready, m + 1)
                            settle(act)
                            a.activation(silu[f % 2][:, :], bank[f % 2][:, :], ACT.Silu,
                                         bias=bg_c[:, bass.ds(pair * 2 + i, 1), f:f + 1].squeeze(2)
                                         ).then_inc(silu_done, 1)

        @block.vector
        def _(dve):
            step = Steps(dve, dve_steps)
            w = nc.vector
            dve.wait_ge(x_in, 16)
            for t in range(T):
                w.bn_stats(stats0[:, t, :], x_all[:, t, :])
            step(w.memset(token[:, :], 0.0))
            for t in range(T):
                ins = w.bn_aggr(mv0[:, t, :], stats0[:, t, :])
            ins.then_inc(var0_ready, 1)
            step(w.memset(group_mask[:, :], 0.0))
            for i in range(G):
                ins = w.memset(group_mask[i * B:(i + 1) * B, i * (D // G):(i + 1) * (D // G)], 1.0)
            step(ins)
            dve.wait_ge(mask_in, 16 * GH)
            step(w.tensor_scalar(masked[:, :], mask_i[:, :], 0.0, 1.0, ALU.is_equal, ALU.mult))
            w.tensor_scalar(mask_add[:, :], masked[:, :], MASKED, None, ALU.mult)
            step(w.tensor_reduce(all_masked[:, :], masked[:, :], AX.X, ALU.min))
            step(w.tensor_scalar(row_valid[:, :], all_masked[:, :], -1.0, 1.0, ALU.mult, ALU.add))
            dve.wait_ge(consts_ready, 1)
            w.tensor_scalar(valid_diag[:, :], ident[0:S, 0:S], row_valid[0:S, 0:1], None, ALU.mult
                            ).then_inc(valid_diag_ready, 1)
            dve.wait_ge(rstd0_ready, 1)
            for t in range(T):
                w.tensor_scalar(xn_all[:, t, :], x_all[:, t, :], mv0[:, t, 0:1], rstd0[:, t:t + 1],
                                ALU.subtract, ALU.mult).then_inc(xn0_ready, 1)
            dve.wait_ge(valid_ps, 1)
            w.tensor_scalar(q_factor[:, :], bank[0][:, 0:S], -QSCALE, None, ALU.mult).then_inc(q_factor_ready, 1)
            dve.wait_ge(q_factor_ready, 1)
            dve.wait_ge(small_in, 16 * 4)
            for n in range(NCH):
                for oc in range(DC):
                    dve.wait_ge(q0_ps, 2 * n + oc + 1)
                    w.scalar_tensor_tensor(
                        qT[:, oc, n * 512:(n + 1) * 512].rearrange("p (b q) -> p b q", q=S),
                        bank[4 + 2 * n + oc][:, :].rearrange("p (b q) -> p b q", q=S), cols[:, 0, oc:oc + 1],
                        q_factor[:, :].unsqueeze(1).to_broadcast([P, 512 // S, S]), ALU.add, ALU.mult
                        ).then_inc(q0_evac, 1)
            dve.wait_ge(ktail_ps, 1)
            for oc in range(DC):
                ins = w.tensor_scalar(k_tail[:, oc, :], bank[1][:, oc * B:(oc + 1) * B], cols[:, 1, oc:oc + 1], None,
                                      ALU.add)
            ins.then_inc(tails_evac, 1)
            dve.wait_ge(vtail_ps, 1)
            w.tensor_tensor(v_tail_m[:, :], bank[2][:, 0:D], group_mask[:, :], ALU.mult).then_inc(tails_evac, 1)
            w.tensor_reduce(parity[:, :], head_mask[:, :].rearrange("p (a b) -> p b a", b=2), AX.X, ALU.add)
            w.memset(sign[:, 0:1], 1.0)
            w.tensor_scalar(sign[:, 1:2], dw[:, :], -1.0, None, ALU.mult)
            step(w.tensor_scalar(one_m_dw[:, :], dw[:, :], -1.0, 1.0, ALU.mult, ALU.add))
            w.tensor_scalar(sbo_s[:, :], sbo_b[:, :], one_m_dw[:, 0:1], None, ALU.mult)
            dve.wait_ge(self_in, 16 * 8)
            for c in range(DC):
                ins = w.tensor_scalar(so[:, c, :], so_raw[:, c, :], cols[:, 3, c:c + 1], None, ALU.mult)
            step(ins)

            def mask_scores(t, j, g):
                b = t * BT + j
                dve.wait_ge(s_ps, 4 * b + g + 1)
                if not (isinstance(b, int) and b == 0):
                    dve.wait_ge(exp_done, 4 * (b - 1) + g + 1)
                settle(dve)
                w.tensor_tensor_reduce(out=s_m[g][:, :], in0=bank[2 + g % 2][:, 0:K], in1=mask_add[:, :], scale=1.0,
                                       scalar=BIG, op0=ALU.add, op1=ALU.min, accum_out=s_min[:, g:g + 1]
                                       ).then_inc(s_masked, 1)

            def normalise(t, j, c):
                b = t * BT + j
                dve.wait_ge(exp_done, 4 * b + 2 * c + 2)
                step(w.reciprocal(p_inv[:, 2 * c:2 * c + 2], p_sum[:, 2 * c:2 * c + 2]))
                for g in (2 * c, 2 * c + 1):
                    w.tensor_scalar(p_n[j % 2][:, g, :], p_exp[g][:, :], p_inv[:, g:g + 1], None, ALU.mult
                                    ).then_inc(p_normed, 1)

            def norm_stats(x_ap, st, m, ready):
                settle(dve)
                step(w.bn_stats(st[:, :], x_ap))
                settle(dve)
                w.bn_aggr(m[:, :], st[:, :]).then_inc(ready, 1)

            def body(t, cross, attend, close):
                misc = bank[7]
                x2 = xn_all[:, bass.ds(t - 2, 1), :].squeeze(1) if close else None
                for j in range(BT):
                    b = t * BT + j
                    pj = (j - 1) % BT
                    has_prev = cross if j else (not (isinstance(t, int) and t <= 0) and (cross or attend))
                    if j == 1 and close:
                        dve.wait_ge(rstd2_ready, t - 1)
                        w.tensor_scalar(xn2[:, :], x2, mv2[:, 0:1], rstd2[:, 0:1], ALU.subtract, ALU.mult
                                        ).then_inc(xn2_ready, 1)
                    if j == 2 and attend:
                        dve.wait_ge(rstd1_ready, t)
                        w.tensor_scalar(xn1[:, :], x1[:, :], mv[:, 0:1], rstd[:, 0:1], ALU.subtract, ALU.mult
                                        ).then_inc(xn1_ready, 1)
                    if j == 3 and attend:
                        dve.wait_ge(s1_ps, t)
                        step(w.transpose(s1[:, :, :].rearrange("p h k -> p (h k)"), misc[:, :]))
                        step(w.tensor_reduce(s1_max[:, :], s1[:, :, :], AX.X, ALU.max))
                        w.tensor_tensor(s1_c[:, :, :], s1[:, :, :],
                                        s1_max[:, :].unsqueeze(2).to_broadcast([P, H, S]), ALU.subtract
                                        ).then_inc(s1_ready, 1)
                    if cross:
                        mask_scores(t, j, 0)
                        mask_scores(t, j, 1)
                    if j == 1 and close:
                        dve.wait_ge(lg_ps, t - 1)
                        w.tensor_copy(logits[:, bass.ds(t - 2, 1), :].squeeze(1), misc[:, 0:E]).then_inc(lg_evac, 1)
                    if has_prev:
                        dve.wait_ge(pT_ps, 2 * b)
                        w.tensor_copy(pT[1][:, :, :], bank[5][:, :].rearrange("p (k n) -> p k n", k=KT)
                                      ).then_inc(pT1_evac, 1)
                        dve.wait_ge(end_ps, b)
                        w.tensor_copy(p_end[:, :], bank[6][0:G, P:2 * P]).then_inc(end_evac, 1)
                    if cross:
                        normalise(t, j, 0)
                        mask_scores(t, j, 2)
                        mask_scores(t, j, 3)
                    if j == 0 and close:
                        dve.wait_ge(y1_ps, t - 1)
                        w.tensor_scalar(ms[:, :], misc[:, D:D + 1], 1.0 / D, RMS_EPS, ALU.mult, ALU.add
                                        ).then_inc(ms_ready, 1)
                    if j == 1 and attend:
                        dve.wait_ge(y_ps, t)
                        if isinstance(t, int) and t == 1:
                            dve.wait_ge(xb_ready, 1)
                        step(w.tensor_tensor(x1[:, :], misc[:, 0:D], x_all[:, bass.ds(t - 1, 1), :].squeeze(1),
                                             ALU.add))
                        w.tensor_tensor(x1b[:, :], x1[:, :], sbo_s[:, :], ALU.add)
                        norm_stats(x1[:, :], stats, mv, var1_ready)
                    if cross:
                        normalise(t, j, 1)
                    if has_prev:
                        dve.wait_ge(o_ps, b)
                        o4 = bank[6][:, 0:P].rearrange("p (c a q) -> p c a q", c=DC, a=2)
                        for c in range(DC):
                            ins = w.tensor_scalar(o_even[:, c, :], o4[:, c, 0, :], parity[:, 0:1], cols[:, 2, c:c + 1],
                                                  ALU.mult, ALU.add)
                        step(ins)
                        w.scalar_tensor_tensor(oT[:, :, pj * S:(pj + 1) * S], o4[:, :, 1, :], parity[:, 1:2],
                                               o_even[:, :, :], ALU.mult, ALU.add).then_inc(o_evac, 1)
                    if j == 0 and close:
                        dve.wait_ge(rms_ready, t - 1)
                        step(w.scalar_tensor_tensor(x2, misc[:, 0:D], rms[:, 0:1], x1b[:, :], ALU.mult, ALU.add))
                        norm_stats(x2, stats2, mv2, var2_ready)
                    if j == 3 and attend:
                        dve.wait_ge(exp1_done, t)
                        step(w.tensor_reduce(p1_sum[:, :], p1[:, :, :], AX.X, ALU.add))
                        step(w.reciprocal(p1_inv[:, :], p1_sum[:, :]))
                        step(w.tensor_tensor(p1_fac[:, :].rearrange("p (h i) -> p h i", i=2),
                                             p1_inv[:, :].rearrange("p (h i) -> p h i", i=2),
                                             sign[:, :].unsqueeze(1).to_broadcast([P, H // 2, 2]), ALU.mult))
                        step(w.tensor_tensor(p1_n[:, :, :], p1[:, :, :],
                                             p1_fac[:, :].unsqueeze(2).to_broadcast([P, H, S]), ALU.mult))
                        p1_v = p1_n[:, :, :].rearrange("p (h i) k -> p h i k", i=2)
                        step(w.tensor_tensor(att[:, :, :], p1_v[:, :, 0, :], p1_v[:, :, 1, :], ALU.add))
                        for q in range(BT):
                            ins = w.transpose(attT_bd[32 * q:32 * q + 32, :, q, :], att[32 * q:32 * q + 32, :, :])
                        ins.then_inc(attT_ready, 1)

            tile_loop(dve, step, DVE_STEPS, body)

            dve.wait_ge(lg_evac, T)
            for t in range(T):
                ins = w.max(top8[:, t, :], logits[:, t, :])
            step(ins)
            for t in range(T):
                w.max_index(top_i[:, t, :], top8[:, t, :], logits[:, t, :])
            step(w.tensor_tensor(lg_c[:, :, :], logits[:, :, :], top8[:, :, 0:1].to_broadcast([P, T, E]), ALU.subtract
                                 ))
            w.tensor_copy(token[:, 0:1], lg_c[:, 0, 0:1]).then_inc(lg_centred, 1)
            step(w.tensor_copy(top_f[:, :, :], top_i[:, :, 0:2]))
            for r in range(2):
                ins = w.tensor_tensor(hit[:, r, :, :], expert_no[:, :].unsqueeze(1).to_broadcast([P, T, E]),
                                      top_f[:, :, r:r + 1].to_broadcast([P, T, E]), ALU.is_equal)
            step(ins)
            dve.wait_ge(lg_exp, 1)
            step(w.tensor_reduce(lg_sum[:, :], lg_e[:, :, :], AX.X, ALU.add))
            step(w.reciprocal(lg_inv[:, :], lg_sum[:, :]))
            step(w.tensor_tensor(pr[:, :, :], lg_e[:, :, :], lg_inv[:, :].unsqueeze(2).to_broadcast([P, T, E]),
                                 ALU.mult))
            step(w.tensor_tensor(hit[:, 0, :, :], hit[:, 0, :, :], hit[:, 1, :, :], ALU.add))
            step(w.tensor_tensor(pr_m[:, :, :], pr[:, :, :], hit[:, 0, :, :], ALU.mult))
            step(w.tensor_reduce(pr_sum[:, :], pr_m[:, :, :], AX.X, ALU.add))
            step(w.tensor_scalar(pr_sum[:, :], pr_sum[:, :], 1e-9, None, ALU.add))
            step(w.reciprocal(pr_inv[:, :], pr_sum[:, :]))
            w.tensor_tensor(gates[:, :, :], pr_m[:, :, :], pr_inv[:, :].unsqueeze(2).to_broadcast([P, T, E]),
                            ALU.mult).then_inc(gates_ready, 1)
            for t in range(T):
                dve.wait_ge(bd_ps, t + 1)
                w.tensor_tensor(xn_all[:, t, :], bank[2 + t % 2][:, 0:D], xn_all[:, t, :], ALU.add
                                ).then_inc(y_seeded, 1)
            dve.wait_ge(y_seeded, T)
            for k in range(H_FREE):
                w.memset(token[:, k:k + 1], 0.0).then_inc(h_ready, 1)
            for k in range(Y_FREE):
                w.memset(token[:, H_FREE + k:H_FREE + k + 1], 0.0).then_inc(y_added, 1)
            with dve.Fori(0, E // 2) as pair:
                for i in range(2):
                    for n in range(NCH):
                        q0 = (pair * 2 + i) * NCH + n
                        for f in range(FT):
                            dve.wait_ge(silu_done, q0 * FT + f + 1)
                            dve.wait_ge(up_ps, q0 * FT + f + 1)
                            w.scalar_tensor_tensor(hT[n % 2][:, f, :], bank[2 + f % 2][:, :],
                                                   bu_c[:, bass.ds(pair * 2 + i, 1), f:f + 1].squeeze(2),
                                                   silu[f % 2][:, :], ALU.add, ALU.mult).then_inc(h_ready, 1)
                        for k in range(4):
                            dve.wait_ge(down_ps, q0 + 1)
                            dve.wait_ge(y_added, q0 * 4 + k + 1)
                            w.scalar_tensor_tensor(xn_all[:, 4 * n + k, :], bank[4 + k][:, 0:D],
                                                   gates[:, 4 * n + k, bass.ds(pair * 2 + i, 1)],
                                                   xn_all[:, 4 * n + k, :], ALU.mult, ALU.add).then_inc(y_added, 1)


def kernel(**inputs):
    import numpy as _np
    import concourse.bacc as _bacc
    from concourse import mybir as _mybir
    from concourse.bass_utils import run_bass_kernel_spmd as _run

    a = {k: _np.asarray(v) for k, v in inputs.items()}
    ctx = a["ctx_1024"]
    ins = {
        "x": a["x"].reshape(TOK, D),
        "ctxT": ctx.transpose(2, 0, 1),
        "ctx_tailT": ctx[:, KM, :].T,
        "mask": a["mask_1x1xSxS2_ik1"].reshape(S, K),
        "wqT": a["L0_xattn_wq"].T, "wkT": a["L0_xattn_wk"].T, "wvT": a["L0_xattn_wv"].T,
        "columns": _np.stack([a[n].reshape(DC, P).T for n in (
            "L0_xattn_bq", "L0_xattn_bk", "L0_xattn_bv", "L0_attn_norm_w")], axis=1),
        "woT": a["L0_xattn_wo"].T, "bo": a["L0_xattn_bo"],
        "sqT": a["L0_attn_Wq"].T, "skT": a["L0_attn_Wk"].T, "svT": a["L0_attn_Wv"].T,
        "soT": a["L0_attn_Wo"].T, "sbo": a["L0_attn_bo"],
        "diff_weight": a["L0_attn_diff_weight"].reshape(1),
        "routerT": a["L0_ffn_router_w"].T,
        "gate_w": a["L0_ffn_gate_w"], "gate_b": a["L0_ffn_gate_b"].reshape(E, FT, P).transpose(2, 0, 1),
        "up_w": a["L0_ffn_up_w"], "up_b": a["L0_ffn_up_b"].reshape(E, FT, P).transpose(2, 0, 1),
        "down_w": a["L0_ffn_down_w"], "down_b": a["L0_ffn_down_b"],
    }
    nc = _bacc.Bacc("TRN2", target_bir_lowering=False, num_devices=1)
    arrays, args = {}, []
    for name, value in ins.items():
        value = _np.ascontiguousarray(value)
        arrays[f"in_{name}"] = value
        args.append(nc.dram_tensor(f"in_{name}", value.shape, _mybir.dt.from_np(value.dtype),
                                   kind="ExternalInput").ap())
    args.append(nc.dram_tensor("out_0", (TOK, D), F32, kind="ExternalOutput").ap())
    perceiver_program(nc, *args)
    r = _run(nc, [arrays], core_ids=[0])
    return r.results[0]["out_0"].reshape(B, S, D)
```

```python
from contextlib import ExitStack

import concourse.bass as bass
from concourse import mybir

ALU = mybir.AluOpType
ACT = mybir.ActivationFunctionType
AX = mybir.AxisListType
F32 = mybir.dt.float32
I32 = mybir.dt.int32
U32 = mybir.dt.uint32

P = 128
D = 256
DC = D // P
B = 32
S = 32
K = 257
KM = 256
KT = KM // P
H = 16
HD = D // H
GH = P // S
G = H // GH
HH = H // DC
T = B * S // P
BT = P // S
E = 8
F = 512
FT = F // P
TOK = B * S
TOPK = 2
REGION = TOK
NB = (TOK * TOPK + E * (P - 1)) // P
SLOTS = (E - 1) * REGION + max(REGION, NB * P)
EW = (2 * DC * F + FT * D)
LATE = 2
NCH = TOK // 512
MASKED = 10000.0
BIG = 3.0e38
LN_EPS = 1e-5
RMS_EPS = 1.1920928955078125e-07
QSCALE = HD ** -0.5
POOL_STEPS, DVE_STEPS = 4, 33


class Steps:

    def __init__(self, eng, sem):
        self.eng, self.sem, self.n, self.base = eng, sem, 0, 0

    def __call__(self, ins):
        self.n += 1
        ins.then_inc(self.sem, 1)
        self.eng.wait_ge(self.sem, self.base + self.n)


def tile_loop(eng, steps, per_tile, body):
    body(0, True, False, False)
    body(1, True, True, False)
    before = steps.n
    with eng.Fori(2, T) as t:
        steps.base, steps.n = (t - 2) * per_tile + before, 0
        body(t, True, True, True)
        assert steps.n == per_tile, (steps.sem, steps.n)
    steps.base, steps.n = 0, before + (T - 2) * per_tile
    body(T, False, True, True)
    body(T + 1, False, False, True)


def perceiver_program(nc, x, ctxT, ctx_tailT, mask, wqT, wkT, wvT, columns, woT, bo,
                      sqT, skT, svT, soT, sbo, diff_weight,
                      routerT, gate_w, gate_b, up_w, up_b, down_w, down_b, empty_slots,
                      v_tail_d, expert_x, slots, out):
    with ExitStack() as ctx:
        def sb(name, shape, dt=F32):
            return ctx.enter_context(nc.sbuf_tensor(name, shape, dt))

        def sem(name):
            return ctx.enter_context(nc.semaphore(name))

        bank = [ctx.enter_context(nc.psum_tensor(f"bank{i}", [P, 512], F32)) for i in range(8)]

        ident = sb("ident", [P, P])
        ones_col = sb("ones_col", [P, 1])
        ones_rows = sb("ones_rows", [S, P])
        head_mask = sb("head_mask", [P, HH])
        parity = sb("parity", [P, 2])
        expert_from = sb("expert_from", [P, E])
        group_mask = sb("group_mask", [P, D])
        neg_half = sb("neg_half", [P, T])
        wq, wk, wv, wo = (sb(n, [P, DC, D]) for n in ("wq", "wk", "wv", "wo"))
        sq, sk, sv, so = (sb(n, [P, DC, D]) for n in ("sq", "sk", "sv", "so"))
        wr = sb("wr", [P, DC, E])
        cols = sb("cols", [P, 4, DC])
        bo_b = sb("bo_b", [P, D])
        sbo_b = sb("sbo_b", [P, D])
        sbo_s = sb("sbo_s", [P, D])
        dw = sb("dw", [P, 1])
        one_m_dw = sb("one_m_dw", [P, 1])
        sign = sb("sign", [P, 2])
        bg_c = sb("bg_c", [P, E, FT])
        bu_c = sb("bu_c", [P, E, FT])
        bd_r = sb("bd_r", [E, D])
        mask_i = sb("mask_i", [P, K], I32)
        masked = sb("masked", [P, K])
        mask_add = sb("mask_add", [P, K])
        all_masked = sb("all_masked", [P, 1])
        row_valid = sb("row_valid", [P, 1])
        valid_diag = sb("valid_diag", [S, S])
        q_factor = sb("q_factor", [P, S])
        arena = sb("arena", [P, E * EW])
        taken = [0]

        def cut(shape, limit=LATE * EW):
            size = 1
            for n in shape:
                size *= n
            part = arena[:, taken[0]:taken[0] + size]
            taken[0] += size
            assert taken[0] <= limit, (taken[0], limit)
            if len(shape) == 1:
                return part
            names = "abc"[:len(shape)]
            sizes = {n: k for n, k in zip(names, shape)}
            return part.rearrange(f"p ({' '.join(names)}) -> p {' '.join(names)}", **sizes)

        ctx_b = [cut([DC, KM]) for _ in range(BT)]
        kT = [cut([DC, K]) for _ in range(2)]
        v = [cut([KT, D]) for _ in range(2)]
        q_bd = [cut([DC, HH, S]) for _ in range(2)]
        taken[0] = E * EW - 2 * T * D
        xn_all = cut([T, D], E * EW)
        xnT_all = cut([DC, TOK], E * EW)
        work = sb("work", [P, 2 * G * K + G * K + DC * KT * 2 * P])
        at = [0]

        def piece(n):
            at[0] += n
            assert at[0] <= work.shape[1], at[0]
            return work[:, at[0] - n:at[0]]

        s_m = [piece(K) for g in range(G)]
        p_exp = [piece(K) for g in range(G)]
        p_n1 = piece(G * K).rearrange("p (g k) -> p g k", g=G)
        pT = [piece(KT * 2 * P).rearrange("p (k n) -> p k n", k=KT) for c in range(DC)]
        p_n = [sb("p_n0", [P, G, K]), p_n1]
        at[0] = 0
        xg = piece(D)
        xgT = piece(D).rearrange("p (c k) -> p c k", c=DC)
        g_rows = piece(F)
        u_rows = piece(F)
        silu = piece(F).rearrange("p (f k) -> p f k", f=FT)
        hT = piece(F).rearrange("p (f k) -> p f k", f=FT)
        y_rows = piece(D)
        x_all = sb("x_all", [P, T, D])
        qT = sb("qT", [P, DC, TOK])
        stats0 = sb("stats0", [P, T, 6])
        mv0 = sb("mv0", [P, T, 2])
        rstd0 = sb("rstd0", [P, T])
        ctx_tail = sb("ctx_tail", [P, DC, G, B])
        k_tail = sb("k_tail", [P, DC, B])
        v_tail_m = sb("v_tail_m", [P, D])
        v_end = [sb(f"v_end{j}", [G, D]) for j in range(BT)]
        s_min = sb("s_min", [P, G])
        p_sum = sb("p_sum", [P, G])
        p_inv = sb("p_inv", [P, G])
        p_end = sb("p_end", [G, P])
        o_even = sb("o_even", [P, DC, S])
        oT = sb("oT", [P, DC, P])
        x1 = sb("x1", [P, D])
        x1b = sb("x1b", [P, D])
        stats = sb("stats", [P, 6])
        mv = sb("mv", [P, 2])
        rstd = sb("rstd", [P, 1])
        xn1 = sb("xn1", [P, D])
        xn1T = sb("xn1T", [P, DC, P])
        qk1 = sb("qk1", [P, 2, DC, P])
        q1_bd = sb("q1_bd", [P, DC, BT, HH, S])
        v1 = sb("v1", [P, D])
        s1 = sb("s1", [P, H, S])
        s1_max = sb("s1_max", [P, H])
        p1_sum = sb("p1_sum", [P, H])
        p1_inv = sb("p1_inv", [P, H])
        p1_fac = sb("p1_fac", [P, H])
        att = sb("att", [P, H // 2, S])
        attT_bd = sb("attT_bd", [P, H // 2, BT, S])
        o1T = sb("o1T", [P, DC, P])
        o1_sq = sb("o1_sq", [P, DC, P])
        ms = sb("ms", [P, 1])
        rms = sb("rms", [P, 1])
        x2 = sb("x2", [P, D])
        stats2 = sb("stats2", [P, 6])
        mv2 = sb("mv2", [P, 2])
        rstd2 = sb("rstd2", [P, 1])
        xn2 = sb("xn2", [P, D])
        xn2T = sb("xn2T", [P, DC, P])
        lg = sb("lg", [P, E])
        top8 = sb("top8", [P, 8])
        lg_rest = sb("lg_rest", [P, E])
        lead = sb("lead", [P, E])
        lead_max = sb("lead_max", [P, 1])
        hit = sb("hit", [P, TOPK, E])
        chosen = sb("chosen", [P, E])
        chosen_sum = sb("chosen_sum", [P, E])
        lg_c = sb("lg_c", [P, E])
        lg_e = sb("lg_e", [P, E])
        lg_sum = sb("lg_sum", [P, 1])
        lg_m = sb("lg_m", [P, E])
        chosen_e = sb("chosen_e", [P, 1])
        gate_den = sb("gate_den", [P, 1])
        gate_inv = sb("gate_inv", [P, 1])
        gates = sb("gates", [P, E])
        gate_hit = sb("gate_hit", [P, TOPK, E])
        gatesT = sb("gatesT", [E, P])
        before = sb("before", [P, P])
        ones_sq = sb("ones_sq", [P, P])
        region = sb("region", [P, E])
        token_no = sb("token_no", [P, T], I32)
        pos = sb("pos", [P, E])
        pos_hit = sb("pos_hit", [P, TOPK, E])
        slot_f = sb("slot_f", [P, TOPK])
        slot_u = sb("slot_u", [P, TOPK], U32)
        entry = sb("entry", [P, TOPK, 2])
        entry_i = entry[:, :, :].bitcast(I32)
        zeros = sb("zeros", [P, D])
        y0 = sb("y0", [P, D])
        up_to = sb("up_to", [P, E, E])
        block_i = sb("block_i", [P, NB], I32)
        block_no = sb("block_no", [P, NB])
        count_i = sb("count_i", [P, E], I32)
        nblocks_i = sb("nblocks_i", [P, E], I32)
        nblocks = sb("nblocks", [P, E])
        nblocks_t = sb("nblocks_t", [P, E, E])
        ends = sb("ends", [P, E])
        past = sb("past", [P, NB, E - 1])
        b_expert = sb("b_expert", [P, NB])
        b_start = sb("b_start", [P, NB])
        b_within = sb("b_within", [P, NB])
        b_region = sb("b_region", [P, NB])
        b_late = sb("b_late", [P, NB])
        table = sb("table", [P, 4, NB], I32)
        ids_i = sb("ids", [P, NB, 2], I32)
        ids = ids_i[:, :, :].bitcast(F32)
        get_i = sb("get_i", [P, 1], I32)
        add_i = sb("add_i", [P, 1], I32)

        x_in, small_in, wq_in, wkv_in, wo_in, self_in, tail_in, vtail_in = (
            sem(n) for n in ("x_in", "small_in", "wq_in", "wkv_in", "wo_in", "self_in", "tail_in", "vtail_in"))
        mask_in = sem("mask_in")
        ctx_in = [sem(f"ctx_in{j}") for j in range(BT)]
        vend_in = [sem(f"vend_in{j}") for j in range(BT)]
        experts_in, late_in, pads_in, xn2_stored, y0_stored, slots_stored, ids_in, rows_in, rows_added = (
            sem(n) for n in ("experts_in", "late_in", "pads_in", "xn2_stored", "y0_stored",
                             "slots_stored", "ids_in", "rows_in", "rows_added"))
        out_done = sem("out_done")
        pool_steps, dve_steps, act_steps = sem("pool_steps"), sem("dve_steps"), sem("act_steps")
        consts_ready, var0_ready, rstd0_ready, xn0_ready = (
            sem(n) for n in ("consts_ready", "var0_ready", "rstd0_ready", "xn0_ready"))
        xT0_ps, xT0_evac, q0_ps, q0_evac, valid_diag_ready, valid_ps, q_factor_ready = (
            sem(n) for n in ("xT0_ps", "xT0_evac", "q0_ps", "q0_evac", "valid_diag_ready", "valid_ps", "q_factor_ready"))
        ktail_ps, tails_evac, vtail_ps, xb_ready = (
            sem(n) for n in ("ktail_ps", "tails_evac", "vtail_ps", "xb_ready"))
        k_ps, k_evac, v_ps, v_evac, batch_ready = (
            sem(n) for n in ("k_ps", "k_evac", "v_ps", "v_evac", "batch_ready"))
        s_ps, s_masked, exp_done, p_normed = (sem(n) for n in ("s_ps", "s_masked", "exp_done", "p_normed"))
        pT_ps, pT0_evac, pT1_evac, end_ps, end_evac, o_ps, o_evac = (
            sem(n) for n in ("pT_ps", "pT0_evac", "pT1_evac", "end_ps", "end_evac", "o_ps", "o_evac"))
        y_ps, var1_ready, x1_ready, rstd1_ready, xn1_ready, x1T_ps, x1T_evac = (
            sem(n) for n in ("y_ps", "var1_ready", "x1_ready", "rstd1_ready", "xn1_ready", "x1T_ps", "x1T_evac"))
        qk1_ps, qk1_evac, q1_bd_ready, v1_ps, v1_evac, s1_ps, s1_evac = (
            sem(n) for n in ("qk1_ps", "qk1_evac", "q1_bd_ready", "v1_ps", "v1_evac", "s1_ps", "s1_evac"))
        s1_ready, exp1_done, attT_ready, o1_ps, o1_evac, y1_ps, ms_ready, rms_ready = (
            sem(n) for n in ("s1_ready", "exp1_done", "attT_ready", "o1_ps", "o1_evac", "y1_ps", "ms_ready", "rms_ready"))
        var2_ready, rstd2_ready, xn2_ready, x2T_ps, x2T_evac, lg_ps, lg_evac = (
            sem(n) for n in ("var2_ready", "rstd2_ready", "xn2_ready", "x2T_ps", "x2T_evac", "lg_ps", "lg_evac"))
        lg_centred, lg_exp, chosen_ready, gates_ready, rank_ps, gT_ready, slots_ready, seed_ps, y0_ready = (
            sem(n) for n in ("lg_centred", "lg_exp", "chosen_ready", "gates_ready", "rank_ps", "gT_ready",
                             "slots_ready", "seed_ps", "y0_ready"))
        p1_fac_ready, att_ready = sem("p1_fac_ready"), sem("att_ready")
        zeros_ready, count_ps, table_ready = (sem(n) for n in ("zeros_ready", "count_ps", "table_ready"))
        get_ready, add_ready = sem("get_ready"), sem("add_ready")
        xgT_ps, xgT_evac, gate_ps, gate_evac, up_ps, up_evac = (
            sem(n) for n in ("xgT_ps", "xgT_evac", "gate_ps", "gate_evac", "up_ps", "up_evac"))
        gT_ps, uT_ps, silu_done, h_ready, down_ps = (
            sem(n) for n in ("gT_ps", "uT_ps", "silu_done", "h_ready", "down_ps"))

        def settle(eng):
            eng.nop(nofuse=True)

        block = ctx.enter_context(nc.Block())

        def halves(w):
            return w.rearrange("(c p) n -> p c n", p=P)

        @block.sync
        def _(sp):
            sp.dma_start(x_all[:, :, :], x.rearrange("(t p) d -> p t d", p=P)).then_inc(x_in, 16)
            sp.dma_start(cols[:, :, :], columns).then_inc(small_in, 16)
            sp.dma_start(bo_b[:, :], bo.partition_broadcast(P)).then_inc(small_in, 16)
            sp.dma_start(sbo_b[:, :], sbo.partition_broadcast(P)).then_inc(small_in, 16)
            sp.dma_start(dw[:, :], diff_weight.partition_broadcast(P)).then_inc(small_in, 16)
            for h in range(GH):
                sp.dma_start(mask_i[h * S:(h + 1) * S, :], mask).then_inc(mask_in, 16)
            sp.dma_start(wq[:, :, :], halves(wqT)).then_inc(wq_in, 16)
            for g in range(G):
                sp.dma_start(ctx_tail[:, :, g, :], halves(ctx_tailT)).then_inc(tail_in, 16)
            sp.dma_start(wk[:, :, :], halves(wkT)).then_inc(wkv_in, 16)
            sp.dma_start(wv[:, :, :], halves(wvT)).then_inc(wkv_in, 16)

            def load_context(t, j):
                sp.dma_start(ctx_b[j][:, :, :],
                             ctxT.rearrange("(c p) (t j) k -> p c t j k", p=P, j=BT)[:, :, t, j, 0:KM]
                             ).then_inc(ctx_in[j], 16)

            for j in range(BT):
                load_context(0, j)
            sp.dma_start(wo[:, :, :], halves(woT)).then_inc(wo_in, 16)
            for dst, src in ((sq, sqT), (sk, skT), (sv, svT), (so, soT), (wr, routerT)):
                sp.dma_start(dst[:, :, :], halves(src)).then_inc(self_in, 16)
            sp.dma_start(bg_c[:, :, :], gate_b).then_inc(self_in, 16)
            sp.dma_start(bu_c[:, :, :], up_b).then_inc(self_in, 16)
            sp.dma_start(bd_r[:, :], down_b).then_inc(self_in, 16)
            sp.dma_start(slots, empty_slots).then_inc(late_in, 16)
            sp.wait_ge(zeros_ready, 1)
            sp.dma_start(expert_x[TOK:TOK + P, :], zeros[:, :]).then_inc(pads_in, 16)
            sp.dma_start(out[TOK:TOK + P, :], zeros[:, :]).then_inc(pads_in, 16)
            sp.wait_ge(tails_evac, 2)
            sp.dma_start(v_tail_d, v_tail_m[:, :]).then_inc(vtail_in, 16)
            sp.wait_ge(vtail_in, 16)

            def load_tail(b, j):
                sp.dma_start(v_end[j][:, :], v_tail_d.rearrange("(g b) d -> g b d", b=B)[:, bass.ds(b, 1), :]
                             .squeeze(1)).then_inc(vend_in[j], 16)

            for j in range(BT - 1):
                load_tail(j, j)

            def load_expert(e, signal):
                at_e = (E - 1 - e) * EW
                for k, (src, n) in enumerate(((gate_w, DC), (up_w, DC), (down_w, FT))):
                    sp.dma_start(arena[:, bass.ds(at_e + k * DC * F, DC * F)].rearrange("p (c f) -> p c f", c=n),
                                 src.rearrange("e (c p) f -> p e c f", p=P)[:, bass.ds(e, 1), :, :].squeeze(1)
                                 ).then_inc(signal, 16)

            def body(s):
                fixed = isinstance(s, int)
                for j in range(BT):
                    if not fixed or s < T:
                        sp.wait_ge(v_ps, (s - 1) * BT + j + 1)
                        load_context(s, j)
                    if not fixed or s < T or (s == T and j == 0):
                        if not (fixed and s == 1 and j == 0):
                            sp.wait_ge(o_ps, (s - 1) * BT + j)
                        load_tail(s * BT + j - 1, (j - 1) % BT)
                    if j == 1 and (not fixed or s >= 3):
                        sp.wait_ge(xn2_ready, s - 2)
                        sp.dma_start(expert_x[bass.ds((s - 3) * P, P), :], xn2[:, :]).then_inc(xn2_stored, 16)
                if not fixed or s >= 3:
                    sp.wait_ge(y0_ready, s - 2)
                    sp.dma_start(out[bass.ds((s - 3) * P, P), :], y0[:, :]).then_inc(y0_stored, 16)

            body(1)
            load_expert(0, experts_in)
            load_expert(1, experts_in)
            body(2)
            load_expert(2, experts_in)
            with sp.Fori(3, 6) as s:
                body(s)
                load_expert(s, experts_in)
            for s in range(6, T + 1):
                body(s)
            sp.wait_ge(o_ps, B)
            for e in range(E - LATE, E):
                load_expert(e, late_in)
            for s in range(T + 1, T + 3):
                body(s)
            sp.wait_ge(slots_stored, 16 * TOPK * T)
            sp.wait_ge(table_ready, 1)
            with sp.Fori(0, NB) as n:
                row = sp.value_load(table[0:1, 2, bass.ds(n, 1)], min_val=0, max_val=SLOTS - P)
                sp.dma_start(ids_i[:, bass.ds(n, 1), :].squeeze(1), slots[bass.ds(row, P), :]).then_inc(ids_in, 16)
                sp.wait_ge(ids_in, 16 * (n + 1))
                settle(sp)
            sp.wait_ge(rows_added, 16 * NB)

        @block.gpsimd
        def _(pool):
            step = Steps(pool, pool_steps)
            g = nc.gpsimd
            g.memset(ident[:, :], 0.0)
            g.memset(ones_col[:, :], 1.0)
            g.memset(ones_rows[:, :], 1.0)
            g.memset(neg_half[:, :], -0.5)
            g.memset(attT_bd[:, :, :, :], 0.0)
            g.memset(zeros[:, :], 0.0).then_inc(zeros_ready, 1)
            for e in range(E):
                g.memset(expert_from[:, e:e + 1], float(E - e))
                g.memset(region[:, e:e + 1], float(e * REGION))
            g.memset(before[:, :], 1.0)
            g.memset(ones_sq[:, :], 1.0)
            g.memset(up_to[:, :, :], 1.0)
            g.iota(token_no[:, :], pattern=[[P, T]], base=0, channel_multiplier=1)
            g.iota(block_i[:, :], pattern=[[1, NB]], base=0, channel_multiplier=0)
            step(g.memset(head_mask[:, :], 1.0))
            step(g.affine_select(out=head_mask[:, :], in_=head_mask[:, :], compare_op=ALU.is_ge, fill=0.0,
                                 base=0, pattern=[[-HD, HH]], channel_multiplier=1))
            g.affine_select(out=ident[:, :], in_=ident[:, :], compare_op=ALU.not_equal, fill=1.0,
                            base=0, pattern=[[-1, P]], channel_multiplier=1)
            g.affine_select(out=before[:, :], in_=before[:, :], compare_op=ALU.is_gt, fill=0.0,
                            base=0, pattern=[[1, P]], channel_multiplier=-1)
            g.affine_select(out=up_to[:, :, :], in_=up_to[:, :, :], compare_op=ALU.is_ge, fill=0.0,
                            base=0, pattern=[[1, E], [-1, E]], channel_multiplier=0)
            g.affine_select(out=head_mask[:, :], in_=head_mask[:, :], compare_op=ALU.is_ge, fill=0.0,
                            base=HD - 1, pattern=[[HD, HH]], channel_multiplier=-1).then_inc(consts_ready, 1)
            pool.wait_ge(var0_ready, 1)
            step(g.tensor_scalar(rstd0[:, :], mv0[:, :, 1], LN_EPS, None, ALU.add))
            g.tensor_tensor(rstd0[:, :], rstd0[:, :], neg_half[:, :], ALU.pow).then_inc(rstd0_ready, 1)
            pool.wait_ge(xn0_ready, T)
            pool.wait_ge(small_in, 16 * 4)
            g.tensor_tensor(x_all[:, :, :], x_all[:, :, :],
                            bo_b[:, :].unsqueeze(1).to_broadcast([P, T, D]), ALU.add).then_inc(xb_ready, 1)

            def prepare_batch(t, j):
                i = j % 2
                b = t * BT + j
                if not isinstance(t, int) or b >= 2:
                    pool.wait_ge(o_ps, b - 1)
                g.tensor_tensor(
                    q_bd[i][:, :, :, :],
                    qT[:, :, bass.ds(b * S, S)].unsqueeze(2).to_broadcast([P, DC, HH, S]),
                    head_mask[:, :].unsqueeze(1).unsqueeze(3).to_broadcast([P, DC, HH, S]), ALU.mult)
                g.tensor_copy(kT[i][:, :, KM:K], k_tail[:, :, bass.ds(b, 1)]).then_inc(batch_ready, 1)

            pool.wait_ge(q0_evac, 2 * NCH)
            pool.wait_ge(tails_evac, 2)

            def body(t, cross, attend, close):
                if cross:
                    prepare_batch(t, 0)
                if close:
                    pool.wait_ge(p1_fac_ready, t - 1)
                    step(g.tensor_tensor(s1[:, :, :], s1[:, :, :],
                                         p1_fac[:, :].unsqueeze(2).to_broadcast([P, H, S]), ALU.mult))
                    p1_v = s1[:, :, :].rearrange("p (h i) k -> p h i k", i=2)
                    g.tensor_tensor(att[:, :, :], p1_v[:, :, 0, :], p1_v[:, :, 1, :], ALU.add).then_inc(att_ready, 1)
                if cross:
                    prepare_batch(t, 1)
                if close:
                    pool.wait_ge(ms_ready, t - 1)
                    step(g.tensor_tensor(rms[:, :], ms[:, :], neg_half[:, 0:1], ALU.pow))
                    settle(pool)
                    g.tensor_scalar(rms[:, :], rms[:, :], one_m_dw[:, 0:1], None, ALU.mult).then_inc(rms_ready, 1)
                    pool.wait_ge(var2_ready, t - 1)
                    settle(pool)
                    step(g.tensor_scalar(rstd2[:, :], mv2[:, 1:2], LN_EPS, None, ALU.add))
                    g.tensor_tensor(rstd2[:, :], rstd2[:, :], neg_half[:, 0:1], ALU.pow).then_inc(rstd2_ready, 1)
                if cross:
                    prepare_batch(t, 2)
                if attend:
                    pool.wait_ge(var1_ready, t)
                    settle(pool)
                    step(g.tensor_scalar(rstd[:, :], mv[:, 1:2], LN_EPS, None, ALU.add))
                    g.tensor_tensor(rstd[:, :], rstd[:, :], neg_half[:, 0:1], ALU.pow).then_inc(rstd1_ready, 1)
                if attend:
                    pool.wait_ge(qk1_evac, t)
                    q4 = qk1[:, 0, :, :].rearrange("p c (b q) -> p c b q", b=BT)
                    for c in range(DC):
                        ins = g.tensor_tensor(
                            q1_bd[:, c, :, :, :],
                            q4[:, c, :, :].unsqueeze(2).to_broadcast([P, BT, HH, S]),
                            head_mask[:, :].unsqueeze(1).unsqueeze(3).to_broadcast([P, BT, HH, S]), ALU.mult)
                    ins.then_inc(q1_bd_ready, 1)
                if cross:
                    prepare_batch(t, 3)
                if close:
                    pool.wait_ge(slots_ready, t - 1)
                    settle(pool)
                    for r in range(TOPK):
                        g.indirect_dma_start(
                            out=slots, out_offset=bass.IndirectOffsetOnAxis(ap=slot_u[:, r:r + 1], axis=0),
                            in_=entry_i[:, r, :], in_offset=None).then_inc(slots_stored, 16)

            pool.wait_ge(late_in, 16)
            tile_loop(pool, step, POOL_STEPS, body)

            def gather(n):
                pool.wait_ge(get_ready, n + 1)
                settle(pool)
                g.indirect_dma_start(
                    out=xg, out_offset=None, in_=expert_x,
                    in_offset=bass.IndirectOffsetOnAxis(ap=get_i[:, 0:1], axis=0)).then_inc(rows_in, 16)

            def add(n):
                pool.wait_ge(add_ready, n + 1)
                settle(pool)
                g.indirect_dma_start(
                    out=out, out_offset=bass.IndirectOffsetOnAxis(ap=add_i[:, 0:1], axis=0),
                    in_=y_rows, in_offset=None, compute_op=ALU.add).then_inc(rows_added, 16)

            pool.wait_ge(pads_in, 32)
            pool.wait_ge(xn2_stored, 16 * T)
            gather(0)
            gather(1)
            pool.wait_ge(y0_stored, 16 * T)
            with pool.Fori(2, NB) as n:
                gather(n)
                add(n - 2)
            add(NB - 2)
            add(NB - 1)

        @block.tensor
        def _(pe):
            step = Steps(pe, None)
            mm = nc.tensor.matmul
            pe.wait_ge(consts_ready, 1)
            for t in range(T):
                pe.wait_ge(xn0_ready, t + 1)
                for c in range(DC):
                    ins = nc.tensor.transpose(bank[t // 2][:, ((t % 2) * DC + c) * P:((t % 2) * DC + c + 1) * P],
                                              xn_all[:, t, c * P:(c + 1) * P], ident[:, :])
                ins.then_inc(xT0_ps, 1)
            pe.wait_ge(wq_in, 16)
            for n in range(NCH):
                pe.wait_ge(xT0_evac, 2 * (n + 1))
                for oc in range(DC):
                    for c in range(DC):
                        ins = mm(bank[4 + 2 * n + oc][:, :], wq[:, c, oc * P:(oc + 1) * P],
                                 xnT_all[:, c, n * 512:(n + 1) * 512], start=(c == 0), stop=(c == DC - 1))
                    ins.then_inc(q0_ps, 1)
            pe.wait_ge(valid_diag_ready, 1)
            mm(bank[0][:, 0:S], ones_rows[:, :], valid_diag[:, :], start=True, stop=True).then_inc(valid_ps, 1)
            pe.wait_ge(tail_in, 16 * G)
            pe.wait_ge(wkv_in, 32)
            for oc in range(DC):
                for c in range(DC):
                    ins = mm(bank[1][:, oc * B:(oc + 1) * B], wk[:, c, oc * P:(oc + 1) * P], ctx_tail[:, c, 0, :],
                             start=(c == 0), stop=(c == DC - 1))
            ins.then_inc(ktail_ps, 1)
            for c in range(DC):
                ins = mm(bank[2][:, 0:D], ctx_tail[:, c, :, :].rearrange("p g b -> p (g b)"), wv[:, c, :],
                         start=(c == 0), stop=(c == DC - 1))
            ins.then_inc(vtail_ps, 1)
            pe.wait_ge(q_factor_ready, 1)
            pe.wait_ge(tails_evac, 2)
            pe.wait_ge(q0_evac, 2 * NCH)

            def first(t, n=0):
                return isinstance(t, int) and t <= n

            def project(t, j):
                b = t * BT + j
                pe.wait_ge(ctx_in[j], 16 * (t + 1))
                if not first(b):
                    pe.wait_ge(k_evac, b)
                for oc in range(DC):
                    for c in range(DC):
                        ins = mm(bank[0][:, oc * KM:(oc + 1) * KM], wk[:, c, oc * P:(oc + 1) * P], ctx_b[j][:, c, :],
                                 start=(c == 0), stop=(c == DC - 1))
                ins.then_inc(k_ps, 1)
                if not first(b):
                    pe.wait_ge(v_evac, b)
                if not first(t, 2) or (t == 2 and j > 0):
                    free, count = ((y0_ready, t - 2), (o1_evac, 2 * (t - 1)), (var2_ready, t - 1),
                                   (lg_evac, t - 1))[j]
                    pe.wait_ge(free, count)
                for kt in range(KT):
                    for c in range(DC):
                        ins = mm(bank[1][:, kt * D:(kt + 1) * D], ctx_b[j][:, c, kt * P:(kt + 1) * P], wv[:, c, :],
                                 start=(c == 0), stop=(c == DC - 1))
                ins.then_inc(v_ps, 1)

            def scores(t, j, c):
                b = t * BT + j
                i = j % 2
                if c == 0:
                    pe.wait_ge(k_evac, b + 1)
                    pe.wait_ge(batch_ready, b + 1)
                for g in (2 * c, 2 * c + 1):
                    if not (isinstance(b, int) and b == 0 and g < 2):
                        pe.wait_ge(s_masked, 4 * b + g - 1)
                    mm(bank[2 + g % 2][:, 0:K],
                       q_bd[i][:, c, (g % 2) * GH:(g % 2 + 1) * GH, :].rearrange("p h q -> p (h q)"),
                       kT[i][:, c, :], start=True, stop=True).then_inc(s_ps, 1)

            def turn(t, j, c):
                b = t * BT + j
                pe.wait_ge(p_normed, 4 * b + 2 * c + 2)
                if not first(b):
                    pe.wait_ge(pT0_evac if c == 0 else pT1_evac, b)
                for kt in range(KT):
                    for g in range(2):
                        ins = nc.tensor.transpose(bank[4 + c][:, kt * 2 * P + g * P:kt * 2 * P + (g + 1) * P],
                                                  p_n[j % 2][:, 2 * c + g, kt * P:(kt + 1) * P], ident[:, :])
                ins.then_inc(pT_ps, 1)
                if c == 1:
                    if not first(b):
                        pe.wait_ge(o_evac, b)
                    nc.tensor.transpose(bank[6][0:G, P:2 * P], p_n[j % 2][:, :, KM:K].squeeze(2),
                                        ident[:, :]).then_inc(end_ps, 1)

            def weigh(t, j):
                b = t * BT + j
                pe.wait_ge(v_evac, b + 1)
                pe.wait_ge(pT0_evac, b + 1)
                pe.wait_ge(pT1_evac, b + 1)
                pe.wait_ge(end_evac, b + 1)
                pe.wait_ge(vend_in[j], 16 * (t + 1))
                for c in range(DC):
                    for kt in range(KT + 1):
                        for r in range(4):
                            o = bank[6][32 * r:32 * r + 32, c * 64:(c + 1) * 64]
                            d0 = c * P + 32 * r
                            if kt < KT:
                                ins = mm(o, v[j % 2][:, kt, d0:d0 + 32], pT[c][:, kt, 64 * r:64 * r + 64],
                                         start=(kt == 0), stop=False)
                            else:
                                ins = mm(o, v_end[j][:, d0:d0 + 32], p_end[:, (64 * r) % P:(64 * r) % P + 64],
                                         start=False, stop=True)
                ins.then_inc(o_ps, 1)

            misc = bank[7]
            aside = bank[1]

            def close_weigh(t):
                if not first(t, 2):
                    pe.wait_ge(y0_ready, t - 2)
                pe.wait_ge(attT_ready, t - 1)
                for h in range(H // 2):
                    r, c = h % 4, h // 4
                    ins = mm(aside[32 * r:32 * r + 32, c * P:(c + 1) * P], v1[:, 32 * h:32 * h + 32],
                             attT_bd[:, h, :, :].rearrange("p b q -> p (b q)"), start=True, stop=True)
                ins.then_inc(o1_ps, 1)

            def close_project(t):
                pe.wait_ge(o1_evac, 2 * (t - 1))
                for c in range(DC):
                    mm(aside[:, 0:D], o1T[:, c, :], so[:, c, :], start=(c == 0), stop=(c == DC - 1))
                for c in range(DC):
                    ins = mm(aside[:, D:D + 1], o1_sq[:, c, :], ones_col[:, :], start=(c == 0), stop=(c == DC - 1))
                ins.then_inc(y1_ps, 1)

            def turn_rows(to, rows, ready, count, done):
                pe.wait_ge(ready, count)
                for c in range(DC):
                    ins = nc.tensor.transpose(to[:, c * P:(c + 1) * P], rows[:, c * P:(c + 1) * P], ident[:, :])
                ins.then_inc(done, 1)

            def close_route(t):
                pe.wait_ge(x2T_evac, t - 1)
                for c in range(DC):
                    ins = mm(aside[:, 0:E], xn2T[:, c, :], wr[:, c, :], start=(c == 0), stop=(c == DC - 1))
                ins.then_inc(lg_ps, 1)

            def close_rank(t):
                pe.wait_ge(chosen_ready, t - 1)
                pe.wait_ge(gates_ready, t - 1)
                if not first(t, 2):
                    pe.wait_ge(slots_ready, t - 2)
                mm(aside[:, 0:E], before[:, :], chosen[:, :], start=True, stop=False)
                mm(aside[:, 0:E], ones_sq[:, :], chosen_sum[:, :], start=False, stop=True)
                nc.tensor.transpose(aside[0:E, P:2 * P], gates[:, :], ident[:, :]).then_inc(rank_ps, 1)

            def close_seed(t):
                pe.wait_ge(gT_ready, t - 1)
                mm(aside[:, 0:D], gatesT[:, :], bd_r[:, :], start=True, stop=True).then_inc(seed_ps, 1)

            def attend_project(t):
                if first(t, 1):
                    pe.wait_ge(wo_in, 16)
                pe.wait_ge(o_evac, BT * t)
                if not first(t, 1):
                    pe.wait_ge(s1_ready, t - 1)
                for c in range(DC):
                    ins = mm(misc[:, 0:D], oT[:, c, :], wo[:, c, :], start=(c == 0), stop=(c == DC - 1))
                ins.then_inc(y_ps, 1)

            def attend_qk(t):
                if first(t, 1):
                    pe.wait_ge(self_in, 16 * 8)
                pe.wait_ge(x1T_evac, t)
                for n, w in enumerate((sq, sk)):
                    for oc in range(DC):
                        for c in range(DC):
                            ins = mm(misc[:, (n * DC + oc) * P:(n * DC + oc + 1) * P],
                                     w[:, c, oc * P:(oc + 1) * P], xn1T[:, c, :], start=(c == 0), stop=(c == DC - 1))
                ins.then_inc(qk1_ps, 1)

            def attend_v(t):
                pe.wait_ge(qk1_evac, t)
                for c in range(DC):
                    ins = mm(misc[:, 0:D], xn1T[:, c, :], sv[:, c, :], start=(c == 0), stop=(c == DC - 1))
                ins.then_inc(v1_ps, 1)

            def attend_scores(t):
                pe.wait_ge(v1_evac, t)
                pe.wait_ge(q1_bd_ready, t)
                for c in range(DC):
                    for b in range(BT):
                        ins = mm(misc[32 * b:32 * b + 32, c * 256:(c + 1) * 256], qk1[:, 1, c, b * S:(b + 1) * S],
                                 q1_bd[:, c, b, :, :].rearrange("p h q -> p (h q)"), start=True, stop=True)
                ins.then_inc(s1_ps, 1)

            def body(t, cross, attend, close):
                for j in range(BT):
                    pt, pj = (t, j - 1) if j else (t - 1, BT - 1)
                    has_prev = cross if j else (not first(t) and (cross or attend))
                    if cross:
                        project(t, j)
                    if j == 3 and attend:
                        attend_scores(t)
                    if has_prev:
                        turn(pt, pj, 0)
                    if cross:
                        scores(t, j, 0)
                    if cross and close:
                        pe.wait_ge(v_evac, t * BT + j + 1)
                    if j == 1 and close:
                        close_project(t)
                    if j == 3 and close:
                        close_rank(t)
                    if j == 2 and attend:
                        turn_rows(misc, xn1, xn1_ready, t, x1T_ps)
                    if j == 2 and close:
                        turn_rows(aside, xn2, xn2_ready, t - 1, x2T_ps)
                    if has_prev:
                        turn(pt, pj, 1)
                    if j == 2 and attend:
                        attend_qk(t)
                    if cross:
                        scores(t, j, 1)
                    if j == 1 and attend:
                        attend_project(t)
                    if j == 2 and close:
                        close_route(t)
                    if j == 2 and attend:
                        attend_v(t)
                    if has_prev:
                        weigh(pt, pj)
                    if j == 0 and close:
                        close_weigh(t)
                    if j == 3 and close:
                        close_seed(t)

            tile_loop(pe, step, 0, body)

            pe.wait_ge(slots_ready, T)
            pe.wait_ge(s1_ready, T)
            mm(misc[:, 0:E], ones_sq[:, :], chosen_sum[:, :], start=True, stop=True).then_inc(count_ps, 1)

            def block_rows(n):
                pe.wait_ge(rows_in, 16 * (n + 1))
                if not first(n):
                    pe.wait_ge(xgT_evac, n)
                for c in range(DC):
                    ins = nc.tensor.transpose(bank[5][:, c * P:(c + 1) * P], xg[:, c * P:(c + 1) * P], ident[:, :])
                ins.then_inc(xgT_ps, 1)

            def block_down(n):
                w = pe.value_load(table[0:1, 1, bass.ds(n, 1)], min_val=0, max_val=(E - 1) * EW)
                pe.wait_ge(h_ready, n + 1)
                if not first(n):
                    pe.wait_ge(add_ready, n)
                for f in range(FT):
                    ins = mm(bank[4][:, 0:D], hT[:, f, :], arena[:, bass.ds(w + 2 * DC * F + f * D, D)],
                             start=(f == 0), stop=(f == FT - 1))
                ins.then_inc(down_ps, 1)

            def block(n, follow=True):
                w = pe.value_load(table[0:1, 1, bass.ds(n, 1)], min_val=0, max_val=(E - 1) * EW)
                late = pe.value_load(table[0:1, 3, bass.ds(n, 1)], min_val=16, max_val=16 + 48 * LATE)
                pe.wait_ge(late_in, late)
                pe.wait_ge(xgT_evac, n + 1)
                for k, (bk, ready, free) in enumerate(((bank[0], gate_ps, gate_evac), (bank[1], up_ps, up_evac))):
                    if not first(n):
                        pe.wait_ge(free, n)
                    for c in range(DC):
                        ins = mm(bk[:, :], xgT[:, c, :], arena[:, bass.ds(w + (k * DC + c) * F, F)],
                                 start=(c == 0), stop=(c == DC - 1))
                    ins.then_inc(ready, 1)
                if not first(n):
                    block_down(n - 1)
                if follow:
                    block_rows(n + 1)
                for bk, rows, ready, free, done in ((bank[2], g_rows, gate_evac, silu_done, gT_ps),
                                                    (bank[3], u_rows, up_evac, h_ready, uT_ps)):
                    pe.wait_ge(ready, n + 1)
                    if not first(n):
                        pe.wait_ge(free, n)
                    for f in range(FT):
                        ins = nc.tensor.transpose(bk[:, f * P:(f + 1) * P], rows[:, f * P:(f + 1) * P], ident[:, :])
                    ins.then_inc(done, 1)

            pe.wait_ge(table_ready, 1)
            pe.wait_ge(experts_in, 48 * (E - LATE))
            block_rows(0)
            block(0)
            block(1)
            with pe.Fori(2, NB - 1) as n:
                block(n)
            block(NB - 1, follow=False)
            block_down(NB - 1)

        @block.scalar
        def _(act):
            a = nc.scalar
            for i in range(T // 2):
                act.wait_ge(xT0_ps, 2 * i + 2)
                a.copy(xnT_all[:, :, 2 * i * P:(2 * i + 2) * P].rearrange("p c (t k) -> p t c k", t=2),
                       bank[i][:, :].rearrange("p (t c k) -> p t c k", t=2, c=DC)).then_inc(xT0_evac, 1)
            act.wait_ge(small_in, 16 * 4)

            def body(t, cross, attend, close):
                misc = bank[7]
                turned, aside = (bk[:, 0:D].rearrange("p (c k) -> p c k", c=DC) for bk in (misc, bank[1]))
                for j in range(BT):
                    b = t * BT + j
                    i = j % 2
                    has_prev = cross if j else (not (isinstance(t, int) and t <= 0) and (cross or attend))
                    if cross:
                        act.wait_ge(k_ps, b + 1)
                        for oc in range(DC):
                            ins = a.activation(kT[i][:, oc, 0:KM], bank[0][:, oc * KM:(oc + 1) * KM], ACT.Identity,
                                               bias=cols[:, 1, oc:oc + 1])
                        ins.then_inc(k_evac, 1)
                    if j == 3 and close:
                        act.wait_ge(lg_centred, t - 1)
                        a.activation(lg_e[:, :], lg_c[:, :], ACT.Exp, accum_out=lg_sum[:, :]).then_inc(lg_exp, 1)
                    if cross:
                        act.wait_ge(v_ps, b + 1)
                        a.copy(v[i][:, :, :], bank[1][:, :].rearrange("p (k d) -> p k d", k=KT)).then_inc(v_evac, 1)
                    if has_prev:
                        act.wait_ge(pT_ps, 2 * b - 1)
                        a.copy(pT[0][:, :, :], bank[4][:, :].rearrange("p (k n) -> p k n", k=KT)).then_inc(pT0_evac, 1)
                    for g in range(G):
                        if cross:
                            act.wait_ge(s_masked, 4 * b + g + 1)
                            if not (isinstance(b, int) and b == 0):
                                act.wait_ge(p_normed, 4 * (b - 1) + g + 1)
                            a.activation(p_exp[g][:, :], s_m[g][:, :], ACT.Exp, bias=s_min[:, g:g + 1], scale=-1.0,
                                         accum_out=p_sum[:, g:g + 1]).then_inc(exp_done, 1)
                        if g == 1 and j == 2 and attend:
                            act.wait_ge(qk1_ps, t)
                            a.activation(qk1[:, :, :, :], misc[:, :].rearrange("p (n c k) -> p n c k", n=2, c=DC),
                                         ACT.Copy, scale=QSCALE ** 0.5).then_inc(qk1_evac, 1)
                        if g == 3 and j == 3 and attend:
                            act.wait_ge(s1_ready, t)
                            a.activation(s1[:, :, :], s1[:, :, :], ACT.Exp).then_inc(exp1_done, 1)
                        if g == 3 and j == 0 and close:
                            act.wait_ge(o1_ps, t - 1)
                            a.copy(o1T[:, :, :], aside).then_inc(o1_evac, 1)
                            a.activation(o1_sq[:, :, :], aside, ACT.Square).then_inc(o1_evac, 1)
                        if g == 0 and j == 2 and attend:
                            act.wait_ge(x1T_ps, t)
                            a.copy(xn1T[:, :, :], turned).then_inc(x1T_evac, 1)
                        if g == 1 and j == 2 and close:
                            act.wait_ge(x2T_ps, t - 1)
                            a.copy(xn2T[:, :, :], aside).then_inc(x2T_evac, 1)
                        if g == 3 and j == 2 and attend:
                            act.wait_ge(v1_ps, t)
                            a.copy(v1[:, :], misc[:, 0:D]).then_inc(v1_evac, 1)

            tile_loop(act, Steps(act, act_steps), 0, body)

            def block_rows(n):
                act.wait_ge(xgT_ps, n + 1)
                a.copy(xgT, bank[5][:, 0:D].rearrange("p (c k) -> p c k", c=DC)).then_inc(xgT_evac, 1)

            def block(n, follow=True):
                act.wait_ge(gate_ps, n + 1)
                a.copy(g_rows, bank[0][:, :]).then_inc(gate_evac, 1)
                if follow:
                    block_rows(n + 1)
                e = act.value_load(table[0:1, 0, bass.ds(n, 1)], min_val=0, max_val=E - 1)
                act.wait_ge(gT_ps, n + 1)
                if not (isinstance(n, int) and n == 0):
                    act.wait_ge(h_ready, n)
                settle(act)
                for f in range(FT):
                    ins = a.activation(silu[:, f, :], bank[2][:, f * P:(f + 1) * P], ACT.Silu,
                                       bias=bg_c[:, bass.ds(e, 1), f:f + 1].squeeze(2))
                ins.then_inc(silu_done, 1)

            act.wait_ge(table_ready, 1)
            block_rows(0)
            block(0)
            with act.Fori(1, NB - 1) as n:
                block(n)
            block(NB - 1, follow=False)

        @block.vector
        def _(dve):
            step = Steps(dve, dve_steps)
            w = nc.vector
            dve.wait_ge(consts_ready, 1)
            dve.wait_ge(x_in, 16)
            for t in range(T):
                w.bn_stats(stats0[:, t, :], x_all[:, t, :])
            step(w.memset(chosen_sum[:, :], 0.0))
            w.tensor_copy(block_no[:, :], block_i[:, :])
            for t in range(T):
                ins = w.bn_aggr(mv0[:, t, :], stats0[:, t, :])
            ins.then_inc(var0_ready, 1)
            step(w.memset(group_mask[:, :], 0.0))
            for i in range(G):
                ins = w.memset(group_mask[i * B:(i + 1) * B, i * (D // G):(i + 1) * (D // G)], 1.0)
            step(ins)
            dve.wait_ge(mask_in, 16 * GH)
            step(w.tensor_scalar(masked[:, :], mask_i[:, :], 0.0, 1.0, ALU.is_equal, ALU.mult))
            w.tensor_scalar(mask_add[:, :], masked[:, :], MASKED, None, ALU.mult)
            step(w.tensor_reduce(all_masked[:, :], masked[:, :], AX.X, ALU.min))
            step(w.tensor_scalar(row_valid[:, :], all_masked[:, :], -1.0, 1.0, ALU.mult, ALU.add))
            dve.wait_ge(consts_ready, 1)
            w.tensor_scalar(valid_diag[:, :], ident[0:S, 0:S], row_valid[0:S, 0:1], None, ALU.mult
                            ).then_inc(valid_diag_ready, 1)
            dve.wait_ge(rstd0_ready, 1)
            for t in range(T):
                w.tensor_scalar(xn_all[:, t, :], x_all[:, t, :], mv0[:, t, 0:1], rstd0[:, t:t + 1],
                                ALU.subtract, ALU.mult).then_inc(xn0_ready, 1)
            dve.wait_ge(valid_ps, 1)
            w.tensor_scalar(q_factor[:, :], bank[0][:, 0:S], -QSCALE, None, ALU.mult).then_inc(q_factor_ready, 1)
            dve.wait_ge(q_factor_ready, 1)
            dve.wait_ge(small_in, 16 * 4)
            for n in range(NCH):
                for oc in range(DC):
                    dve.wait_ge(q0_ps, 2 * n + oc + 1)
                    w.scalar_tensor_tensor(
                        qT[:, oc, n * 512:(n + 1) * 512].rearrange("p (b q) -> p b q", q=S),
                        bank[4 + 2 * n + oc][:, :].rearrange("p (b q) -> p b q", q=S), cols[:, 0, oc:oc + 1],
                        q_factor[:, :].unsqueeze(1).to_broadcast([P, 512 // S, S]), ALU.add, ALU.mult
                        ).then_inc(q0_evac, 1)
            dve.wait_ge(ktail_ps, 1)
            for oc in range(DC):
                ins = w.tensor_scalar(k_tail[:, oc, :], bank[1][:, oc * B:(oc + 1) * B], cols[:, 1, oc:oc + 1], None,
                                      ALU.add)
            ins.then_inc(tails_evac, 1)
            dve.wait_ge(vtail_ps, 1)
            w.tensor_tensor(v_tail_m[:, :], bank[2][:, 0:D], group_mask[:, :], ALU.mult).then_inc(tails_evac, 1)
            w.tensor_reduce(parity[:, :], head_mask[:, :].rearrange("p (a b) -> p b a", b=2), AX.X, ALU.add)
            w.memset(sign[:, 0:1], 1.0)
            w.tensor_scalar(sign[:, 1:2], dw[:, :], -1.0, None, ALU.mult)
            step(w.tensor_scalar(one_m_dw[:, :], dw[:, :], -1.0, 1.0, ALU.mult, ALU.add))
            w.tensor_scalar(sbo_s[:, :], sbo_b[:, :], one_m_dw[:, 0:1], None, ALU.mult)
            dve.wait_ge(self_in, 16 * 8)
            for c in range(DC):
                ins = w.tensor_scalar(so[:, c, :], so[:, c, :], cols[:, 3, c:c + 1], None, ALU.mult)
            step(ins)

            def mask_scores(t, j, g):
                b = t * BT + j
                dve.wait_ge(s_ps, 4 * b + g + 1)
                if not (isinstance(b, int) and b == 0):
                    dve.wait_ge(exp_done, 4 * (b - 1) + g + 1)
                settle(dve)
                w.tensor_tensor_reduce(out=s_m[g][:, :], in0=bank[2 + g % 2][:, 0:K], in1=mask_add[:, :], scale=1.0,
                                       scalar=BIG, op0=ALU.add, op1=ALU.min, accum_out=s_min[:, g:g + 1]
                                       ).then_inc(s_masked, 1)

            def normalise(t, j, c):
                b = t * BT + j
                dve.wait_ge(exp_done, 4 * b + 2 * c + 2)
                step(w.reciprocal(p_inv[:, 2 * c:2 * c + 2], p_sum[:, 2 * c:2 * c + 2]))
                for g in (2 * c, 2 * c + 1):
                    w.tensor_scalar(p_n[j % 2][:, g, :], p_exp[g][:, :], p_inv[:, g:g + 1], None, ALU.mult
                                    ).then_inc(p_normed, 1)

            def norm_stats(x_ap, st, m, ready):
                settle(dve)
                step(w.bn_stats(st[:, :], x_ap))
                settle(dve)
                w.bn_aggr(m[:, :], st[:, :]).then_inc(ready, 1)

            def body(t, cross, attend, close):
                misc, aside = bank[7], bank[1]
                for j in range(BT):
                    b = t * BT + j
                    pj = (j - 1) % BT
                    has_prev = cross if j else (not (isinstance(t, int) and t <= 0) and (cross or attend))
                    if j == 0 and close:
                        dve.wait_ge(exp1_done, t - 1)
                        step(w.tensor_reduce(p1_sum[:, :], s1[:, :, :], AX.X, ALU.add))
                        step(w.reciprocal(p1_inv[:, :], p1_sum[:, :]))
                        w.tensor_tensor(p1_fac[:, :].rearrange("p (h i) -> p h i", i=2),
                                        p1_inv[:, :].rearrange("p (h i) -> p h i", i=2),
                                        sign[:, :].unsqueeze(1).to_broadcast([P, H // 2, 2]), ALU.mult
                                        ).then_inc(p1_fac_ready, 1)
                    if j == 2 and attend:
                        dve.wait_ge(rstd1_ready, t)
                        w.tensor_scalar(xn1[:, :], x1[:, :], mv[:, 0:1], rstd[:, 0:1], ALU.subtract, ALU.mult
                                        ).then_inc(xn1_ready, 1)
                    if j == 2 and close:
                        dve.wait_ge(rstd2_ready, t - 1)
                        if not (isinstance(t, int) and t <= 2):
                            dve.wait_ge(xn2_stored, 16 * (t - 2))
                        w.tensor_scalar(xn2[:, :], x2[:, :], mv2[:, 0:1], rstd2[:, 0:1], ALU.subtract, ALU.mult
                                        ).then_inc(xn2_ready, 1)
                    if j == 3 and close:
                        dve.wait_ge(lg_exp, t - 1)
                        dve.wait_ge(chosen_ready, t - 1)
                        step(w.tensor_tensor_reduce(out=lg_m[:, :], in0=lg_e[:, :], in1=chosen[:, :], scale=1.0,
                                                    scalar=0.0, op0=ALU.mult, op1=ALU.add, accum_out=chosen_e[:, :]))
                        step(w.scalar_tensor_tensor(gate_den[:, :], lg_sum[:, :], 1e-9, chosen_e[:, :],
                                                    ALU.mult, ALU.add))
                        step(w.reciprocal(gate_inv[:, :], gate_den[:, :]))
                        w.tensor_scalar(gates[:, :], lg_m[:, :], gate_inv[:, 0:1], None, ALU.mult
                                        ).then_inc(gates_ready, 1)
                    if cross:
                        mask_scores(t, j, 0)
                        mask_scores(t, j, 1)
                    if has_prev:
                        dve.wait_ge(pT_ps, 2 * b)
                        w.tensor_copy(pT[1][:, :, :], bank[5][:, :].rearrange("p (k n) -> p k n", k=KT)
                                      ).then_inc(pT1_evac, 1)
                        dve.wait_ge(end_ps, b)
                        w.tensor_copy(p_end[:, :], bank[6][0:G, P:2 * P]).then_inc(end_evac, 1)
                    if j == 0 and close:
                        dve.wait_ge(att_ready, t - 1)
                        for q in range(BT):
                            ins = w.transpose(attT_bd[32 * q:32 * q + 32, :, q, :], att[32 * q:32 * q + 32, :, :])
                        ins.then_inc(attT_ready, 1)
                    if cross:
                        normalise(t, j, 0)
                    if j == 1 and close:
                        dve.wait_ge(y1_ps, t - 1)
                        w.tensor_scalar(ms[:, :], aside[:, D:D + 1], 1.0 / D, RMS_EPS, ALU.mult, ALU.add
                                        ).then_inc(ms_ready, 1)
                    if cross:
                        mask_scores(t, j, 2)
                        mask_scores(t, j, 3)
                    if j == 3 and close:
                        dve.wait_ge(rank_ps, t - 1)
                        step(w.tensor_tensor(pos[:, :], aside[:, 0:E], region[:, :], ALU.add))
                        w.tensor_copy(gatesT[:, :], aside[0:E, P:2 * P]).then_inc(gT_ready, 1)
                        dve.wait_ge(gates_ready, t - 1)
                        if not (isinstance(t, int) and t <= 2):
                            dve.wait_ge(slots_stored, 16 * TOPK * (t - 2))
                        for r in range(TOPK):
                            w.tensor_tensor_reduce(out=gate_hit[:, r, :], in0=gates[:, :], in1=hit[:, r, :], scale=1.0,
                                                   scalar=0.0, op0=ALU.mult, op1=ALU.add, accum_out=entry[:, r, 1:2])
                        for r in range(TOPK):
                            ins = w.tensor_tensor_reduce(out=pos_hit[:, r, :], in0=pos[:, :], in1=hit[:, r, :],
                                                         scale=1.0, scalar=0.0, op0=ALU.mult, op1=ALU.add,
                                                         accum_out=slot_f[:, r:r + 1])
                        step(ins)
                        w.tensor_copy(slot_u[:, :], slot_f[:, :])
                        w.tensor_copy(entry_i[:, :, 0], token_no[:, bass.ds(t - 2, 1)].to_broadcast([P, TOPK]))
                        w.tensor_tensor(chosen_sum[:, :], chosen_sum[:, :], chosen[:, :], ALU.add
                                        ).then_inc(slots_ready, 1)
                    if j == 1 and close:
                        dve.wait_ge(rms_ready, t - 1)
                        step(w.scalar_tensor_tensor(x2[:, :], aside[:, 0:D], rms[:, 0:1], x1b[:, :],
                                                    ALU.mult, ALU.add))
                        norm_stats(x2[:, :], stats2, mv2, var2_ready)
                    if j == 1 and attend:
                        dve.wait_ge(y_ps, t)
                        if isinstance(t, int) and t == 1:
                            dve.wait_ge(xb_ready, 1)
                        step(w.tensor_tensor(x1[:, :], misc[:, 0:D], x_all[:, bass.ds(t - 1, 1), :].squeeze(1),
                                             ALU.add))
                        w.tensor_tensor(x1b[:, :], x1[:, :], sbo_s[:, :], ALU.add)
                        norm_stats(x1[:, :], stats, mv, var1_ready)
                    if j == 3 and close:
                        dve.wait_ge(seed_ps, t - 1)
                        if not (isinstance(t, int) and t <= 2):
                            dve.wait_ge(y0_stored, 16 * (t - 2))
                        w.tensor_tensor(y0[:, :], aside[:, 0:D], x2[:, :], ALU.add).then_inc(y0_ready, 1)
                    if j == 3 and attend:
                        dve.wait_ge(s1_ps, t)
                        step(w.transpose(s1[:, :, :].rearrange("p h k -> p (h k)"), misc[:, :]))
                        step(w.tensor_reduce(s1_max[:, :], s1[:, :, :], AX.X, ALU.max))
                        w.tensor_tensor(s1[:, :, :], s1[:, :, :],
                                        s1_max[:, :].unsqueeze(2).to_broadcast([P, H, S]), ALU.subtract
                                        ).then_inc(s1_ready, 1)
                    if cross:
                        normalise(t, j, 1)
                    if j == 2 and close:
                        dve.wait_ge(lg_ps, t - 1)
                        w.tensor_copy(lg[:, :], aside[:, 0:E]).then_inc(lg_evac, 1)
                    if has_prev:
                        dve.wait_ge(o_ps, b)
                        o4 = bank[6][:, 0:P].rearrange("p (c a q) -> p c a q", c=DC, a=2)
                        for c in range(DC):
                            ins = w.tensor_scalar(o_even[:, c, :], o4[:, c, 0, :], parity[:, 0:1], cols[:, 2, c:c + 1],
                                                  ALU.mult, ALU.add)
                        step(ins)
                        w.scalar_tensor_tensor(oT[:, :, pj * S:(pj + 1) * S], o4[:, :, 1, :], parity[:, 1:2],
                                               o_even[:, :, :], ALU.mult, ALU.add).then_inc(o_evac, 1)
                    if j == 2 and close:
                        dve.wait_ge(lg_evac, t - 1)
                        settle(dve)
                        step(w.max(top8[:, :], lg[:, :]))
                        w.tensor_scalar(lg_c[:, :], lg[:, :], top8[:, 0:1], None, ALU.subtract).then_inc(lg_centred, 1)
                        for r, rest in enumerate((lg, lg_rest)):
                            step(w.scalar_tensor_tensor(lead[:, :], rest[:, :], top8[:, r:r + 1], expert_from[:, :],
                                                        ALU.is_equal, ALU.mult))
                            step(w.tensor_reduce(lead_max[:, :], lead[:, :], AX.X, ALU.max))
                            step(w.tensor_scalar(hit[:, r, :], expert_from[:, :], lead_max[:, 0:1], None,
                                                 ALU.is_equal))
                            if r == 0:
                                step(w.scalar_tensor_tensor(lg_rest[:, :], hit[:, 0, :], -BIG, lg[:, :],
                                                            ALU.mult, ALU.add))
                        w.tensor_tensor(chosen[:, :], hit[:, 0, :], hit[:, 1, :], ALU.add).then_inc(chosen_ready, 1)

            tile_loop(dve, step, DVE_STEPS, body)

            dve.wait_ge(count_ps, 1)
            step(w.tensor_scalar(count_i[:, :], bank[7][:, 0:E], float(P - 1), None, ALU.add))
            step(w.tensor_scalar(nblocks_i[:, :], count_i[:, :], P.bit_length() - 1, None, ALU.logical_shift_right))
            step(w.tensor_copy(nblocks[:, :], nblocks_i[:, :]))
            step(w.tensor_tensor(nblocks_t[:, :, :], nblocks[:, :].unsqueeze(1).to_broadcast([P, E, E]),
                                 up_to[:, :, :], ALU.mult))
            step(w.tensor_reduce(ends[:, :], nblocks_t[:, :, :], AX.X, ALU.add))
            step(w.tensor_tensor(past[:, :, :], ends[:, 0:E - 1].unsqueeze(1).to_broadcast([P, NB, E - 1]),
                                 block_no[:, :].unsqueeze(2).to_broadcast([P, NB, E - 1]), ALU.is_le))
            step(w.tensor_reduce(b_expert[:, :], past[:, :, :], AX.X, ALU.add))
            step(w.tensor_tensor(past[:, :, :], past[:, :, :],
                                 nblocks[:, 0:E - 1].unsqueeze(1).to_broadcast([P, NB, E - 1]), ALU.mult))
            step(w.tensor_reduce(b_start[:, :], past[:, :, :], AX.X, ALU.add))
            w.tensor_scalar(b_region[:, :], b_expert[:, :], float(REGION), None, ALU.mult)
            w.tensor_scalar(b_late[:, :], b_expert[:, :], float(E - LATE), 48.0 * LATE, ALU.is_ge, ALU.mult)
            step(w.tensor_tensor(b_within[:, :], block_no[:, :], b_start[:, :], ALU.subtract))
            w.tensor_copy(table[:, 0, :], b_expert[:, :])
            w.tensor_scalar(table[:, 1, :], b_expert[:, :], float(-EW), float((E - 1) * EW), ALU.mult, ALU.add)
            w.tensor_scalar(table[:, 3, :], b_late[:, :], 16.0, None, ALU.add)
            w.scalar_tensor_tensor(table[:, 2, :], b_within[:, :], float(P), b_region[:, :], ALU.mult, ALU.add
                                   ).then_inc(table_ready, 1)

            def get(n):
                if not (isinstance(n, int) and n == 0):
                    dve.wait_ge(xgT_ps, n)
                dve.wait_ge(ids_in, 16 * (n + 1))
                w.tensor_copy(get_i[:, :], ids_i[:, bass.ds(n, 1), 0]).then_inc(get_ready, 1)

            def weigh(n):
                dve.wait_ge(down_ps, n + 1)
                if not (isinstance(n, int) and n == 0):
                    dve.wait_ge(rows_added, 16 * n)
                w.tensor_copy(add_i[:, :], ids_i[:, bass.ds(n, 1), 0])
                w.tensor_scalar(y_rows, bank[4][:, 0:D], ids[:, bass.ds(n, 1), 1:2].squeeze(1), None, ALU.mult
                                ).then_inc(add_ready, 1)

            def block(n, follow=True):
                dve.wait_ge(up_ps, n + 1)
                w.tensor_copy(u_rows, bank[1][:, :]).then_inc(up_evac, 1)
                if not (isinstance(n, int) and n == 0):
                    weigh(n - 1)
                if follow:
                    get(n + 2)
                e = dve.value_load(table[0:1, 0, bass.ds(n, 1)], min_val=0, max_val=E - 1)
                dve.wait_ge(uT_ps, n + 1)
                dve.wait_ge(silu_done, n + 1)
                for f in range(FT):
                    ins = w.scalar_tensor_tensor(hT[:, f, :], bank[3][:, f * P:(f + 1) * P],
                                                 bu_c[:, bass.ds(e, 1), f:f + 1].squeeze(2), silu[:, f, :],
                                                 ALU.add, ALU.mult)
                ins.then_inc(h_ready, 1)

            dve.wait_ge(table_ready, 1)
            get(0)
            get(1)
            block(0)
            with dve.Fori(1, NB - 2) as n:
                block(n)
            block(NB - 2, follow=False)
            block(NB - 1, follow=False)
            weigh(NB - 1)


def kernel(**inputs):
    import numpy as _np
    import concourse.bacc as _bacc
    from concourse import mybir as _mybir
    from concourse.bass_utils import run_bass_kernel_spmd as _run

    a = {k: _np.asarray(v) for k, v in inputs.items()}
    ctx = a["ctx_1024"]
    ins = {
        "x": a["x"].reshape(TOK, D),
        "ctxT": ctx.transpose(2, 0, 1),
        "ctx_tailT": ctx[:, KM, :].T,
        "mask": a["mask_1x1xSxS2_ik1"].reshape(S, K),
        "wqT": a["L0_xattn_wq"].T, "wkT": a["L0_xattn_wk"].T, "wvT": a["L0_xattn_wv"].T,
        "columns": _np.stack([a[n].reshape(DC, P).T for n in (
            "L0_xattn_bq", "L0_xattn_bk", "L0_xattn_bv", "L0_attn_norm_w")], axis=1),
        "woT": a["L0_xattn_wo"].T, "bo": a["L0_xattn_bo"],
        "sqT": a["L0_attn_Wq"].T, "skT": a["L0_attn_Wk"].T, "svT": a["L0_attn_Wv"].T,
        "soT": a["L0_attn_Wo"].T, "sbo": a["L0_attn_bo"],
        "diff_weight": a["L0_attn_diff_weight"].reshape(1),
        "routerT": a["L0_ffn_router_w"].T,
        "gate_w": a["L0_ffn_gate_w"], "gate_b": a["L0_ffn_gate_b"].reshape(E, FT, P).transpose(2, 0, 1),
        "up_w": a["L0_ffn_up_w"], "up_b": a["L0_ffn_up_b"].reshape(E, FT, P).transpose(2, 0, 1),
        "down_w": a["L0_ffn_down_w"], "down_b": a["L0_ffn_down_b"],
        "empty_slots": _np.stack([TOK + _np.arange(SLOTS) % P, _np.zeros(SLOTS)], axis=1).astype(_np.int32),
    }
    nc = _bacc.Bacc("TRN2", target_bir_lowering=False, num_devices=1)
    arrays, args = {}, []
    for name, value in ins.items():
        value = _np.ascontiguousarray(value)
        arrays[f"in_{name}"] = value
        args.append(nc.dram_tensor(f"in_{name}", value.shape, _mybir.dt.from_np(value.dtype),
                                   kind="ExternalInput").ap())
    args.append(nc.dram_tensor("v_tail_d", (G * B, D), F32, kind="Internal").ap())
    args.append(nc.dram_tensor("expert_x", (TOK + P, D), F32, kind="Internal").ap())
    args.append(nc.dram_tensor("slots", (SLOTS, 2), I32, kind="Internal").ap())
    args.append(nc.dram_tensor("out_0", (TOK + P, D), F32, kind="ExternalOutput").ap())
    perceiver_program(nc, *args)
    r = _run(nc, [arrays], core_ids=[0])
    return r.results[0]["out_0"][:TOK].reshape(B, S, D)
```

```python
from contextlib import ExitStack

import concourse.bass as bass
from concourse import mybir

ALU = mybir.AluOpType
ACT = mybir.ActivationFunctionType
AX = mybir.AxisListType
F32 = mybir.dt.float32
I32 = mybir.dt.int32
U32 = mybir.dt.uint32

P = 128
D = 256
DC = D // P
B = 32
S = 32
K = 257
KM = 256
KT = KM // P
H = 16
HD = D // H
GH = P // S
G = H // GH
HH = H // DC
T = B * S // P
BT = P // S
E = 8
F = 512
FT = F // P
TOK = B * S
TOPK = 2
REGION = TOK
NB = (TOK * TOPK + E * (P - 1)) // P
TA = T - 2
NA = -(-(TOPK * P * TA - E * (P - 1)) // P)
assert NA == 5
SLOTS = (E - 1) * REGION + max(REGION, NB * P)
EW = (2 * DC * F + FT * D)
LATE = 2
NCH = TOK // 512
MASKED = 10000.0
BIG = 3.0e38
LN_EPS = 1e-5
RMS_EPS = 1.1920928955078125e-07
QSCALE = HD ** -0.5
POOL_STEPS, DVE_STEPS = 4, 33


class Steps:

    def __init__(self, eng, sem):
        self.eng, self.sem, self.n, self.base = eng, sem, 0, 0

    def __call__(self, ins):
        self.n += 1
        ins.then_inc(self.sem, 1)
        self.eng.wait_ge(self.sem, self.base + self.n)


def tile_loop(eng, steps, per_tile, body):
    body(0, True, False, False)
    body(1, True, True, False)
    before = steps.n
    with eng.Fori(2, T) as t:
        steps.base, steps.n = (t - 2) * per_tile + before, 0
        body(t, True, True, True)
        assert steps.n == per_tile, (steps.sem, steps.n)
    steps.base, steps.n = 0, before + (T - 2) * per_tile
    body(T, False, True, True)
    body(T + 1, False, False, True)


def perceiver_program(nc, x, ctxT, ctx_tailT, mask, wqT, wkT, wvT, columns, woT, bo,
                      sqT, skT, svT, soT, sbo, diff_weight,
                      routerT, gate_w, gate_b, up_w, up_b, down_w, down_b, empty_slots,
                      v_tail_d, expert_x, slots, out):
    with ExitStack() as ctx:
        def sb(name, shape, dt=F32):
            return ctx.enter_context(nc.sbuf_tensor(name, shape, dt))

        def sem(name):
            return ctx.enter_context(nc.semaphore(name))

        bank = [ctx.enter_context(nc.psum_tensor(f"bank{i}", [P, 512], F32)) for i in range(8)]

        ident = sb("ident", [P, P])
        ones_col = sb("ones_col", [P, 1])
        ones_rows = sb("ones_rows", [S, P])
        head_mask = sb("head_mask", [P, HH])
        parity = sb("parity", [P, 2])
        expert_from = sb("expert_from", [P, E])
        group_mask = sb("group_mask", [P, D])
        neg_half = sb("neg_half", [P, T])
        wq, wk, wv, wo = (sb(n, [P, DC, D]) for n in ("wq", "wk", "wv", "wo"))
        sq, sk, sv, so = (sb(n, [P, DC, D]) for n in ("sq", "sk", "sv", "so"))
        wr = sb("wr", [P, DC, E])
        cols = sb("cols", [P, 4, DC])
        bo_b = sb("bo_b", [P, D])
        sbo_b = sb("sbo_b", [P, D])
        sbo_s = sb("sbo_s", [P, D])
        dw = sb("dw", [P, 1])
        one_m_dw = sb("one_m_dw", [P, 1])
        sign = sb("sign", [P, 2])
        bg_c = sb("bg_c", [P, E, FT])
        bu_c = sb("bu_c", [P, E, FT])
        bd_r = sb("bd_r", [E, D])
        mask_i = sb("mask_i", [P, K], I32)
        masked = sb("masked", [P, K])
        mask_add = sb("mask_add", [P, K])
        all_masked = sb("all_masked", [P, 1])
        row_valid = sb("row_valid", [P, 1])
        valid_diag = sb("valid_diag", [S, S])
        q_factor = sb("q_factor", [P, S])
        arena = sb("arena", [P, E * EW])
        taken = [0]

        def cut(shape, limit=LATE * EW):
            size = 1
            for n in shape:
                size *= n
            part = arena[:, taken[0]:taken[0] + size]
            taken[0] += size
            assert taken[0] <= limit, (taken[0], limit)
            if len(shape) == 1:
                return part
            names = "abc"[:len(shape)]
            sizes = {n: k for n, k in zip(names, shape)}
            return part.rearrange(f"p ({' '.join(names)}) -> p {' '.join(names)}", **sizes)

        ctx_b = [cut([DC, KM]) for _ in range(BT)]
        kT = [cut([DC, K]) for _ in range(2)]
        v = [cut([KT, D]) for _ in range(2)]
        q_bd = [cut([DC, HH, S]) for _ in range(2)]
        taken[0] = E * EW - 2 * T * D
        xn_all = cut([T, D], E * EW)
        xnT_all = cut([DC, TOK], E * EW)
        work = sb("work", [P, 2 * G * K + G * K + DC * KT * 2 * P])
        at = [0]

        def piece(n):
            at[0] += n
            assert at[0] <= work.shape[1], at[0]
            return work[:, at[0] - n:at[0]]

        s_m = [piece(K) for g in range(G)]
        p_exp = [piece(K) for g in range(G)]
        p_n1 = piece(G * K).rearrange("p (g k) -> p g k", g=G)
        pT = [piece(KT * 2 * P).rearrange("p (k n) -> p k n", k=KT) for c in range(DC)]
        p_n = [sb("p_n0", [P, G, K]), p_n1]
        at[0] = 0
        xg = piece(D)
        xgT = piece(D).rearrange("p (c k) -> p c k", c=DC)
        g_rows = piece(F)
        u_rows = piece(F)
        silu = piece(F).rearrange("p (f k) -> p f k", f=FT)
        hT = piece(F).rearrange("p (f k) -> p f k", f=FT)
        y_rows = piece(D)
        x_all = sb("x_all", [P, T, D])
        qT = sb("qT", [P, DC, TOK])
        stats0 = sb("stats0", [P, T, 6])
        mv0 = sb("mv0", [P, T, 2])
        rstd0 = sb("rstd0", [P, T])
        ctx_tail = sb("ctx_tail", [P, DC, G, B])
        k_tail = sb("k_tail", [P, DC, B])
        v_tail_m = sb("v_tail_m", [P, D])
        v_end = [sb(f"v_end{j}", [G, D]) for j in range(BT)]
        s_min = sb("s_min", [P, G])
        p_sum = sb("p_sum", [P, G])
        p_inv = sb("p_inv", [P, G])
        p_end = sb("p_end", [G, P])
        o_even = sb("o_even", [P, DC, S])
        oT = sb("oT", [P, DC, P])
        x1 = sb("x1", [P, D])
        x1b = sb("x1b", [P, D])
        stats = sb("stats", [P, 6])
        mv = sb("mv", [P, 2])
        rstd = sb("rstd", [P, 1])
        xn1 = sb("xn1", [P, D])
        xn1T = sb("xn1T", [P, DC, P])
        qk1 = sb("qk1", [P, 2, DC, P])
        q1_bd = sb("q1_bd", [P, DC, BT, HH, S])
        v1 = sb("v1", [P, D])
        s1 = sb("s1", [P, H, S])
        s1_max = sb("s1_max", [P, H])
        p1_sum = sb("p1_sum", [P, H])
        p1_inv = sb("p1_inv", [P, H])
        p1_fac = sb("p1_fac", [P, H])
        att = sb("att", [P, H // 2, S])
        attT_bd = sb("attT_bd", [P, H // 2, BT, S])
        o1T = sb("o1T", [P, DC, P])
        o1_sq = sb("o1_sq", [P, DC, P])
        ms = sb("ms", [P, 1])
        rms = sb("rms", [P, 1])
        x2 = sb("x2", [P, D])
        stats2 = sb("stats2", [P, 6])
        mv2 = sb("mv2", [P, 2])
        rstd2 = sb("rstd2", [P, 1])
        xn2 = sb("xn2", [P, D])
        xn2T = sb("xn2T", [P, DC, P])
        lg = sb("lg", [P, E])
        top8 = sb("top8", [P, 8])
        lg_rest = sb("lg_rest", [P, E])
        lead = sb("lead", [P, E])
        lead_max = sb("lead_max", [P, 1])
        hit = sb("hit", [P, TOPK, E])
        chosen = sb("chosen", [P, E])
        chosen_sum = sb("chosen_sum", [P, E])
        lg_c = sb("lg_c", [P, E])
        lg_e = sb("lg_e", [P, E])
        lg_sum = sb("lg_sum", [P, 1])
        lg_m = sb("lg_m", [P, E])
        chosen_e = sb("chosen_e", [P, 1])
        gate_den = sb("gate_den", [P, 1])
        gate_inv = sb("gate_inv", [P, 1])
        gates = sb("gates", [P, E])
        gate_hit = sb("gate_hit", [P, TOPK, E])
        gatesT = sb("gatesT", [E, P])
        before = sb("before", [P, P])
        ones_sq = sb("ones_sq", [P, P])
        region = sb("region", [P, E])
        region_no = sb("region_no", [P, E])
        token_no = sb("token_no", [P, T], I32)
        pos = sb("pos", [P, E])
        pos_hit = sb("pos_hit", [P, TOPK, E])
        slot_f = sb("slot_f", [P, TOPK])
        slot_u = sb("slot_u", [P, TOPK], U32)
        entry = sb("entry", [P, TOPK, 2])
        entry_i = entry[:, :, :].bitcast(I32)
        zeros = sb("zeros", [P, D])
        y0 = sb("y0", [P, D])
        up_to = sb("up_to", [P, E, E])
        block_i = sb("block_i", [P, NB], I32)
        block_no = sb("block_no", [P, NB])
        count_i = sb("count_i", [P, E], I32)
        nblocks_i = sb("nblocks_i", [P, E], I32)
        nblocks = sb("nblocks", [P, E])
        nblocks_t = sb("nblocks_t", [P, E, E])
        ends = sb("ends", [P, E])
        past = sb("past", [P, NB, E + 1])
        of_expert = sb("of_expert", [P, NB, E])
        whole = sb("whole", [P, E])
        early = sb("early", [P, E])
        base = sb("base", [P, E])
        b_expert = sb("b_expert", [P, NB])
        b_base = sb("b_base", [P, NB])
        b_first = sb("b_first", [P, NB])
        table = sb("table", [P, 3, NB], I32)
        ids_i = sb("ids", [P, NB, 2], I32)
        ids = ids_i[:, :, :].bitcast(F32)
        get_i = sb("get_i", [P, 1], I32)
        add_i = sb("add_i", [P, 1], I32)

        x_in, small_in, wq_in, wkv_in, wo_in, self_in, tail_in, vtail_in = (
            sem(n) for n in ("x_in", "small_in", "wq_in", "wkv_in", "wo_in", "self_in", "tail_in", "vtail_in"))
        mask_in = sem("mask_in")
        ctx_in = [sem(f"ctx_in{j}") for j in range(BT)]
        vend_in = [sem(f"vend_in{j}") for j in range(BT)]
        experts_in, late_in, empty_in, pads_in, xn2_stored, y0_stored, slots_stored, ids_in, rows_in, rows_added = (
            sem(n) for n in ("experts_in", "late_in", "empty_in", "pads_in", "xn2_stored", "y0_stored",
                             "slots_stored", "ids_in", "rows_in", "rows_added"))
        last_xn2_stored, last_y0_stored, last_slots_stored = (
            sem(n) for n in ("last_xn2_stored", "last_y0_stored", "last_slots_stored"))
        pool_steps, dve_steps, act_steps = sem("pool_steps"), sem("dve_steps"), sem("act_steps")
        consts_ready, var0_ready, rstd0_ready, xn0_ready = (
            sem(n) for n in ("consts_ready", "var0_ready", "rstd0_ready", "xn0_ready"))
        xT0_ps, xT0_evac, q0_ps, q0_evac, valid_diag_ready, valid_ps, q_factor_ready = (
            sem(n) for n in ("xT0_ps", "xT0_evac", "q0_ps", "q0_evac", "valid_diag_ready", "valid_ps", "q_factor_ready"))
        ktail_ps, tails_evac, vtail_ps, xb_ready = (
            sem(n) for n in ("ktail_ps", "tails_evac", "vtail_ps", "xb_ready"))
        k_ps, k_evac, v_ps, v_evac, batch_ready = (
            sem(n) for n in ("k_ps", "k_evac", "v_ps", "v_evac", "batch_ready"))
        s_ps, s_masked, exp_done, p_normed = (sem(n) for n in ("s_ps", "s_masked", "exp_done", "p_normed"))
        pT_ps, pT0_evac, pT1_evac, end_ps, end_evac, o_ps, o_evac = (
            sem(n) for n in ("pT_ps", "pT0_evac", "pT1_evac", "end_ps", "end_evac", "o_ps", "o_evac"))
        y_ps, var1_ready, rstd1_ready, xn1_ready, x1T_ps, x1T_evac = (
            sem(n) for n in ("y_ps", "var1_ready", "rstd1_ready", "xn1_ready", "x1T_ps", "x1T_evac"))
        qk1_ps, qk1_evac, q1_bd_ready, v1_ps, v1_evac, s1_ps = (
            sem(n) for n in ("qk1_ps", "qk1_evac", "q1_bd_ready", "v1_ps", "v1_evac", "s1_ps"))
        s1_ready, exp1_done, attT_ready, o1_ps, o1_evac, y1_ps, ms_ready, rms_ready = (
            sem(n) for n in ("s1_ready", "exp1_done", "attT_ready", "o1_ps", "o1_evac", "y1_ps", "ms_ready", "rms_ready"))
        var2_ready, rstd2_ready, xn2_ready, x2T_ps, x2T_evac, lg_ps, lg_evac = (
            sem(n) for n in ("var2_ready", "rstd2_ready", "xn2_ready", "x2T_ps", "x2T_evac", "lg_ps", "lg_evac"))
        lg_centred, lg_exp, chosen_ready, gates_ready, rank_ps, gT_ready, slots_ready, seed_ps, y0_ready = (
            sem(n) for n in ("lg_centred", "lg_exp", "chosen_ready", "gates_ready", "rank_ps", "gT_ready",
                             "slots_ready", "seed_ps", "y0_ready"))
        q1_bd_half_ready = sem("q1_bd_half_ready")
        p1_fac_ready, att_ready = sem("p1_fac_ready"), sem("att_ready")
        zeros_ready, count_ps, table_ready = (sem(n) for n in ("zeros_ready", "count_ps", "table_ready"))
        get_ready, add_ready = sem("get_ready"), sem("add_ready")
        xgT_ps, xgT_evac, gate_ps, gate_evac, up_ps, up_evac = (
            sem(n) for n in ("xgT_ps", "xgT_evac", "gate_ps", "gate_evac", "up_ps", "up_evac"))
        gT_ps, uT_ps, silu_done, h_ready, down_ps = (
            sem(n) for n in ("gT_ps", "uT_ps", "silu_done", "h_ready", "down_ps"))

        def settle(eng):
            eng.nop(nofuse=True)

        block = ctx.enter_context(nc.Block())

        def halves(w):
            return w.rearrange("(c p) n -> p c n", p=P)

        @block.sync
        def _(sp):
            sp.dma_start(x_all[:, :, :], x.rearrange("(t p) d -> p t d", p=P)).then_inc(x_in, 16)
            sp.dma_start(cols[:, :, :], columns).then_inc(small_in, 16)
            sp.dma_start(bo_b[:, :], bo.partition_broadcast(P)).then_inc(small_in, 16)
            sp.dma_start(sbo_b[:, :], sbo.partition_broadcast(P)).then_inc(small_in, 16)
            sp.dma_start(dw[:, :], diff_weight.partition_broadcast(P)).then_inc(small_in, 16)
            for h in range(GH):
                sp.dma_start(mask_i[h * S:(h + 1) * S, :], mask).then_inc(mask_in, 16)
            sp.dma_start(wq[:, :, :], halves(wqT)).then_inc(wq_in, 16)
            for g in range(G):
                sp.dma_start(ctx_tail[:, :, g, :], halves(ctx_tailT)).then_inc(tail_in, 16)
            sp.dma_start(wk[:, :, :], halves(wkT)).then_inc(wkv_in, 16)
            sp.dma_start(wv[:, :, :], halves(wvT)).then_inc(wkv_in, 16)

            def load_context(t, j):
                sp.dma_start(ctx_b[j][:, :, :],
                             ctxT.rearrange("(c p) (t j) k -> p c t j k", p=P, j=BT)[:, :, t, j, 0:KM]
                             ).then_inc(ctx_in[j], 16)

            for j in range(BT):
                load_context(0, j)
            sp.dma_start(wo[:, :, :], halves(woT)).then_inc(wo_in, 16)
            for dst, src in ((sq, sqT), (sk, skT), (sv, svT), (so, soT), (wr, routerT)):
                sp.dma_start(dst[:, :, :], halves(src)).then_inc(self_in, 16)
            sp.dma_start(bg_c[:, :, :], gate_b).then_inc(self_in, 16)
            sp.dma_start(bu_c[:, :, :], up_b).then_inc(self_in, 16)
            sp.dma_start(bd_r[:, :], down_b).then_inc(self_in, 16)
            sp.dma_start(slots, empty_slots).then_inc(empty_in, 16)
            sp.wait_ge(zeros_ready, 1)
            sp.dma_start(expert_x[TOK:TOK + P, :], zeros[:, :]).then_inc(pads_in, 16)
            sp.dma_start(out[TOK:TOK + P, :], zeros[:, :]).then_inc(pads_in, 16)
            for t in range(TA, T):
                sp.dma_start(expert_x[t * P:(t + 1) * P, :], zeros[:, :]).then_inc(pads_in, 16)
                sp.dma_start(out[t * P:(t + 1) * P, :], zeros[:, :]).then_inc(pads_in, 16)
            sp.wait_ge(tails_evac, 2)
            sp.dma_start(v_tail_d, v_tail_m[:, :]).then_inc(vtail_in, 16)
            sp.wait_ge(vtail_in, 16)

            def load_tail(b, j):
                sp.dma_start(v_end[j][:, :], v_tail_d.rearrange("(g b) d -> g b d", b=B)[:, bass.ds(b, 1), :]
                             .squeeze(1)).then_inc(vend_in[j], 16)

            for j in range(BT - 1):
                load_tail(j, j)

            def load_expert(e, signal):
                at_e = (E - 1 - e) * EW
                for k, (src, n) in enumerate(((gate_w, DC), (up_w, DC), (down_w, FT))):
                    sp.dma_start(arena[:, bass.ds(at_e + k * DC * F, DC * F)].rearrange("p (c f) -> p c f", c=n),
                                 src.rearrange("e (c p) f -> p e c f", p=P)[:, bass.ds(e, 1), :, :].squeeze(1)
                                 ).then_inc(signal, 16)

            def body(s):
                fixed = isinstance(s, int)
                for j in range(BT):
                    if not fixed or s < T:
                        sp.wait_ge(v_ps, (s - 1) * BT + j + 1)
                        load_context(s, j)
                    if not fixed or s < T or (s == T and j == 0):
                        if not (fixed and s == 1 and j == 0):
                            sp.wait_ge(o_ps, (s - 1) * BT + j)
                        load_tail(s * BT + j - 1, (j - 1) % BT)
                    if j == 1 and (not fixed or s >= 3):
                        sp.wait_ge(xn2_ready, s - 2)
                        sp.dma_start(expert_x[bass.ds((s - 3) * P, P), :], xn2[:, :]
                                     ).then_inc(last_xn2_stored if fixed and s - 3 >= TA else xn2_stored, 16)
                if not fixed or s >= 3:
                    sp.wait_ge(y0_ready, s - 2)
                    sp.dma_start(out[bass.ds((s - 3) * P, P), :], y0[:, :]
                                 ).then_inc(last_y0_stored if fixed and s - 3 >= TA else y0_stored, 16)

            body(1)
            load_expert(0, experts_in)
            load_expert(1, experts_in)
            body(2)
            load_expert(2, experts_in)
            with sp.Fori(3, 6) as s:
                body(s)
                load_expert(s, experts_in)
            for s in range(6, T + 1):
                body(s)

            def load_ids(first, after):
                with sp.Fori(first, after) as n:
                    row = sp.value_load(table[0:1, 2, bass.ds(n, 1)], min_val=0, max_val=SLOTS - P)
                    sp.dma_start(ids_i[:, bass.ds(n, 1), :].squeeze(1), slots[bass.ds(row, P), :]).then_inc(ids_in, 16)
                    sp.wait_ge(ids_in, 16 * (n + 1))
                    settle(sp)

            sp.wait_ge(o_ps, B)
            for e in range(E - LATE, E):
                load_expert(e, late_in)
            sp.wait_ge(slots_stored, 16 * TOPK * TA)
            sp.wait_ge(table_ready, 1)
            load_ids(0, NA)
            body(T + 1)
            body(T + 2)
            sp.wait_ge(last_slots_stored, 16 * TOPK * (T - TA))
            sp.wait_ge(table_ready, 2)
            load_ids(NA, NB)
            sp.wait_ge(rows_added, 16 * NB)

        @block.gpsimd
        def _(pool):
            step = Steps(pool, pool_steps)
            g = nc.gpsimd
            g.memset(ident[:, :], 0.0)
            g.memset(ones_col[:, :], 1.0)
            g.memset(ones_rows[:, :], 1.0)
            g.memset(neg_half[:, :], -0.5)
            g.memset(attT_bd[:, :, :, :], 0.0)
            g.memset(zeros[:, :], 0.0).then_inc(zeros_ready, 1)
            for e in range(E):
                g.memset(expert_from[:, e:e + 1], float(E - e))
                g.memset(region[:, e:e + 1], float(e * REGION))
                g.memset(region_no[:, e:e + 1], float(e * REGION // P))
            g.memset(before[:, :], 1.0)
            g.memset(ones_sq[:, :], 1.0)
            g.memset(past[:, :, 1:E + 1], 0.0)
            g.memset(past[:, :, 0:1], 1.0)
            g.memset(up_to[:, :, :], 1.0)
            g.iota(token_no[:, :], pattern=[[P, T]], base=0, channel_multiplier=1)
            g.iota(block_i[:, :], pattern=[[1, NB]], base=0, channel_multiplier=0)
            step(g.memset(head_mask[:, :], 1.0))
            step(g.affine_select(out=head_mask[:, :], in_=head_mask[:, :], compare_op=ALU.is_ge, fill=0.0,
                                 base=0, pattern=[[-HD, HH]], channel_multiplier=1))
            g.affine_select(out=ident[:, :], in_=ident[:, :], compare_op=ALU.not_equal, fill=1.0,
                            base=0, pattern=[[-1, P]], channel_multiplier=1)
            g.affine_select(out=before[:, :], in_=before[:, :], compare_op=ALU.is_gt, fill=0.0,
                            base=0, pattern=[[1, P]], channel_multiplier=-1)
            g.affine_select(out=up_to[:, :, :], in_=up_to[:, :, :], compare_op=ALU.is_ge, fill=0.0,
                            base=0, pattern=[[1, E], [-1, E]], channel_multiplier=0)
            g.affine_select(out=head_mask[:, :], in_=head_mask[:, :], compare_op=ALU.is_ge, fill=0.0,
                            base=HD - 1, pattern=[[HD, HH]], channel_multiplier=-1).then_inc(consts_ready, 1)
            pool.wait_ge(var0_ready, 1)
            step(g.tensor_scalar(rstd0[:, :], mv0[:, :, 1], LN_EPS, None, ALU.add))
            g.tensor_tensor(rstd0[:, :], rstd0[:, :], neg_half[:, :], ALU.pow).then_inc(rstd0_ready, 1)
            pool.wait_ge(xn0_ready, T)
            pool.wait_ge(small_in, 16 * 4)
            g.tensor_tensor(x_all[:, :, :], x_all[:, :, :],
                            bo_b[:, :].unsqueeze(1).to_broadcast([P, T, D]), ALU.add).then_inc(xb_ready, 1)

            def prepare_batch(t, j):
                i = j % 2
                b = t * BT + j
                if not isinstance(t, int) or b >= 2:
                    pool.wait_ge(o_ps, b - 1)
                g.tensor_tensor(
                    q_bd[i][:, :, :, :],
                    qT[:, :, bass.ds(b * S, S)].unsqueeze(2).to_broadcast([P, DC, HH, S]),
                    head_mask[:, :].unsqueeze(1).unsqueeze(3).to_broadcast([P, DC, HH, S]), ALU.mult)
                g.tensor_copy(kT[i][:, :, KM:K], k_tail[:, :, bass.ds(b, 1)]).then_inc(batch_ready, 1)

            def gather(n):
                pool.wait_ge(get_ready, n + 1)
                settle(pool)
                g.indirect_dma_start(
                    out=xg, out_offset=None, in_=expert_x,
                    in_offset=bass.IndirectOffsetOnAxis(ap=get_i[:, 0:1], axis=0)).then_inc(rows_in, 16)

            def add(n):
                pool.wait_ge(add_ready, n + 1)
                settle(pool)
                g.indirect_dma_start(
                    out=out, out_offset=bass.IndirectOffsetOnAxis(ap=add_i[:, 0:1], axis=0),
                    in_=y_rows, in_offset=None, compute_op=ALU.add).then_inc(rows_added, 16)

            pool.wait_ge(q0_evac, 2 * NCH)
            pool.wait_ge(tails_evac, 2)

            def body(t, cross, attend, close):
                before_last, last = (isinstance(t, int) and t == n for n in (T, T + 1))
                if cross:
                    prepare_batch(t, 0)
                if close:
                    pool.wait_ge(p1_fac_ready, t - 1)
                    step(g.tensor_tensor(s1[:, :, :], s1[:, :, :],
                                         p1_fac[:, :].unsqueeze(2).to_broadcast([P, H, S]), ALU.mult))
                    p1_v = s1[:, :, :].rearrange("p (h i) k -> p h i k", i=2)
                    g.tensor_tensor(att[:, :, :], p1_v[:, :, 0, :], p1_v[:, :, 1, :], ALU.add).then_inc(att_ready, 1)
                if last:
                    gather(2)
                    add(0)
                    gather(3)
                if cross:
                    prepare_batch(t, 1)
                if close:
                    pool.wait_ge(ms_ready, t - 1)
                    step(g.tensor_tensor(rms[:, :], ms[:, :], neg_half[:, 0:1], ALU.pow))
                    settle(pool)
                    g.tensor_scalar(rms[:, :], rms[:, :], one_m_dw[:, 0:1], None, ALU.mult).then_inc(rms_ready, 1)
                    pool.wait_ge(var2_ready, t - 1)
                    settle(pool)
                    step(g.tensor_scalar(rstd2[:, :], mv2[:, 1:2], LN_EPS, None, ALU.add))
                    g.tensor_tensor(rstd2[:, :], rstd2[:, :], neg_half[:, 0:1], ALU.pow).then_inc(rstd2_ready, 1)
                if cross:
                    prepare_batch(t, 2)
                if attend:
                    pool.wait_ge(var1_ready, t)
                    settle(pool)
                    step(g.tensor_scalar(rstd[:, :], mv[:, 1:2], LN_EPS, None, ALU.add))
                    g.tensor_tensor(rstd[:, :], rstd[:, :], neg_half[:, 0:1], ALU.pow).then_inc(rstd1_ready, 1)
                if attend:
                    pool.wait_ge(qk1_evac, t)
                    q4 = qk1[:, 0, :, :].rearrange("p c (b q) -> p c b q", b=BT)
                    for c in range(1 if before_last else DC):
                        ins = g.tensor_tensor(
                            q1_bd[:, c, :, :, :],
                            q4[:, c, :, :].unsqueeze(2).to_broadcast([P, BT, HH, S]),
                            head_mask[:, :].unsqueeze(1).unsqueeze(3).to_broadcast([P, BT, HH, S]), ALU.mult)
                    ins.then_inc(q1_bd_ready, 1)
                if cross:
                    prepare_batch(t, 3)
                if close:
                    if before_last:
                        pool.wait_ge(pads_in, 32 * (1 + T - TA))
                        pool.wait_ge(xn2_stored, 16 * TA)
                        gather(0)
                        pool.wait_ge(y0_stored, 16 * TA)
                    if last:
                        add(1)
                        gather(4)
                    pool.wait_ge(slots_ready, t - 1)
                    settle(pool)
                    for r in range(TOPK):
                        g.indirect_dma_start(
                            out=slots, out_offset=bass.IndirectOffsetOnAxis(ap=slot_u[:, r:r + 1], axis=0),
                            in_=entry_i[:, r, :], in_offset=None
                            ).then_inc(last_slots_stored if before_last or last else slots_stored, 16)
                    if before_last:
                        gather(1)
                    if last:
                        add(2)

            pool.wait_ge(empty_in, 16)
            tile_loop(pool, step, POOL_STEPS, body)

            pool.wait_ge(last_xn2_stored, 16 * (T - TA))
            pool.wait_ge(last_y0_stored, 16 * (T - TA))
            with pool.Fori(NA, NB) as n:
                gather(n)
                add(n - 2)
            add(NB - 2)
            add(NB - 1)

        @block.tensor
        def _(pe):
            step = Steps(pe, None)
            mm = nc.tensor.matmul
            pe.wait_ge(consts_ready, 1)
            pe.wait_ge(valid_diag_ready, 1)
            mm(bank[7][:, 0:S], ones_rows[:, :], valid_diag[:, :], start=True, stop=True).then_inc(valid_ps, 1)
            for t in range(T):
                pe.wait_ge(xn0_ready, t + 1)
                for c in range(DC):
                    ins = nc.tensor.transpose(bank[t // 2][:, ((t % 2) * DC + c) * P:((t % 2) * DC + c + 1) * P],
                                              xn_all[:, t, c * P:(c + 1) * P], ident[:, :])
                ins.then_inc(xT0_ps, 1)
            pe.wait_ge(wq_in, 16)
            for n in range(NCH):
                pe.wait_ge(xT0_evac, 2 * (n + 1))
                if n == NCH - 1:
                    pe.wait_ge(q_factor_ready, 1)
                for oc in range(DC):
                    for c in range(DC):
                        ins = mm(bank[4 + 2 * n + oc][:, :], wq[:, c, oc * P:(oc + 1) * P],
                                 xnT_all[:, c, n * 512:(n + 1) * 512], start=(c == 0), stop=(c == DC - 1))
                    ins.then_inc(q0_ps, 1)
            pe.wait_ge(tail_in, 16 * G)
            pe.wait_ge(wkv_in, 32)
            for oc in range(DC):
                for c in range(DC):
                    ins = mm(bank[1][:, oc * B:(oc + 1) * B], wk[:, c, oc * P:(oc + 1) * P], ctx_tail[:, c, 0, :],
                             start=(c == 0), stop=(c == DC - 1))
            ins.then_inc(ktail_ps, 1)
            for c in range(DC):
                ins = mm(bank[2][:, 0:D], ctx_tail[:, c, :, :].rearrange("p g b -> p (g b)"), wv[:, c, :],
                         start=(c == 0), stop=(c == DC - 1))
            ins.then_inc(vtail_ps, 1)
            pe.wait_ge(tails_evac, 1)

            def first(t, n=0):
                return isinstance(t, int) and t <= n

            def project(t, j):
                b = t * BT + j
                pe.wait_ge(ctx_in[j], 16 * (t + 1))
                if not first(b):
                    pe.wait_ge(k_evac, b)
                for oc in range(DC):
                    for c in range(DC):
                        ins = mm(bank[0][:, oc * KM:(oc + 1) * KM], wk[:, c, oc * P:(oc + 1) * P], ctx_b[j][:, c, :],
                                 start=(c == 0), stop=(c == DC - 1))
                ins.then_inc(k_ps, 1)
                if not first(b):
                    pe.wait_ge(v_evac, b)
                if not first(t, 2) or (t == 2 and j > 0):
                    free, count = ((y0_ready, t - 2), (o1_evac, 2 * (t - 1)), (var2_ready, t - 1),
                                   (lg_evac, t - 1))[j]
                    pe.wait_ge(free, count)
                for kt in range(KT):
                    for c in range(DC):
                        ins = mm(bank[1][:, kt * D:(kt + 1) * D], ctx_b[j][:, c, kt * P:(kt + 1) * P], wv[:, c, :],
                                 start=(c == 0), stop=(c == DC - 1))
                ins.then_inc(v_ps, 1)

            def scores(t, j, c):
                b = t * BT + j
                i = j % 2
                if first(b):
                    pe.wait_ge(tails_evac, 2)
                if c == 0:
                    pe.wait_ge(k_evac, b + 1)
                    pe.wait_ge(batch_ready, b + 1)
                for g in (2 * c, 2 * c + 1):
                    if not (isinstance(b, int) and b == 0 and g < 2):
                        pe.wait_ge(s_masked, 4 * b + g - 1)
                    mm(bank[2 + g % 2][:, 0:K],
                       q_bd[i][:, c, (g % 2) * GH:(g % 2 + 1) * GH, :].rearrange("p h q -> p (h q)"),
                       kT[i][:, c, :], start=True, stop=True).then_inc(s_ps, 1)

            def turn(t, j, c):
                b = t * BT + j
                pe.wait_ge(p_normed, 4 * b + 2 * c + 2)
                if first(b):
                    pe.wait_ge(q0_evac, 2 * NCH)
                if c == 1:
                    if not first(b):
                        pe.wait_ge(o_evac, b)
                    nc.tensor.transpose(bank[6][0:G, P:2 * P], p_n[j % 2][:, :, KM:K].squeeze(2),
                                        ident[:, :]).then_inc(end_ps, 1)
                if not first(b):
                    pe.wait_ge(pT0_evac if c == 0 else pT1_evac, b)
                for kt in range(KT):
                    for g in range(2):
                        ins = nc.tensor.transpose(bank[4 + c][:, kt * 2 * P + g * P:kt * 2 * P + (g + 1) * P],
                                                  p_n[j % 2][:, 2 * c + g, kt * P:(kt + 1) * P], ident[:, :])
                ins.then_inc(pT_ps, 1)

            def weigh(t, j):
                b = t * BT + j
                pe.wait_ge(v_evac, b + 1)
                pe.wait_ge(pT0_evac, b + 1)
                pe.wait_ge(end_evac, b + 1)
                pe.wait_ge(vend_in[j], 16 * (t + 1))
                for c in range(DC):
                    if c == 1:
                        pe.wait_ge(pT1_evac, b + 1)
                        settle(pe)
                    for kt in range(KT + 1):
                        for r in range(4):
                            o = bank[6][32 * r:32 * r + 32, c * 64:(c + 1) * 64]
                            d0 = c * P + 32 * r
                            if kt < KT:
                                ins = mm(o, v[j % 2][:, kt, d0:d0 + 32], pT[c][:, kt, 64 * r:64 * r + 64],
                                         start=(kt == 0), stop=False)
                            else:
                                ins = mm(o, v_end[j][:, d0:d0 + 32], p_end[:, (64 * r) % P:(64 * r) % P + 64],
                                         start=False, stop=True)
                ins.then_inc(o_ps, 1)

            misc = bank[7]

            def place(t):
                return {T: bank[6], T + 1: bank[7]}.get(t, bank[1]) if isinstance(t, int) else bank[1]

            def count_choices(to):
                mm(to[:, 0:E], ones_sq[:, :], chosen_sum[:, :], start=True, stop=True).then_inc(count_ps, 1)

            def block_rows(n):
                pe.wait_ge(rows_in, 16 * (n + 1))
                if not first(n):
                    pe.wait_ge(xgT_evac, n)
                for c in range(DC):
                    ins = nc.tensor.transpose(bank[5][:, c * P:(c + 1) * P], xg[:, c * P:(c + 1) * P], ident[:, :])
                ins.then_inc(xgT_ps, 1)

            def block_down(n):
                w = pe.value_load(table[0:1, 1, bass.ds(n, 1)], min_val=0, max_val=(E - 1) * EW)
                pe.wait_ge(h_ready, n + 1)
                if not first(n):
                    pe.wait_ge(add_ready, n)
                for f in range(FT):
                    ins = mm(bank[4][:, 0:D], hT[:, f, :], arena[:, bass.ds(w + 2 * DC * F + f * D, D)],
                             start=(f == 0), stop=(f == FT - 1))
                ins.then_inc(down_ps, 1)

            def block_up(n):
                w = pe.value_load(table[0:1, 1, bass.ds(n, 1)], min_val=0, max_val=(E - 1) * EW)
                pe.wait_ge(xgT_evac, n + 1)
                for k, (bk, ready, free) in enumerate(((bank[0], gate_ps, gate_evac), (bank[1], up_ps, up_evac))):
                    if not first(n):
                        pe.wait_ge(free, n)
                    for c in range(DC):
                        ins = mm(bk[:, :], xgT[:, c, :], arena[:, bass.ds(w + (k * DC + c) * F, F)],
                                 start=(c == 0), stop=(c == DC - 1))
                    ins.then_inc(ready, 1)

            def block_turn(n, follow=True):
                if not first(n):
                    block_down(n - 1)
                if follow:
                    block_rows(n + 1)
                for bk, rows, ready, free, done in ((bank[2], g_rows, gate_evac, silu_done, gT_ps),
                                                    (bank[3], u_rows, up_evac, h_ready, uT_ps)):
                    pe.wait_ge(ready, n + 1)
                    if not first(n):
                        pe.wait_ge(free, n)
                    for f in range(FT):
                        ins = nc.tensor.transpose(bk[:, f * P:(f + 1) * P], rows[:, f * P:(f + 1) * P], ident[:, :])
                    ins.then_inc(done, 1)

            def block(n, follow=True):
                block_up(n)
                block_turn(n, follow)

            def close_weigh(t):
                aside = place(t)
                if not first(t, 2):
                    pe.wait_ge(y0_ready, t - 2)
                pe.wait_ge(attT_ready, t - 1)
                for h in range(H // 2):
                    r, c = h % 4, h // 4
                    ins = mm(aside[32 * r:32 * r + 32, c * P:(c + 1) * P], v1[:, 32 * h:32 * h + 32],
                             attT_bd[:, h, :, :].rearrange("p b q -> p (b q)"), start=True, stop=True)
                ins.then_inc(o1_ps, 1)

            def close_project(t):
                aside = place(t)
                pe.wait_ge(o1_evac, 2 * (t - 1))
                for c in range(DC):
                    mm(aside[:, 0:D], o1T[:, c, :], so[:, c, :], start=(c == 0), stop=(c == DC - 1))
                for c in range(DC):
                    ins = mm(aside[:, D:D + 1], o1_sq[:, c, :], ones_col[:, :], start=(c == 0), stop=(c == DC - 1))
                ins.then_inc(y1_ps, 1)

            def turn_rows(to, rows, ready, count, done):
                pe.wait_ge(ready, count)
                for c in range(DC):
                    ins = nc.tensor.transpose(to[:, c * P:(c + 1) * P], rows[:, c * P:(c + 1) * P], ident[:, :])
                ins.then_inc(done, 1)

            def close_route(t):
                aside = place(t)
                pe.wait_ge(x2T_evac, t - 1)
                for c in range(DC):
                    ins = mm(aside[:, 0:E], xn2T[:, c, :], wr[:, c, :], start=(c == 0), stop=(c == DC - 1))
                ins.then_inc(lg_ps, 1)

            def close_rank(t):
                aside = place(t)
                pe.wait_ge(chosen_ready, t - 1)
                pe.wait_ge(gates_ready, t - 1)
                if not first(t, 2):
                    pe.wait_ge(slots_ready, t - 2)
                mm(aside[:, 0:E], before[:, :], chosen[:, :], start=True, stop=False)
                mm(aside[:, 0:E], ones_sq[:, :], chosen_sum[:, :], start=False, stop=True)
                nc.tensor.transpose(aside[0:E, P:2 * P], gates[:, :], ident[:, :]).then_inc(rank_ps, 1)

            def close_seed(t):
                aside = place(t)
                pe.wait_ge(gT_ready, t - 1)
                mm(aside[:, 0:D], gatesT[:, :], bd_r[:, :], start=True, stop=True).then_inc(seed_ps, 1)

            def attend_project(t):
                if first(t, 1):
                    pe.wait_ge(wo_in, 16)
                pe.wait_ge(o_evac, BT * t)
                if not first(t, 1):
                    pe.wait_ge(s1_ready, t - 1)
                for c in range(DC):
                    ins = mm(misc[:, 0:D], oT[:, c, :], wo[:, c, :], start=(c == 0), stop=(c == DC - 1))
                ins.then_inc(y_ps, 1)

            def attend_qk(t):
                if first(t, 1):
                    pe.wait_ge(self_in, 16 * 8)
                pe.wait_ge(x1T_evac, t)
                for n, w in enumerate((sq, sk)):
                    for oc in range(DC):
                        for c in range(DC):
                            ins = mm(misc[:, (n * DC + oc) * P:(n * DC + oc + 1) * P],
                                     w[:, c, oc * P:(oc + 1) * P], xn1T[:, c, :], start=(c == 0), stop=(c == DC - 1))
                ins.then_inc(qk1_ps, 1)

            def attend_v(t):
                pe.wait_ge(qk1_evac, t)
                for c in range(DC):
                    ins = mm(misc[:, 0:D], xn1T[:, c, :], sv[:, c, :], start=(c == 0), stop=(c == DC - 1))
                ins.then_inc(v1_ps, 1)

            def attend_scores(t):
                pe.wait_ge(v1_evac, t)
                pe.wait_ge(q1_bd_ready, t)
                if isinstance(t, int) and t == T:
                    pe.wait_ge(q1_bd_half_ready, 1)
                for c in range(DC):
                    for b in range(BT):
                        ins = mm(misc[32 * b:32 * b + 32, c * 256:(c + 1) * 256], qk1[:, 1, c, b * S:(b + 1) * S],
                                 q1_bd[:, c, b, :, :].rearrange("p h q -> p (h q)"), start=True, stop=True)
                ins.then_inc(s1_ps, 1)

            def body(t, cross, attend, close):
                before_last, last = (isinstance(t, int) and t == n for n in (T, T + 1))
                for j in range(BT):
                    pt, pj = (t, j - 1) if j else (t - 1, BT - 1)
                    has_prev = cross if j else (not first(t) and (cross or attend))
                    if cross:
                        project(t, j)
                    if j == 3 and attend:
                        attend_scores(t)
                    if has_prev:
                        turn(pt, pj, 0)
                    if cross:
                        scores(t, j, 0)
                    if before_last and j == 0:
                        pe.wait_ge(slots_ready, TA)
                        pe.wait_ge(k_evac, B)
                        count_choices(bank[0])
                    if cross and close:
                        pe.wait_ge(v_evac, t * BT + j + 1)
                    if j == 1 and close:
                        close_project(t)
                    if j == 3 and close:
                        close_rank(t)
                    if j == 2 and attend:
                        turn_rows(misc, xn1, xn1_ready, t, x1T_ps)
                    if j == 2 and close:
                        turn_rows(place(t), xn2, xn2_ready, t - 1, x2T_ps)
                    if has_prev:
                        turn(pt, pj, 1)
                    if j == 2 and attend:
                        attend_qk(t)
                    if cross:
                        scores(t, j, 1)
                    if j == 1 and attend:
                        attend_project(t)
                    if last and j == 2:
                        block_up(3)
                    if j == 2 and close:
                        close_route(t)
                    if last and j == 2:
                        block_turn(3)
                    if j == 2 and attend:
                        attend_v(t)
                    if has_prev:
                        weigh(pt, pj)
                    if before_last and j == 0:
                        pe.wait_ge(o_evac, B)
                    if j == 0 and close:
                        close_weigh(t)
                    if j == 3 and close:
                        close_seed(t)
                    if before_last and j == 3:
                        pe.wait_ge(table_ready, 1)
                        pe.wait_ge(experts_in, 48 * (E - LATE))
                        pe.wait_ge(late_in, 48 * LATE)
                        block_rows(0)
                        block(0)
                        block(1)
                    if last and j == 1:
                        block(2)

            tile_loop(pe, step, 0, body)

            pe.wait_ge(slots_ready, T)
            count_choices(bank[6])
            block_up(BT)
            block_turn(BT, follow=False)
            block_rows(BT + 1)
            pe.wait_ge(table_ready, 2)
            with pe.Fori(BT + 1, NB - 1) as n:
                block(n)
            block(NB - 1, follow=False)
            block_down(NB - 1)

        @block.scalar
        def _(act):
            a = nc.scalar
            for i in range(T // 2):
                act.wait_ge(xT0_ps, 2 * i + 2)
                a.copy(xnT_all[:, :, 2 * i * P:(2 * i + 2) * P].rearrange("p c (t k) -> p t c k", t=2),
                       bank[i][:, :].rearrange("p (t c k) -> p t c k", t=2, c=DC)).then_inc(xT0_evac, 1)
            act.wait_ge(small_in, 16 * 4)

            def block_rows(n):
                act.wait_ge(xgT_ps, n + 1)
                a.copy(xgT, bank[5][:, 0:D].rearrange("p (c k) -> p c k", c=DC)).then_inc(xgT_evac, 1)

            def block_gate(n, follow=True):
                act.wait_ge(gate_ps, n + 1)
                a.copy(g_rows, bank[0][:, :]).then_inc(gate_evac, 1)
                if follow:
                    block_rows(n + 1)

            def block_silu(n):
                e = act.value_load(table[0:1, 0, bass.ds(n, 1)], min_val=0, max_val=E - 1)
                act.wait_ge(gT_ps, n + 1)
                if not (isinstance(n, int) and n == 0):
                    act.wait_ge(h_ready, n)
                settle(act)
                for f in range(FT):
                    ins = a.activation(silu[:, f, :], bank[2][:, f * P:(f + 1) * P], ACT.Silu,
                                       bias=bg_c[:, bass.ds(e, 1), f:f + 1].squeeze(2))
                ins.then_inc(silu_done, 1)

            def block(n, follow=True):
                block_gate(n, follow)
                block_silu(n)

            def body(t, cross, attend, close):
                misc = bank[7]
                before_last, last = (isinstance(t, int) and t == n for n in (T, T + 1))
                turned, aside = (bk[:, 0:D].rearrange("p (c k) -> p c k", c=DC) for bk in (
                    misc, bank[6] if before_last else misc if last else bank[1]))
                for j in range(BT):
                    b = t * BT + j
                    i = j % 2
                    has_prev = cross if j else (not (isinstance(t, int) and t <= 0) and (cross or attend))
                    if cross:
                        act.wait_ge(k_ps, b + 1)
                        for oc in range(DC):
                            ins = a.activation(kT[i][:, oc, 0:KM], bank[0][:, oc * KM:(oc + 1) * KM], ACT.Identity,
                                               bias=cols[:, 1, oc:oc + 1])
                        ins.then_inc(k_evac, 1)
                    if j == 3 and close:
                        act.wait_ge(lg_centred, t - 1)
                        a.activation(lg_e[:, :], lg_c[:, :], ACT.Exp, accum_out=lg_sum[:, :]).then_inc(lg_exp, 1)
                    if cross:
                        act.wait_ge(v_ps, b + 1)
                        a.copy(v[i][:, :, :], bank[1][:, :].rearrange("p (k d) -> p k d", k=KT)).then_inc(v_evac, 1)
                    if has_prev:
                        act.wait_ge(pT_ps, 2 * b - 1)
                        a.copy(pT[0][:, :, :], bank[4][:, :].rearrange("p (k n) -> p k n", k=KT)).then_inc(pT0_evac, 1)
                    if j == 2 and attend:
                        act.wait_ge(x1T_ps, t)
                        a.copy(xn1T[:, :, :], turned).then_inc(x1T_evac, 1)
                    for g in range(G):
                        if cross:
                            act.wait_ge(s_masked, 4 * b + g + 1)
                            if not (isinstance(b, int) and b == 0):
                                act.wait_ge(p_normed, 4 * (b - 1) + g + 1)
                            a.activation(p_exp[g][:, :], s_m[g][:, :], ACT.Exp, bias=s_min[:, g:g + 1], scale=-1.0,
                                         accum_out=p_sum[:, g:g + 1]).then_inc(exp_done, 1)
                        if g == 1 and j == 2 and close:
                            act.wait_ge(x2T_ps, t - 1)
                            a.copy(xn2T[:, :, :], aside).then_inc(x2T_evac, 1)
                        if g == 1 and j == 2 and attend:
                            act.wait_ge(qk1_ps, t)
                            a.activation(qk1[:, :, :, :], misc[:, :].rearrange("p (n c k) -> p n c k", n=2, c=DC),
                                         ACT.Copy, scale=QSCALE ** 0.5).then_inc(qk1_evac, 1)
                        if g == 3 and j == 3 and before_last:
                            block_rows(0)
                        if g == 3 and j == 3 and attend:
                            act.wait_ge(s1_ready, t)
                            a.activation(s1[:, :, :], s1[:, :, :], ACT.Exp).then_inc(exp1_done, 1)
                        if g == 1 and j == 0 and close:
                            act.wait_ge(o1_ps, t - 1)
                            a.copy(o1T[:, :, :], aside).then_inc(o1_evac, 1)
                            a.activation(o1_sq[:, :, :], aside, ACT.Square).then_inc(o1_evac, 1)
                        if g == 3 and j == 2 and attend:
                            act.wait_ge(v1_ps, t)
                            a.copy(v1[:, :], misc[:, 0:D]).then_inc(v1_evac, 1)
                    if before_last and j == 3:
                        act.wait_ge(table_ready, 1)
                        block(0)
                        block(1)
                    if last and j == 1:
                        block(2)
                    if last and j == 2:
                        block_gate(3, follow=False)
                    if last and j == 3:
                        block_rows(4)
                        block_silu(3)

            tile_loop(act, Steps(act, act_steps), 0, body)

            block_gate(BT, follow=False)
            block_silu(BT)
            block_rows(BT + 1)
            act.wait_ge(table_ready, 2)
            with act.Fori(BT + 1, NB - 1) as n:
                block(n)
            block(NB - 1, follow=False)

        @block.vector
        def _(dve):
            step = Steps(dve, dve_steps)
            w = nc.vector
            dve.wait_ge(consts_ready, 1)
            dve.wait_ge(x_in, 16)
            for t in range(T):
                w.bn_stats(stats0[:, t, :], x_all[:, t, :])
            step(w.memset(chosen_sum[:, :], 0.0))
            w.tensor_copy(block_no[:, :], block_i[:, :])
            for t in range(T):
                ins = w.bn_aggr(mv0[:, t, :], stats0[:, t, :])
            ins.then_inc(var0_ready, 1)
            step(w.memset(group_mask[:, :], 0.0))
            for i in range(G):
                ins = w.memset(group_mask[i * B:(i + 1) * B, i * (D // G):(i + 1) * (D // G)], 1.0)
            step(ins)
            dve.wait_ge(mask_in, 16 * GH)
            step(w.tensor_scalar(masked[:, :], mask_i[:, :], 0.0, 1.0, ALU.is_equal, ALU.mult))
            w.tensor_scalar(mask_add[:, :], masked[:, :], MASKED, None, ALU.mult)
            step(w.tensor_reduce(all_masked[:, :], masked[:, :], AX.X, ALU.min))
            step(w.tensor_scalar(row_valid[:, :], all_masked[:, :], -1.0, 1.0, ALU.mult, ALU.add))
            dve.wait_ge(consts_ready, 1)
            w.tensor_scalar(valid_diag[:, :], ident[0:S, 0:S], row_valid[0:S, 0:1], None, ALU.mult
                            ).then_inc(valid_diag_ready, 1)
            dve.wait_ge(rstd0_ready, 1)
            for t in range(T):
                w.tensor_scalar(xn_all[:, t, :], x_all[:, t, :], mv0[:, t, 0:1], rstd0[:, t:t + 1],
                                ALU.subtract, ALU.mult).then_inc(xn0_ready, 1)
            dve.wait_ge(valid_ps, 1)
            w.tensor_scalar(q_factor[:, :], bank[7][:, 0:S], -QSCALE, None, ALU.mult).then_inc(q_factor_ready, 1)
            dve.wait_ge(q_factor_ready, 1)
            dve.wait_ge(small_in, 16 * 4)
            for n in range(NCH):
                for oc in range(DC):
                    dve.wait_ge(q0_ps, 2 * n + oc + 1)
                    w.scalar_tensor_tensor(
                        qT[:, oc, n * 512:(n + 1) * 512].rearrange("p (b q) -> p b q", q=S),
                        bank[4 + 2 * n + oc][:, :].rearrange("p (b q) -> p b q", q=S), cols[:, 0, oc:oc + 1],
                        q_factor[:, :].unsqueeze(1).to_broadcast([P, 512 // S, S]), ALU.add, ALU.mult
                        ).then_inc(q0_evac, 1)
            dve.wait_ge(ktail_ps, 1)
            for oc in range(DC):
                ins = w.tensor_scalar(k_tail[:, oc, :], bank[1][:, oc * B:(oc + 1) * B], cols[:, 1, oc:oc + 1], None,
                                      ALU.add)
            ins.then_inc(tails_evac, 1)
            dve.wait_ge(vtail_ps, 1)
            w.tensor_tensor(v_tail_m[:, :], bank[2][:, 0:D], group_mask[:, :], ALU.mult).then_inc(tails_evac, 1)
            w.tensor_reduce(parity[:, :], head_mask[:, :].rearrange("p (a b) -> p b a", b=2), AX.X, ALU.add)
            w.memset(sign[:, 0:1], 1.0)
            w.tensor_scalar(sign[:, 1:2], dw[:, :], -1.0, None, ALU.mult)
            step(w.tensor_scalar(one_m_dw[:, :], dw[:, :], -1.0, 1.0, ALU.mult, ALU.add))
            w.tensor_scalar(sbo_s[:, :], sbo_b[:, :], one_m_dw[:, 0:1], None, ALU.mult)
            dve.wait_ge(self_in, 16 * 8)
            for c in range(DC):
                ins = w.tensor_scalar(so[:, c, :], so[:, c, :], cols[:, 3, c:c + 1], None, ALU.mult)
            step(ins)

            def mask_scores(t, j, g):
                b = t * BT + j
                dve.wait_ge(s_ps, 4 * b + g + 1)
                if not (isinstance(b, int) and b == 0):
                    dve.wait_ge(exp_done, 4 * (b - 1) + g + 1)
                settle(dve)
                w.tensor_tensor_reduce(out=s_m[g][:, :], in0=bank[2 + g % 2][:, 0:K], in1=mask_add[:, :], scale=1.0,
                                       scalar=BIG, op0=ALU.add, op1=ALU.min, accum_out=s_min[:, g:g + 1]
                                       ).then_inc(s_masked, 1)

            def normalise(t, j, c):
                b = t * BT + j
                dve.wait_ge(exp_done, 4 * b + 2 * c + 2)
                step(w.reciprocal(p_inv[:, 2 * c:2 * c + 2], p_sum[:, 2 * c:2 * c + 2]))
                for g in (2 * c, 2 * c + 1):
                    w.tensor_scalar(p_n[j % 2][:, g, :], p_exp[g][:, :], p_inv[:, g:g + 1], None, ALU.mult
                                    ).then_inc(p_normed, 1)

            def norm_stats(x_ap, st, m, ready):
                settle(dve)
                step(w.bn_stats(st[:, :], x_ap))
                settle(dve)
                w.bn_aggr(m[:, :], st[:, :]).then_inc(ready, 1)

            def make_table(first, after):
                blocks = after - first
                step(w.tensor_tensor(nblocks_t[:, :, :], nblocks[:, :].unsqueeze(1).to_broadcast([P, E, E]),
                                     up_to[:, :, :], ALU.mult))
                step(w.tensor_reduce(ends[:, :], nblocks_t[:, :, :], AX.X, ALU.add))
                step(w.tensor_tensor(base[:, :], nblocks[:, :], ends[:, :], ALU.subtract))
                step(w.tensor_tensor(base[:, :], base[:, :], region_no[:, :], ALU.add))
                if first:
                    step(w.tensor_tensor(base[:, :], base[:, :], early[:, :], ALU.add))
                step(w.tensor_tensor(past[:, 0:blocks, 1:E], ends[:, 0:E - 1].unsqueeze(1).to_broadcast([P, blocks, E - 1]),
                                     block_no[:, 0:blocks].unsqueeze(2).to_broadcast([P, blocks, E - 1]), ALU.is_le))
                step(w.tensor_reduce(b_expert[:, 0:blocks], past[:, 0:blocks, 1:E], AX.X, ALU.add))
                step(w.tensor_tensor(of_expert[:, 0:blocks, :], past[:, 0:blocks, 0:E], past[:, 0:blocks, 1:E + 1],
                                     ALU.subtract))
                step(w.tensor_tensor(of_expert[:, 0:blocks, :], of_expert[:, 0:blocks, :],
                                     base[:, :].unsqueeze(1).to_broadcast([P, blocks, E]), ALU.mult))
                step(w.tensor_reduce(b_base[:, 0:blocks], of_expert[:, 0:blocks, :], AX.X, ALU.add))
                step(w.tensor_tensor(b_first[:, 0:blocks], b_base[:, 0:blocks], block_no[:, 0:blocks], ALU.add))
                w.tensor_copy(table[:, 0, first:after], b_expert[:, 0:blocks])
                w.tensor_scalar(table[:, 1, first:after], b_expert[:, 0:blocks], float(-EW), float((E - 1) * EW),
                                ALU.mult, ALU.add)
                w.tensor_scalar(table[:, 2, first:after], b_first[:, 0:blocks], float(P), None, ALU.mult
                                ).then_inc(table_ready, 1)

            def count_blocks(bk, less_than_a_block):
                step(w.tensor_scalar(count_i[:, :], bk[:, 0:E], float(less_than_a_block), None, ALU.add))
                step(w.tensor_scalar(nblocks_i[:, :], count_i[:, :], P.bit_length() - 1, None, ALU.logical_shift_right))
                step(w.tensor_copy(nblocks[:, :], nblocks_i[:, :]))

            def early_table():
                dve.wait_ge(count_ps, 1)
                count_blocks(bank[0], 0)
                make_table(0, NA)
                step(w.tensor_tensor(early[:, :], nblocks[:, :], ends[:, :], ALU.subtract))
                step(w.tensor_scalar(early[:, :], early[:, :], float(NA), 0.0, ALU.add, ALU.max))
                step(w.tensor_tensor(early[:, :], early[:, :], nblocks[:, :], ALU.min))

            def late_table():
                dve.wait_ge(count_ps, 2)
                count_blocks(bank[6], P - 1)
                step(w.tensor_tensor(nblocks[:, :], nblocks[:, :], early[:, :], ALU.subtract))
                make_table(NA, NB)

            def get(n):
                if not (isinstance(n, int) and n == 0):
                    dve.wait_ge(xgT_ps, n)
                dve.wait_ge(ids_in, 16 * (n + 1))
                w.tensor_copy(get_i[:, :], ids_i[:, bass.ds(n, 1), 0]).then_inc(get_ready, 1)

            def weigh(n):
                dve.wait_ge(down_ps, n + 1)
                if not (isinstance(n, int) and n == 0):
                    dve.wait_ge(rows_added, 16 * n)
                w.tensor_copy(add_i[:, :], ids_i[:, bass.ds(n, 1), 0])
                w.tensor_scalar(y_rows, bank[4][:, 0:D], ids[:, bass.ds(n, 1), 1:2].squeeze(1), None, ALU.mult
                                ).then_inc(add_ready, 1)

            def block_up(n):
                dve.wait_ge(up_ps, n + 1)
                w.tensor_copy(u_rows, bank[1][:, :]).then_inc(up_evac, 1)

            def block_hidden(n, follow=True):
                if not (isinstance(n, int) and n == 0):
                    weigh(n - 1)
                if follow:
                    get(n + 2)
                e = dve.value_load(table[0:1, 0, bass.ds(n, 1)], min_val=0, max_val=E - 1)
                dve.wait_ge(uT_ps, n + 1)
                dve.wait_ge(silu_done, n + 1)
                for f in range(FT):
                    ins = w.scalar_tensor_tensor(hT[:, f, :], bank[3][:, f * P:(f + 1) * P],
                                                 bu_c[:, bass.ds(e, 1), f:f + 1].squeeze(2), silu[:, f, :],
                                                 ALU.add, ALU.mult)
                ins.then_inc(h_ready, 1)

            def block(n, follow=True):
                block_up(n)
                block_hidden(n, follow)

            def body(t, cross, attend, close):
                misc = bank[7]
                before_last, last = (isinstance(t, int) and t == n for n in (T, T + 1))
                aside = bank[6] if before_last else misc if last else bank[1]
                for j in range(BT):
                    b = t * BT + j
                    pj = (j - 1) % BT
                    has_prev = cross if j else (not (isinstance(t, int) and t <= 0) and (cross or attend))
                    if j == 0 and close:
                        dve.wait_ge(exp1_done, t - 1)
                        step(w.tensor_reduce(p1_sum[:, :], s1[:, :, :], AX.X, ALU.add))
                        step(w.reciprocal(p1_inv[:, :], p1_sum[:, :]))
                        w.tensor_tensor(p1_fac[:, :].rearrange("p (h i) -> p h i", i=2),
                                        p1_inv[:, :].rearrange("p (h i) -> p h i", i=2),
                                        sign[:, :].unsqueeze(1).to_broadcast([P, H // 2, 2]), ALU.mult
                                        ).then_inc(p1_fac_ready, 1)
                        if last:
                            block(0)
                    if j == 3 and close:
                        dve.wait_ge(lg_exp, t - 1)
                        dve.wait_ge(chosen_ready, t - 1)
                        step(w.tensor_tensor_reduce(out=lg_m[:, :], in0=lg_e[:, :], in1=chosen[:, :], scale=1.0,
                                                    scalar=0.0, op0=ALU.mult, op1=ALU.add, accum_out=chosen_e[:, :]))
                        step(w.scalar_tensor_tensor(gate_den[:, :], lg_sum[:, :], 1e-9, chosen_e[:, :],
                                                    ALU.mult, ALU.add))
                        step(w.reciprocal(gate_inv[:, :], gate_den[:, :]))
                        w.tensor_scalar(gates[:, :], lg_m[:, :], gate_inv[:, 0:1], None, ALU.mult
                                        ).then_inc(gates_ready, 1)
                    if cross:
                        mask_scores(t, j, 0)
                        mask_scores(t, j, 1)
                    if has_prev:
                        dve.wait_ge(end_ps, b)
                        w.tensor_copy(p_end[:, :], bank[6][0:G, P:2 * P]).then_inc(end_evac, 1)
                        dve.wait_ge(pT_ps, 2 * b)
                        w.tensor_copy(pT[1][:, :, :], bank[5][:, :].rearrange("p (k n) -> p k n", k=KT)
                                      ).then_inc(pT1_evac, 1)
                    if j == 0 and close:
                        dve.wait_ge(att_ready, t - 1)
                        for q in range(BT):
                            ins = w.transpose(attT_bd[32 * q:32 * q + 32, :, q, :], att[32 * q:32 * q + 32, :, :])
                        ins.then_inc(attT_ready, 1)
                    if cross:
                        normalise(t, j, 0)
                    if j == 1 and close:
                        dve.wait_ge(y1_ps, t - 1)
                        w.tensor_scalar(ms[:, :], aside[:, D:D + 1], 1.0 / D, RMS_EPS, ALU.mult, ALU.add
                                        ).then_inc(ms_ready, 1)
                    if j == 3 and close:
                        dve.wait_ge(rank_ps, t - 1)
                        step(w.tensor_tensor(pos[:, :], aside[:, 0:E], region[:, :], ALU.add))
                        w.tensor_copy(gatesT[:, :], aside[0:E, P:2 * P]).then_inc(gT_ready, 1)
                    if cross:
                        mask_scores(t, j, 2)
                        mask_scores(t, j, 3)
                    if j == 3 and close:
                        dve.wait_ge(gates_ready, t - 1)
                        if last:
                            dve.wait_ge(last_slots_stored, 16 * TOPK)
                        elif not (isinstance(t, int) and t <= 2):
                            dve.wait_ge(slots_stored, 16 * TOPK * (t - 2))
                        for r in range(TOPK):
                            w.tensor_tensor_reduce(out=gate_hit[:, r, :], in0=gates[:, :], in1=hit[:, r, :], scale=1.0,
                                                   scalar=0.0, op0=ALU.mult, op1=ALU.add, accum_out=entry[:, r, 1:2])
                        for r in range(TOPK):
                            ins = w.tensor_tensor_reduce(out=pos_hit[:, r, :], in0=pos[:, :], in1=hit[:, r, :],
                                                         scale=1.0, scalar=0.0, op0=ALU.mult, op1=ALU.add,
                                                         accum_out=slot_f[:, r:r + 1])
                        step(ins)
                        w.tensor_copy(slot_u[:, :], slot_f[:, :])
                        w.tensor_copy(entry_i[:, :, 0], token_no[:, bass.ds(t - 2, 1)].to_broadcast([P, TOPK]))
                        w.tensor_tensor(chosen_sum[:, :], chosen_sum[:, :], chosen[:, :], ALU.add
                                        ).then_inc(slots_ready, 1)
                    if j == 1 and close:
                        dve.wait_ge(rms_ready, t - 1)
                        step(w.scalar_tensor_tensor(x2[:, :], aside[:, 0:D], rms[:, 0:1], x1b[:, :],
                                                    ALU.mult, ALU.add))
                        norm_stats(x2[:, :], stats2, mv2, var2_ready)
                    if j == 1 and attend:
                        dve.wait_ge(y_ps, t)
                        if isinstance(t, int) and t == 1:
                            dve.wait_ge(xb_ready, 1)
                        step(w.tensor_tensor(x1[:, :], misc[:, 0:D], x_all[:, bass.ds(t - 1, 1), :].squeeze(1),
                                             ALU.add))
                        w.tensor_tensor(x1b[:, :], x1[:, :], sbo_s[:, :], ALU.add)
                        norm_stats(x1[:, :], stats, mv, var1_ready)
                    if j == 3 and close:
                        dve.wait_ge(seed_ps, t - 1)
                        if last:
                            dve.wait_ge(last_y0_stored, 16)
                        elif not (isinstance(t, int) and t <= 2):
                            dve.wait_ge(y0_stored, 16 * (t - 2))
                        w.tensor_tensor(y0[:, :], aside[:, 0:D], x2[:, :], ALU.add).then_inc(y0_ready, 1)
                    if last and j == 3:
                        late_table()
                        block_hidden(3, follow=False)
                    if j == 3 and attend:
                        dve.wait_ge(s1_ps, t)
                        step(w.transpose(s1[:, :, :].rearrange("p h k -> p (h k)"), misc[:, :]))
                        step(w.tensor_reduce(s1_max[:, :], s1[:, :, :], AX.X, ALU.max))
                        w.tensor_tensor(s1[:, :, :], s1[:, :, :],
                                        s1_max[:, :].unsqueeze(2).to_broadcast([P, H, S]), ALU.subtract
                                        ).then_inc(s1_ready, 1)
                    if cross:
                        normalise(t, j, 1)
                    if last and j == 2:
                        block_up(3)
                    if j == 2 and close:
                        dve.wait_ge(lg_ps, t - 1)
                        w.tensor_copy(lg[:, :], aside[:, 0:E]).then_inc(lg_evac, 1)
                    if has_prev:
                        dve.wait_ge(o_ps, b)
                        o4 = bank[6][:, 0:P].rearrange("p (c a q) -> p c a q", c=DC, a=2)
                        for c in range(DC):
                            ins = w.tensor_scalar(o_even[:, c, :], o4[:, c, 0, :], parity[:, 0:1], cols[:, 2, c:c + 1],
                                                  ALU.mult, ALU.add)
                        step(ins)
                        w.scalar_tensor_tensor(oT[:, :, pj * S:(pj + 1) * S], o4[:, :, 1, :], parity[:, 1:2],
                                               o_even[:, :, :], ALU.mult, ALU.add).then_inc(o_evac, 1)
                    if j == 1 and attend:
                        dve.wait_ge(rstd1_ready, t)
                        w.tensor_scalar(xn1[:, :], x1[:, :], mv[:, 0:1], rstd[:, 0:1], ALU.subtract, ALU.mult
                                        ).then_inc(xn1_ready, 1)
                    if j == 1 and close:
                        dve.wait_ge(rstd2_ready, t - 1)
                        if last:
                            dve.wait_ge(last_xn2_stored, 16)
                        elif not (isinstance(t, int) and t <= 2):
                            dve.wait_ge(xn2_stored, 16 * (t - 2))
                        w.tensor_scalar(xn2[:, :], x2[:, :], mv2[:, 0:1], rstd2[:, 0:1], ALU.subtract, ALU.mult
                                        ).then_inc(xn2_ready, 1)
                    if j == 2 and close:
                        dve.wait_ge(lg_evac, t - 1)
                        settle(dve)
                        step(w.max(top8[:, :], lg[:, :]))
                        w.tensor_scalar(lg_c[:, :], lg[:, :], top8[:, 0:1], None, ALU.subtract).then_inc(lg_centred, 1)
                        for r, rest in enumerate((lg, lg_rest)):
                            step(w.scalar_tensor_tensor(lead[:, :], rest[:, :], top8[:, r:r + 1], expert_from[:, :],
                                                        ALU.is_equal, ALU.mult))
                            step(w.tensor_reduce(lead_max[:, :], lead[:, :], AX.X, ALU.max))
                            step(w.tensor_scalar(hit[:, r, :], expert_from[:, :], lead_max[:, 0:1], None,
                                                 ALU.is_equal))
                            if r == 0:
                                step(w.scalar_tensor_tensor(lg_rest[:, :], hit[:, 0, :], -BIG, lg[:, :],
                                                            ALU.mult, ALU.add))
                        w.tensor_tensor(chosen[:, :], hit[:, 0, :], hit[:, 1, :], ALU.add).then_inc(chosen_ready, 1)
                    if before_last and j == 0:
                        early_table()
                    if before_last and j == 1:
                        get(0)
                    if before_last and j == 2:
                        dve.wait_ge(qk1_evac, t)
                        w.tensor_tensor(
                            q1_bd[:, 1, :, :, :],
                            qk1[:, 0, 1, :].rearrange("p (b q) -> p b q", b=BT).unsqueeze(2
                                ).to_broadcast([P, BT, HH, S]),
                            head_mask[:, :].unsqueeze(1).unsqueeze(3).to_broadcast([P, BT, HH, S]), ALU.mult
                            ).then_inc(q1_bd_half_ready, 1)
                    if before_last and j == 3:
                        get(1)
                    if last and j <= 1:
                        block(j + 1)

            tile_loop(dve, step, DVE_STEPS, body)

            block_up(BT)
            get(NA)
            block_hidden(BT)
            with dve.Fori(BT + 1, NB - 2) as n:
                block(n)
            block(NB - 2, follow=False)
            block(NB - 1, follow=False)
            weigh(NB - 1)


def kernel(**inputs):
    import numpy as _np
    import concourse.bacc as _bacc
    from concourse import mybir as _mybir
    from concourse.bass_utils import run_bass_kernel_spmd as _run

    a = {k: _np.asarray(v) for k, v in inputs.items()}
    ctx = a["ctx_1024"]
    ins = {
        "x": a["x"].reshape(TOK, D),
        "ctxT": ctx.transpose(2, 0, 1),
        "ctx_tailT": ctx[:, KM, :].T,
        "mask": a["mask_1x1xSxS2_ik1"].reshape(S, K),
        "wqT": a["L0_xattn_wq"].T, "wkT": a["L0_xattn_wk"].T, "wvT": a["L0_xattn_wv"].T,
        "columns": _np.stack([a[n].reshape(DC, P).T for n in (
            "L0_xattn_bq", "L0_xattn_bk", "L0_xattn_bv", "L0_attn_norm_w")], axis=1),
        "woT": a["L0_xattn_wo"].T, "bo": a["L0_xattn_bo"],
        "sqT": a["L0_attn_Wq"].T, "skT": a["L0_attn_Wk"].T, "svT": a["L0_attn_Wv"].T,
        "soT": a["L0_attn_Wo"].T, "sbo": a["L0_attn_bo"],
        "diff_weight": a["L0_attn_diff_weight"].reshape(1),
        "routerT": a["L0_ffn_router_w"].T,
        "gate_w": a["L0_ffn_gate_w"], "gate_b": a["L0_ffn_gate_b"].reshape(E, FT, P).transpose(2, 0, 1),
        "up_w": a["L0_ffn_up_w"], "up_b": a["L0_ffn_up_b"].reshape(E, FT, P).transpose(2, 0, 1),
        "down_w": a["L0_ffn_down_w"], "down_b": a["L0_ffn_down_b"],
        "empty_slots": _np.stack([TOK + _np.arange(SLOTS) % P, _np.zeros(SLOTS)], axis=1).astype(_np.int32),
    }
    nc = _bacc.Bacc("TRN2", target_bir_lowering=False, num_devices=1)
    arrays, args = {}, []
    for name, value in ins.items():
        value = _np.ascontiguousarray(value)
        arrays[f"in_{name}"] = value
        args.append(nc.dram_tensor(f"in_{name}", value.shape, _mybir.dt.from_np(value.dtype),
                                   kind="ExternalInput").ap())
    args.append(nc.dram_tensor("v_tail_d", (G * B, D), F32, kind="Internal").ap())
    args.append(nc.dram_tensor("expert_x", (TOK + P, D), F32, kind="Internal").ap())
    args.append(nc.dram_tensor("slots", (SLOTS, 2), I32, kind="Internal").ap())
    args.append(nc.dram_tensor("out_0", (TOK + P, D), F32, kind="ExternalOutput").ap())
    perceiver_program(nc, *args)
    r = _run(nc, [arrays], core_ids=[0])
    return r.results[0]["out_0"][:TOK].reshape(B, S, D)
```
